# Optimizing a Trainium2 kernel written in Bass

```python
import numpy as np
import jax
import jax.numpy as jnp

def _softmax(x, axis=-1):
    return jax.nn.softmax(x, axis=axis)

def _gelu(x):
    return jax.nn.gelu(x, approximate=True)

def _silu(x):
    return jax.nn.silu(x)

def _sigmoid(x):
    return jax.nn.sigmoid(x)

def _layernorm(x, axis=-1, eps=1e-05):
    m = jnp.mean(x, axis=axis, keepdims=True)
    v = jnp.var(x, axis=axis, keepdims=True)
    return (x - m) / jnp.sqrt(v + eps)

def _scatter_add(tgt, idx, src, axis=0):
    return tgt.at[idx].add(src)

def _segment_sum(src, seg, n):
    return jax.ops.segment_sum(src, seg, n)
kernel_name = 'mk_xattn_seq_d2_seqx_r4_fddf95'

def setup_inputs(seed: int=0):
    np.random.seed(seed)
    _w = jnp.asarray

    def _rec_inputs():
        import jax
        import jax.numpy as jnp
        _rk = jax.random.key(seed)
        x = -0.0002928 + 1 * jax.random.normal(jax.random.fold_in(_rk, 1), (2, 1024, 256), jnp.float32)
        _lenS = 1024 - jax.random.randint(jax.random.fold_in(_rk, 7), (2,), 0, max(1, 1024 // 4) + 1, jnp.int32)
        _lenS2 = 77 - jax.random.randint(jax.random.fold_in(_rk, 8), (2,), 0, max(1, 77 // 4) + 1, jnp.int32)
        _ctx_768P = jax.random.normal(jax.random.fold_in(_rk, 11), (2, 16, 192), jnp.float32)
        _ctx_768c = jax.random.dirichlet(jax.random.fold_in(_rk, 511), 0.3 * jnp.ones((16,), jnp.float32), (2, 77))
        _ctx_768t = jnp.einsum('bsk,bkd->bsd', _ctx_768c, _ctx_768P)
        _ctx_768t = _ctx_768t * jax.lax.rsqrt(jnp.mean(jnp.square(_ctx_768t)) + 1e-12) * 0.953939
        ctx_768 = 2.09791e-05 + 1.00001 * (_ctx_768t + 0.3 * jax.random.normal(jax.random.fold_in(_rk, 611), (2, 77, 192), jnp.float32))
        return (x, ctx_768)
    x, ctx_768 = _rec_inputs()

    def _L0_xattn_setup():
        import jax, jax.numpy as jnp
        import numpy as np
        DIM1, DIM2, H = (256, 192, 16)
        HID = 4 * DIM1
        EPS = 1e-05

        def layernorm(x, w, b):
            mu = jnp.mean(x, axis=-1, keepdims=True)
            var = jnp.mean((x - mu) ** 2, axis=-1, keepdims=True)
            return (x - mu) * jax.lax.rsqrt(var + EPS) * w + b
        key = jax.random.key(seed)
        ks = jax.random.split(key, 12)
        s1 = 1.0 / np.sqrt(DIM1)
        s2 = 1.0 / np.sqrt(DIM2)
        sh = 1.0 / np.sqrt(HID)
        return {'x': jax.random.normal(ks[0], (4, 256, DIM1), jnp.float32), 'y': jax.random.normal(ks[1], (4, 256, DIM2), jnp.float32), 'ln1_w': jnp.ones((DIM1,), jnp.float32), 'ln1_b': jnp.zeros((DIM1,), jnp.float32), 'ln2_w': jnp.ones((DIM2,), jnp.float32), 'ln2_b': jnp.zeros((DIM2,), jnp.float32), 'ln3_w': jnp.ones((DIM1,), jnp.float32), 'ln3_b': jnp.zeros((DIM1,), jnp.float32), 'Wq': jax.random.uniform(ks[2], (DIM1, DIM1), jnp.float32, -s1, s1), 'Wkv': jax.random.uniform(ks[3], (DIM2, 2 * DIM1), jnp.float32, -s2, s2), 'Wproj': jax.random.uniform(ks[4], (DIM1, DIM1), jnp.float32, -s1, s1), 'bproj': jnp.zeros((DIM1,), jnp.float32), 'W1': jax.random.uniform(ks[5], (DIM1, HID), jnp.float32, -s1, s1), 'b1': jnp.zeros((HID,), jnp.float32), 'W2': jax.random.uniform(ks[6], (HID, DIM1), jnp.float32, -sh, sh), 'b2': jnp.zeros((DIM1,), jnp.float32)}
    _L0_xattn_all = _L0_xattn_setup()
    _L0_xattn_in = {k: v for k, v in _L0_xattn_all.items() if k in ('ln1_w', 'ln1_b', 'ln2_w', 'ln2_b', 'ln3_w', 'ln3_b', 'Wq', 'Wkv', 'Wproj', 'bproj', 'W1', 'b1', 'W2', 'b2')}
    del _L0_xattn_all

    def _L1_xattn_setup():
        import jax, jax.numpy as jnp
        import numpy as np
        B, S, L = (2, 512, 128)
        WIDTH, HEADS, CTX = (256, 16, 192)
        HD = WIDTH // HEADS
        EPS = 1e-05

        def _layernorm(x, g, b):
            m = jnp.mean(x, axis=-1, keepdims=True)
            v = jnp.mean(jnp.square(x - m), axis=-1, keepdims=True)
            return (x - m) * jax.lax.rsqrt(v + EPS) * g + b

        def _mha(q_in, kv_in, wq, bq, wk, bk, wv, bv, wo, bo):
            b = q_in.shape[0]
            q = (q_in @ wq.T + bq).reshape(b, -1, HEADS, HD).transpose(0, 2, 1, 3)
            k = (kv_in @ wk.T + bk).reshape(b, -1, HEADS, HD).transpose(0, 2, 1, 3)
            v = (kv_in @ wv.T + bv).reshape(b, -1, HEADS, HD).transpose(0, 2, 1, 3)
            scores = jnp.einsum('bhqd,bhkd->bhqk', q, k) * HD ** (-0.5)
            p = jax.nn.softmax(scores, axis=-1)
            o = jnp.einsum('bhqk,bhkd->bhqd', p, v)
            o = o.transpose(0, 2, 1, 3).reshape(b, -1, WIDTH)
            return o @ wo.T + bo
        key = jax.random.key(seed)
        ks = jax.random.split(key, 32)

        def xav(k, shape, gain=1.0):
            fan_out, fan_in = shape
            a = gain * np.sqrt(6.0 / (fan_in + fan_out))
            return jax.random.uniform(k, shape, jnp.float32, -a, a)
        g2 = 1.0 / np.sqrt(2.0)
        inp = {'x': jax.random.normal(ks[0], (B, S, WIDTH), jnp.float32), 'context': jax.random.normal(ks[1], (B, L, CTX), jnp.float32), 'ln1_g': jnp.ones((WIDTH,), jnp.float32), 'ln1_b': jnp.zeros((WIDTH,), jnp.float32), 'ln2_g': jnp.ones((WIDTH,), jnp.float32), 'ln2_b': jnp.zeros((WIDTH,), jnp.float32), 'ln3_g': jnp.ones((WIDTH,), jnp.float32), 'ln3_b': jnp.zeros((WIDTH,), jnp.float32), 'sa_wq': xav(ks[2], (WIDTH, WIDTH), g2), 'sa_bq': jnp.zeros((WIDTH,), jnp.float32), 'sa_wk': xav(ks[3], (WIDTH, WIDTH), g2), 'sa_bk': jnp.zeros((WIDTH,), jnp.float32), 'sa_wv': xav(ks[4], (WIDTH, WIDTH), g2), 'sa_bv': jnp.zeros((WIDTH,), jnp.float32), 'sa_wo': xav(ks[5], (WIDTH, WIDTH), 1.0), 'sa_bo': jnp.zeros((WIDTH,), jnp.float32), 'ca_wq': xav(ks[6], (WIDTH, WIDTH), g2), 'ca_bq': jnp.zeros((WIDTH,), jnp.float32), 'ca_wk': xav(ks[7], (WIDTH, CTX), g2), 'ca_bk': jnp.zeros((WIDTH,), jnp.float32), 'ca_wv': xav(ks[8], (WIDTH, CTX), g2), 'ca_bv': jnp.zeros((WIDTH,), jnp.float32), 'ca_wo': xav(ks[9], (WIDTH, WIDTH), 1.0), 'ca_bo': jnp.zeros((WIDTH,), jnp.float32), 'mlp_w1': 0.02 * jax.random.normal(ks[10], (4 * WIDTH, WIDTH), jnp.float32), 'mlp_b1': jnp.zeros((4 * WIDTH,), jnp.float32), 'mlp_w2': 0.02 * jax.random.normal(ks[11], (WIDTH, 4 * WIDTH), jnp.float32), 'mlp_b2': jnp.zeros((WIDTH,), jnp.float32)}
        return inp
    _L1_xattn_all = _L1_xattn_setup()
    _L1_xattn_in = {k: v for k, v in _L1_xattn_all.items() if k in ('ln1_g', 'ln1_b', 'ln2_g', 'ln2_b', 'ln3_g', 'ln3_b', 'sa_wq', 'sa_bq', 'sa_wk', 'sa_bk', 'sa_wv', 'sa_bv', 'sa_wo', 'sa_bo', 'ca_wq', 'ca_bq', 'ca_wk', 'ca_bk', 'ca_wv', 'ca_bv', 'ca_wo', 'ca_bo', 'mlp_w1', 'mlp_b1', 'mlp_w2', 'mlp_b2')}
    del _L1_xattn_all
    return {'x': x, 'ctx_768': ctx_768, 'L0_xattn_ln1_w': _L0_xattn_in['ln1_w'], 'L0_xattn_ln1_b': _L0_xattn_in['ln1_b'], 'L0_xattn_ln2_w': _L0_xattn_in['ln2_w'], 'L0_xattn_ln2_b': _L0_xattn_in['ln2_b'], 'L0_xattn_ln3_w': _L0_xattn_in['ln3_w'], 'L0_xattn_ln3_b': _L0_xattn_in['ln3_b'], 'L0_xattn_Wq': _L0_xattn_in['Wq'], 'L0_xattn_Wkv': _L0_xattn_in['Wkv'], 'L0_xattn_Wproj': _L0_xattn_in['Wproj'], 'L0_xattn_bproj': _L0_xattn_in['bproj'], 'L0_xattn_W1': _L0_xattn_in['W1'], 'L0_xattn_b1': _L0_xattn_in['b1'], 'L0_xattn_W2': _L0_xattn_in['W2'], 'L0_xattn_b2': _L0_xattn_in['b2'], 'L1_xattn_ln1_g': _L1_xattn_in['ln1_g'], 'L1_xattn_ln1_b': _L1_xattn_in['ln1_b'], 'L1_xattn_ln2_g': _L1_xattn_in['ln2_g'], 'L1_xattn_ln2_b': _L1_xattn_in['ln2_b'], 'L1_xattn_ln3_g': _L1_xattn_in['ln3_g'], 'L1_xattn_ln3_b': _L1_xattn_in['ln3_b'], 'L1_xattn_sa_wq': _L1_xattn_in['sa_wq'], 'L1_xattn_sa_bq': _L1_xattn_in['sa_bq'], 'L1_xattn_sa_wk': _L1_xattn_in['sa_wk'], 'L1_xattn_sa_bk': _L1_xattn_in['sa_bk'], 'L1_xattn_sa_wv': _L1_xattn_in['sa_wv'], 'L1_xattn_sa_bv': _L1_xattn_in['sa_bv'], 'L1_xattn_sa_wo': _L1_xattn_in['sa_wo'], 'L1_xattn_sa_bo': _L1_xattn_in['sa_bo'], 'L1_xattn_ca_wq': _L1_xattn_in['ca_wq'], 'L1_xattn_ca_bq': _L1_xattn_in['ca_bq'], 'L1_xattn_ca_wk': _L1_xattn_in['ca_wk'], 'L1_xattn_ca_bk': _L1_xattn_in['ca_bk'], 'L1_xattn_ca_wv': _L1_xattn_in['ca_wv'], 'L1_xattn_ca_bv': _L1_xattn_in['ca_bv'], 'L1_xattn_ca_wo': _L1_xattn_in['ca_wo'], 'L1_xattn_ca_bo': _L1_xattn_in['ca_bo'], 'L1_xattn_mlp_w1': _L1_xattn_in['mlp_w1'], 'L1_xattn_mlp_b1': _L1_xattn_in['mlp_b1'], 'L1_xattn_mlp_w2': _L1_xattn_in['mlp_w2'], 'L1_xattn_mlp_b2': _L1_xattn_in['mlp_b2']}

def reference(x, ctx_768, L0_xattn_ln1_w, L0_xattn_ln1_b, L0_xattn_ln2_w, L0_xattn_ln2_b, L0_xattn_ln3_w, L0_xattn_ln3_b, L0_xattn_Wq, L0_xattn_Wkv, L0_xattn_Wproj, L0_xattn_bproj, L0_xattn_W1, L0_xattn_b1, L0_xattn_W2, L0_xattn_b2, L1_xattn_ln1_g, L1_xattn_ln1_b, L1_xattn_ln2_g, L1_xattn_ln2_b, L1_xattn_ln3_g, L1_xattn_ln3_b, L1_xattn_sa_wq, L1_xattn_sa_bq, L1_xattn_sa_wk, L1_xattn_sa_bk, L1_xattn_sa_wv, L1_xattn_sa_bv, L1_xattn_sa_wo, L1_xattn_sa_bo, L1_xattn_ca_wq, L1_xattn_ca_bq, L1_xattn_ca_wk, L1_xattn_ca_bk, L1_xattn_ca_wv, L1_xattn_ca_bv, L1_xattn_ca_wo, L1_xattn_ca_bo, L1_xattn_mlp_w1, L1_xattn_mlp_b1, L1_xattn_mlp_w2, L1_xattn_mlp_b2):
    import jax
    import jax.numpy as jnp

    def _L0_xattn_ref(x, y, ln1_w, ln1_b, ln2_w, ln2_b, ln3_w, ln3_b, Wq, Wkv, Wproj, bproj, W1, b1, W2, b2):
        import jax, jax.numpy as jnp
        import numpy as np
        DIM1, DIM2, H = (256, 192, 16)
        HID = 4 * DIM1
        EPS = 1e-05

        def layernorm(x, w, b):
            mu = jnp.mean(x, axis=-1, keepdims=True)
            var = jnp.mean((x - mu) ** 2, axis=-1, keepdims=True)
            return (x - mu) * jax.lax.rsqrt(var + EPS) * w + b
        B, N1, C1 = x.shape
        hd = C1 // H
        scale = hd ** (-0.5)
        xn = layernorm(x, ln1_w, ln1_b)
        yn = layernorm(y, ln2_w, ln2_b)
        q = (xn @ Wq).reshape(B, N1, H, hd).transpose(0, 2, 1, 3)
        kv = (yn @ Wkv).reshape(B, y.shape[1], 2, H, hd)
        k = kv[:, :, 0].transpose(0, 2, 1, 3)
        v = kv[:, :, 1].transpose(0, 2, 1, 3)
        attn = jax.nn.softmax(jnp.einsum('bhqd,bhkd->bhqk', q, k) * scale, axis=-1)
        o = jnp.einsum('bhqk,bhkd->bhqd', attn, v).transpose(0, 2, 1, 3).reshape(B, N1, C1)
        x = x + (o @ Wproj + bproj)
        h = jax.nn.gelu(layernorm(x, ln3_w, ln3_b) @ W1 + b1, approximate=False)
        x = x + (h @ W2 + b2)
        return x

    def _L1_xattn_ref(x, context, ln1_g, ln1_b, ln2_g, ln2_b, ln3_g, ln3_b, sa_wq, sa_bq, sa_wk, sa_bk, sa_wv, sa_bv, sa_wo, sa_bo, ca_wq, ca_bq, ca_wk, ca_bk, ca_wv, ca_bv, ca_wo, ca_bo, mlp_w1, mlp_b1, mlp_w2, mlp_b2):
        import jax, jax.numpy as jnp
        import numpy as np
        B, S, L = (2, 512, 128)
        WIDTH, HEADS, CTX = (256, 16, 192)
        HD = WIDTH // HEADS
        EPS = 1e-05

        def _layernorm(x, g, b):
            m = jnp.mean(x, axis=-1, keepdims=True)
            v = jnp.mean(jnp.square(x - m), axis=-1, keepdims=True)
            return (x - m) * jax.lax.rsqrt(v + EPS) * g + b

        def _mha(q_in, kv_in, wq, bq, wk, bk, wv, bv, wo, bo):
            b = q_in.shape[0]
            q = (q_in @ wq.T + bq).reshape(b, -1, HEADS, HD).transpose(0, 2, 1, 3)
            k = (kv_in @ wk.T + bk).reshape(b, -1, HEADS, HD).transpose(0, 2, 1, 3)
            v = (kv_in @ wv.T + bv).reshape(b, -1, HEADS, HD).transpose(0, 2, 1, 3)
            scores = jnp.einsum('bhqd,bhkd->bhqk', q, k) * HD ** (-0.5)
            p = jax.nn.softmax(scores, axis=-1)
            o = jnp.einsum('bhqk,bhkd->bhqd', p, v)
            o = o.transpose(0, 2, 1, 3).reshape(b, -1, WIDTH)
            return o @ wo.T + bo
        h = _layernorm(x, ln1_g, ln1_b)
        x = x + _mha(h, h, sa_wq, sa_bq, sa_wk, sa_bk, sa_wv, sa_bv, sa_wo, sa_bo)
        h = _layernorm(x, ln2_g, ln2_b)
        x = x + _mha(h, context, ca_wq, ca_bq, ca_wk, ca_bk, ca_wv, ca_bv, ca_wo, ca_bo)
        h = _layernorm(x, ln3_g, ln3_b)
        h = jax.nn.gelu(h @ mlp_w1.T + mlp_b1, approximate=False) @ mlp_w2.T + mlp_b2
        return x + h
    x = _L0_xattn_ref(x, ctx_768, L0_xattn_ln1_w, L0_xattn_ln1_b, L0_xattn_ln2_w, L0_xattn_ln2_b, L0_xattn_ln3_w, L0_xattn_ln3_b, L0_xattn_Wq, L0_xattn_Wkv, L0_xattn_Wproj, L0_xattn_bproj, L0_xattn_W1, L0_xattn_b1, L0_xattn_W2, L0_xattn_b2)
    x = _L1_xattn_ref(x, ctx_768, L1_xattn_ln1_g, L1_xattn_ln1_b, L1_xattn_ln2_g, L1_xattn_ln2_b, L1_xattn_ln3_g, L1_xattn_ln3_b, L1_xattn_sa_wq, L1_xattn_sa_bq, L1_xattn_sa_wk, L1_xattn_sa_bk, L1_xattn_sa_wv, L1_xattn_sa_bv, L1_xattn_sa_wo, L1_xattn_sa_bo, L1_xattn_ca_wq, L1_xattn_ca_bq, L1_xattn_ca_wk, L1_xattn_ca_bk, L1_xattn_ca_wv, L1_xattn_ca_bv, L1_xattn_ca_wo, L1_xattn_ca_bo, L1_xattn_mlp_w1, L1_xattn_mlp_b1, L1_xattn_mlp_w2, L1_xattn_mlp_b2)
    return x

_drawn_inputs = setup_inputs


def setup_inputs(seed=0):
    import zlib

    import numpy as np

    out = dict(_drawn_inputs(seed))
    spreads = {'L0_xattn_ln1_w': (1.0, 0.6),
     'L0_xattn_ln1_b': (0.0, 0.8),
     'L0_xattn_ln2_w': (1.0, 0.2),
     'L0_xattn_ln2_b': (0.0, 0.1),
     'L0_xattn_ln3_w': (1.0, 0.2),
     'L0_xattn_ln3_b': (0.0, 0.342),
     'L0_xattn_bproj': (0.0, 0.1),
     'L0_xattn_b1': (0.0, 0.1),
     'L0_xattn_b2': (0.0, 0.1),
     'L1_xattn_ln1_g': (1.0, 0.2),
     'L1_xattn_ln1_b': (0.0, 0.1),
     'L1_xattn_ln2_g': (1.0, 0.6),
     'L1_xattn_ln2_b': (0.0, 0.8),
     'L1_xattn_ln3_g': (1.0, 0.6),
     'L1_xattn_ln3_b': (0.0, 0.8),
     'L1_xattn_sa_bq': (0.0, 2.0),
     'L1_xattn_sa_bk': (0.0, 2.0),
     'L1_xattn_sa_bv': (0.0, 0.1),
     'L1_xattn_sa_bo': (0.0, 0.1),
     'L1_xattn_ca_bq': (0.0, 0.8),
     'L1_xattn_ca_bk': (0.0, 2.0),
     'L1_xattn_ca_bv': (0.0, 0.1),
     'L1_xattn_ca_bo': (0.0, 0.1),
     'L1_xattn_mlp_b1': (0.0, 0.1),
     'L1_xattn_mlp_b2': (0.0, 0.1)}
    factors = {'L0_xattn_Wq': 2.801}
    for name, (base, spread) in spreads.items():
        noise = np.random.default_rng([zlib.crc32(name.encode()), seed]).standard_normal(out[name].shape)
        drawn = base * np.exp(spread * noise) if base else spread * noise
        out[name] = jnp.asarray(drawn.astype(out[name].dtype))
    for name, factor in factors.items():
        out[name] = (out[name] * factor).astype(out[name].dtype)
    return out
```

```python
from contextlib import ExitStack

import concourse.bass as bass
from concourse import mybir

F32, F32R, BF16 = mybir.dt.float32, mybir.dt.float32r, mybir.dt.bfloat16
ALU, ACT, AX = mybir.AluOpType, mybir.ActivationFunctionType, mybir.AxisListType

P = 128
B, S, D, CTX, L = 2, 1024, 256, 192, 77
HEADS, HD, HID = 16, 16, 1024
T = B * S
NT = T // P
CH = 512
NC = T // CH
TPC = CH // P
CT = D // P
KT = S // P
HB = HID // P
EPS = 1e-5
SCALE = HD ** -0.5
GROUPS = 7
SK = GROUPS * HD
SKM = SK + 3
VW = 32
OW = HD + 1
CREDIT = 64

COLS, ROWS = {}, {}
for _n, _w in (("l0_ln1_w", 2), ("l0_ln1_b", 2), ("l0_ln3_w", 2), ("l0_ln3_b", 2), ("l1_ln1_w", 2),
               ("l1_ln1_b", 2), ("l1_ln2_w", 2), ("l1_ln2_b", 2), ("l1_ln3_w", 2), ("l1_ln3_b", 2),
               ("l0_ln2_w", 2), ("l0_ln2_b", 2), ("sa_bq", 2), ("sa_bk", 2), ("ca_bq", 2), ("ca_bk", 2),
               ("l0_b1", 8), ("l1_b1", 8), ("zero", 2)):
    COLS[_n] = (sum(w for _, w in COLS.values()), _w)
NCOLS = sum(w for _, w in COLS.values())
for _n in ("l0_bproj", "l0_b2", "sa_bv", "sa_bo", "ca_bo", "l1_b2", "ca_bv"):
    ROWS[_n] = len(ROWS)

WB_Q0, WB_P0, WB_SQ, WB_SK, WB_SV, WB_SO, WB_CQ, WB_CO, WB_W1, WB_W2 = 0, 1, 2, 3, 4, 5, 6, 7, 8, 12
NWB = 16


class Tally:

    def __init__(self, sem, start, total):
        self.sem, self.start, self.total = sem, start, total

    def at(self, n):
        return n + self.start

    @property
    def end(self):
        return self.start + self.total


def build(nc, x_d, ctx_d, w_d, wm_d, wkv_d, wck_d, wcv_d, cols_d, rows_d, out_d):
    es = ExitStack()
    with es:
        def sb(name, shape, dt):
            return es.enter_context(nc.sbuf_tensor(name, shape, dt))

        def scratch(name, n):
            return nc.dram_tensor(name, [D, 3, n], BF16, kind="Internal").ap()
        q_parts = [scratch("q_parts_l0", T), scratch("q_parts_self", T), scratch("q_parts_cross", T)]
        k_parts = scratch("k_parts_self", T)
        kc_parts = [scratch("kc_parts_l0", B * L), scratch("kc_parts_l1", B * L)]

        X = sb("X", [P, NT, D], F32)
        WH = sb("WH", [P, NWB, 512], F32R)
        WL = sb("WL", [P, NWB, 512], F32R)
        XTH = sb("XTH", [P, 2, CT, CH], F32R)
        XTL = sb("XTL", [P, 2, CT, CH], F32R)
        XN = sb("XN", [P, 2, TPC, D], F32)
        SCR = sb("SCR", [P, 6144], F32)
        STK = sb("STK", [P, 8, T], BF16)
        V = sb("V", [P, NT, D], F32)
        VS = sb("VS", [P, 2, B, KT, VW], F32)
        OU = sb("OU", [P, NT, HEADS, OW], F32)
        KSC = sb("KSC", [P, 2, HEADS, B * L], BF16)
        VC = sb("VC", [L, 2, B, D], F32)
        colv = sb("colv", [P, NCOLS], F32)
        rowv = sb("rowv", [P, len(ROWS), D], F32)
        identf = sb("identf", [P, P], F32)
        identb = sb("identb", [P, P], BF16)
        bst = sb("bst", [P, 8, 6], F32)
        mv = sb("mv", [P, 8, 2], F32)
        var_eps = sb("var_eps", [P, 8], F32)
        rstd = sb("rstd", [P, 8], F32)
        half = sb("half", [P, 8], F32)
        rsum = sb("rsum", [P, 2, TPC * HEADS], F32)
        nmax = sb("nmax", [P, 2, NT], F32)
        nres = sb("nres", [P, 2, NT], F32)
        nparts = sb("nparts", [P, 2, 3 * NT], BF16)
        nrow = sb("nrow", [3 * NT, 2, P], BF16)
        PS = es.enter_context(nc.psum_tensor("PS", [P, 8, 512], F32))

        XF = SCR[:, 0:2048].rearrange("p (a c n) -> p a c n", a=2, c=CT)
        RES = SCR[:, 2048:3072].rearrange("p (r n) -> p r n", r=2)
        QP = SCR[:, 3072:6144].bitcast(BF16).rearrange("p (s t n) -> p s t n", s=4, t=3)
        GF = SCR[:, 2048:3072].rearrange("p (r n) -> p r n", r=2)
        PT = SCR[:, 0:4096].rearrange("p (s n) -> p s n", s=2)
        OS = SCR[:, 4096:5120].rearrange("p (s n) -> p s n", s=2)
        RAW = STK[:, :, :].rearrange("p s n -> p (s n)").bitcast(F32).rearrange("p (b n) -> p b n", b=NWB)
        Vf = V[:, :, :].rearrange("p t c -> p (t c)")
        WCA = Vf[:, 0:1024].rearrange("p (l n) -> p l n", l=2)
        WCB = Vf[0:CTX - P, 1024:2048].rearrange("p (l n) -> p l n", l=2)
        OUf = OU[:, :, :, :].rearrange("p t h w -> p (t h w)")
        CX = OUf[0:L, 0:384].rearrange("p (b c) -> p b c", b=B)
        CN = OUf[0:L, 384:768].rearrange("p (b c) -> p b c", b=B)
        YT = OUf[:, 768:768 + 4 * B * L].rearrange("p (k n) -> p k n", k=4)
        KR = OUf[:, 1408:1408 + 4 * B * L].rearrange("p (k n) -> p k n", k=4)
        KP = OUf[:, 2048:2048 + 6 * B * L].bitcast(BF16).rearrange("p (k t n) -> p k t n", k=4, t=3)

        def whl(w, blk, ct, off, n):
            return w[:, blk, ct * D + off:ct * D + off + n]

        def w1(w, ct, h):
            f = ct * HID + h * P
            return w[:, WB_W1 + f // 512, f % 512:f % 512 + P]

        def w2(w, h):
            f = h * D
            return w[:, WB_W2 + f // 512, f % 512:f % 512 + D]

        def col(name, i):
            return colv[:, COLS[name][0] + i:COLS[name][0] + i + 1]

        def row(name):
            return rowv[:, ROWS[name], :]

        sems, starts = {}, {}

        def stage(**totals):
            out = {}
            for name, total in totals.items():
                if name not in sems:
                    sems[name] = es.enter_context(nc.semaphore(name))
                    starts[name] = CREDIT
                out[name] = Tally(sems[name], starts[name], total)
                starts[name] += total
            return out

        ld = {n: es.enter_context(nc.semaphore("ld_" + n)) for n in ("x", "ctx", "wq", "w", "wc", "vec", "mlp1")}
        s_const = es.enter_context(nc.semaphore("s_const"))
        s_const2 = es.enter_context(nc.semaphore("s_const2"))
        s_credit = es.enter_context(nc.semaphore("s_credit"))
        s_passed = es.enter_context(nc.semaphore("s_passed"))
        s_out = es.enter_context(nc.semaphore("s_out"))

        W_SPLIT = dict(w_high=0, w_low=0)

        def split_stage(blocks):
            return stage(w_high=blocks, w_low=blocks)

        def front(nout, qk):
            t = dict(bn=NT, bn2=NT if qk else 0, rs=2 if qk else 0, xn=NT, tr=NC * CT, xf=NC * CT, xh=NC * CT, xl=NC * CT,
                     mm=nout * NC, ev=nout * NC)
            if qk:
                t |= dict(part1=qk * NC, part2=qk * NC, part3=qk * NC)
                t |= {f"stored{s}": 16 * qk * NC // 4 for s in range(4)}
            else:
                t |= dict(xr=NT)
            return stage(**t)

        def mlp():
            return stage(bn=NT, bn2=NT, rs=NC, xn=NT, tr=NC * CT, xf=NC * CT, xh=NC * CT, xl=NC * CT,
                         m1=HB * NC, gelu=HB * NC, gh=HB * NC, gl=HB * NC, m2=(HB - 1) * NC, ev=NT, acc=NT, xr=NT)

        def attention(keys_steps, loads, groups):
            n = HEADS
            return stage(stack0=loads * n // 2, stack1=loads * n // 2, smax=groups * n, maxed=groups * n,
                         msplit=5 * n, mtr=n, mrow=n, mdma0=8 * n, mdma1=8 * n,
                         st=4 * keys_steps * n, exped=4 * keys_steps * n, vs=n, pv=4 * keys_steps * n,
                         os=n, otr=n, ou=n)

        cx = stage(c_bn=2, c_bn2=2, c_rs=1, c_n=2, c_tr=4, c_yt=4, c_mm=8, c_p1=4, c_r=4, c_p2=4, c_p3=4,
                   c_v=4, c_store=16 * 4, c_stack=16 * 14)
        sp0 = split_stage(NWB)
        A0 = front(2, 2)
        C0 = attention(1, 32, 2)
        P0 = front(4, 0)
        M0 = mlp()
        A1 = front(8, 4)
        sp1 = split_stage(8)
        ones_set = stage(ones_rows=1)
        C1 = attention(KT, 80, NT)
        P1 = front(4, 0)
        A2 = front(2, 2)
        C2 = attention(1, 32, 2)
        P2 = front(4, 0)
        M1 = mlp()

        def join(eng, st, names):
            for name in names.split():
                eng.wait_ge(st[name].sem, st[name].end)

        ALL_A = "xn tr xf xh xl mm ev part1 part2 part3 stored0 stored1 stored2 stored3"
        ALL_P = "xn tr xf xh xl mm ev xr"
        ALL_M = "xn tr xf xh xl m1 gelu gh gl m2 ev xr"
        ALL_C = "stack0 stack1 smax maxed msplit mtr mrow mdma0 mdma1 st exped vs pv os otr ou"

        def wait(eng, tally, n):
            eng.wait_ge(tally.sem, tally.at(n))

        def wait_apart(eng, tally, n):
            eng.wait_ge(tally.sem, tally.at(n))
            eng.sem_inc(s_passed, 1)

        def pe_transposes(pe, st, c, a):
            wait(pe, st["xn"], 4 * c + 4)
            for ct in range(CT):
                wait(pe, st["xf"], 2 * c + ct - 3 if a is not None else 2 * c + ct - 1)
                s = a or 0
                for t in range(TPC):
                    last = nc.tensor.transpose(PS[:, 2 * s + ct, t * P:(t + 1) * P],
                                               XN[:, s, t, ct * P:(ct + 1) * P], identf[:])
                last.then_inc(st["tr"].sem, 1)

        def split_mm(out, pairs):
            n = len(pairs)
            for k, (lh, ll, rh, rl) in enumerate(pairs):
                nc.tensor.matmul(out, lh, rh, start=(k == 0), stop=False)
                nc.tensor.matmul(out, ll, rh, start=False, stop=False)
                last = nc.tensor.matmul(out, lh, rl, start=False, stop=(k == n - 1))
            return last

        def pe_front(pe, st, tform, tokform, nout):
            with pe.Fori(0, 2) as p:
                for a in range(2):
                    pe_transposes(pe, st, 2 * p + a, a)
                for a in range(2):
                    c = 2 * p + a
                    wait(pe, st["xl"], 2 * c + 2)
                    o = 0
                    for blk, m in tform:
                        wait(pe, st["ev"], nout * c + o - 3)
                        split_mm(PS[:, 4 + (nout * a + o) % 4, :],
                                 [(whl(WH, blk, ct, m * P, P), whl(WL, blk, ct, m * P, P),
                                   XTH[:, a, ct, :], XTL[:, a, ct, :]) for ct in range(CT)]
                                 ).then_inc(st["mm"].sem, 1)
                        o += 1
                    for blk in tokform:
                        for t in range(TPC):
                            wait(pe, st["ev"], nout * c + o - 3)
                            split_mm(PS[:, 4 + (nout * a + o) % 4, 0:D],
                                     [(XTH[:, a, ct, t * P:(t + 1) * P], XTL[:, a, ct, t * P:(t + 1) * P],
                                       whl(WH, blk, ct, 0, D), whl(WL, blk, ct, 0, D)) for ct in range(CT)]
                                     ).then_inc(st["mm"].sem, 1)
                            o += 1

        def pe_mlp(pe, st):
            def m1(c, h):
                wait(pe, st["gelu"], 8 * c + h - 1)
                split_mm(PS[:, 2 + h % 2, :], [(w1(WH, ct, h), w1(WL, ct, h), XTH[:, 0, ct, :], XTL[:, 0, ct, :])
                                               for ct in range(CT)]).then_inc(st["m1"].sem, 1)

            def m2(c, h):
                wait(pe, st["gh"], 8 * c + h + 1)
                for t in range(TPC):
                    if h == 0:
                        wait(pe, st["ev"], 4 * c + t - 3)
                    g = XTH[:, 1, h % 2, t * P:(t + 1) * P]
                    nc.tensor.matmul(PS[:, 4 + t, 0:D], g, w2(WH, h), start=(h == 0), stop=False)
                    nc.tensor.matmul(PS[:, 4 + t, 0:D], g, w2(WL, h), start=False, stop=False)
                wait(pe, st["gl"], 8 * c + h + 1)
                for t in range(TPC):
                    mm = nc.tensor.matmul(PS[:, 4 + t, 0:D], XTL[:, 1, h % 2, t * P:(t + 1) * P], w2(WH, h),
                                          start=False, stop=(h == HB - 1))
                    if h == HB - 1:
                        mm.then_inc(st["acc"].sem, 1)
                    elif t == TPC - 1:
                        mm.then_inc(st["m2"].sem, 1)

            def chunk(c, last):
                wait(pe, st["xl"], 2 * c + 2)
                m1(c, 0)
                for h in range(1, HB):
                    m1(c, h)
                    if h < HB - 1:
                        m2(c, h - 1)
                if not last:
                    pe_transposes(pe, st, c + 1, None)
                m2(c, HB - 2)
                m2(c, HB - 1)

            pe_transposes(pe, st, 0, None)
            with pe.Fori(0, NC - 1) as c:
                chunk(c, False)
            chunk(NC - 1, True)

        def pe_mrow(pe, st, h, par, out):
            wait(pe, st["msplit"], 5 * h + 5)
            wait(pe, st["mrow"], h)
            wait_apart(pe, st["ou"], out)
            nc.tensor.transpose(PS[0:3 * NT, 7, 0:P // 2].bitcast(BF16), nparts[:, par, :], identb[:]
                                ).then_inc(st["mtr"].sem, 1)

        def pe_ot(pe, st, h, par):
            wait(pe, st["os"], h + 1)
            wait(pe, st["ou"], h)
            for i in range(TPC):
                last = nc.tensor.transpose(PS[:, 7, i * P:(i + 1) * P], OS[:, par, i * P:(i + 1) * P], identf[:])
            last.then_inc(st["otr"].sem, 1)

        def pe_cross(pe, st, layer):
            def smax(h, par, g):
                if g == 0:
                    wait(pe, st[f"stack{par}"], 32 * half_of(h, par) + 32)
                wait(pe, st["maxed"], 2 * h + g - 1)
                for i in range(8):
                    tile = 8 * g + i
                    b = g
                    last = nc.tensor.matmul(PS[:, 2 * g + i // 4, (i % 4) * P:(i % 4) * P + L],
                                            STK[0:SK, h % 8, tile * P:(tile + 1) * P],
                                            KSC[0:SK, layer, h, b * L:(b + 1) * L], start=True, stop=True)
                last.then_inc(st["smax"].sem, 1)

            def score(h, par, j):
                if j == 0:
                    wait(pe, st[f"mdma{par}"], 16 * half_of(h, par) + 16)
                wait(pe, st["exped"], 4 * h + j - 1)
                b = j // 2
                nc.tensor.matmul(PS[0:L, 4 + j % 2, :], KSC[0:SKM, layer, h, b * L:(b + 1) * L],
                                 STK[0:SKM, h % 8, j * CH:(j + 1) * CH], start=True, stop=True
                                 ).then_inc(st["st"].sem, 1)

            def values(h, par, j):
                if j == 0:
                    wait(pe, st["vs"], h + 1)
                    wait(pe, st["os"], h)
                wait(pe, st["exped"], 4 * h + j + 1)
                nc.tensor.matmul(PS[32 * j:32 * j + VW, 6, :], VS[0:L, par, j // 2, 0, :],
                                 PT[0:L, par, j * CH:(j + 1) * CH], start=True, stop=True
                                 ).then_inc(st["pv"].sem, 1)

            def unit(u, par, on):
                for g in range(2):
                    if on(0):
                        smax(u, par, g)
                    for j in (2 * g, 2 * g + 1):
                        if on(4):
                            score(u - 4, par, j)
                        if on(5):
                            values(u - 5, 1 - par, j)
                    if g == 0 and on(2):
                        pe_mrow(pe, st, u - 2, par, u - 6)
                if on(6):
                    wait(pe, st["mrow"], heads_until(u - 1))
                    pe_ot(pe, st, u - 6, par)

            pipeline(unit)

        def heads_until(n):
            return min(n, HEADS) if isinstance(n, int) else n

        def half_of(h, par):
            return (h - par) // 2

        def pipeline(unit, first=0, last=HEADS + 8):
            for u in range(first, last):
                unit(u, u % 2, lambda k, u=u: 0 <= u - k < HEADS)

        def self_lag(s, lag):
            g = s - lag
            return -(g // KT), g % KT

        def pipeline_self(eng, unit):
            for u in range(2):
                unit(u, u % 4, lambda k, u=u: 0 <= u - k < HEADS)
            with eng.Fori(0, 3) as i:
                for k in range(2, 6):
                    unit(4 * i + k, k % 4, lambda k: True)
            for u in range(14, HEADS + 3):
                unit(u, u % 4, lambda k, u=u: 0 <= u - k < HEADS)

        SELF_STEP = [(dict(m="max", s="score", v="values")[w[0]], int(w[1]))
                     for w in "m0 s0 m1 s1 v0 v1 v2 v3 s2 m2 s3 m3".split()]

        def pe_self(pe, st):
            def smax(h, m, i, n):
                if i == 0 and n == 0:
                    wait(pe, st[f"stack{m % 2}"], 80 * half_of(h, m % 2) + 80)
                if n == 0:
                    wait(pe, st["maxed"], 16 * h + i - 1)
                b = i // KT
                mm = nc.tensor.matmul(PS[:, 2 * (i % 2) + n, :], STK[0:SK, m, i * P:(i + 1) * P],
                                      STK[0:SK, m + 4, b * S + n * CH:b * S + (n + 1) * CH],
                                      start=True, stop=True)
                if n == 1:
                    mm.then_inc(st["smax"].sem, 1)

            def score(h, m, kt, j):
                if kt == 0 and j == 0:
                    wait(pe, st[f"mdma{m % 2}"], 16 * half_of(h, m % 2) + 16)
                wait(pe, st["exped"], 32 * h + 4 * kt + j - 1)
                b = j // 2
                nc.tensor.matmul(PS[:, 4 + j % 2, :], STK[0:SKM, m + 4, b * S + kt * P:b * S + (kt + 1) * P],
                                 STK[0:SKM, m, j * CH:(j + 1) * CH], start=True, stop=True
                                 ).then_inc(st["st"].sem, 1)

            def values(h, par, kt, j):
                if kt == 0 and j == 0:
                    wait(pe, st["vs"], h + 1)
                    wait(pe, st["os"], h)
                wait(pe, st["exped"], 32 * h + 4 * kt + j + 1)
                nc.tensor.matmul(PS[32 * j:32 * j + VW, 6, :], VS[:, par, j // 2, kt, :],
                                 PT[:, kt % 2, j * CH:(j + 1) * CH], start=(kt == 0), stop=(kt == KT - 1)
                                 ).then_inc(st["pv"].sem, 1)

            def unit(u, m, on):
                par = m % 2
                for s in range(KT):
                    if s == 2 and on(1):
                        pe_mrow(pe, st, u - 1, 1 - par, u - 2)
                    back, kt = self_lag(s, 12)
                    vback, vkt = self_lag(s, 13)
                    for what, j in SELF_STEP:
                        if what == "max" and on(0):
                            smax(u, m, 2 * s + j // 2, j % 2)
                        if what == "score" and on(back):
                            score(u - back, (m - back) % 4, kt, j)
                        if what == "values" and on(vback):
                            values(u - vback, (m - vback) % 2, vkt, j)
                    if s == 6 and on(2):
                        wait(pe, st["mrow"], heads_until(u))
                        pe_ot(pe, st, u - 2, par)

            pipeline_self(pe, unit)

        def act_xf(act, st, c, a, w, b):
            s = a or 0
            for ct in range(CT):
                wait(act, st["tr"], 2 * c + ct + 1)
                wait(act, st["xl"], 2 * c + ct - 3 if a is not None else 2 * c + ct - 1)
                if w is None:
                    i = nc.scalar.copy(XF[:, s, ct, :], PS[:, 2 * s + ct, :])
                else:
                    i = nc.scalar.activation(XF[:, s, ct, :], PS[:, 2 * s + ct, :], ACT.Identity,
                                             scale=col(w, ct), bias=col(b, ct))
                i.then_inc(st["xf"].sem, 1)

        def act_front(act, st, w, b, biases, nout):
            qk = len(biases)
            with act.Fori(0, 2) as p:
                for a in range(2):
                    act_xf(act, st, 2 * p + a, a, w, b)
                for a in range(2):
                    c = 2 * p + a
                    for o, (name, m) in enumerate(biases):
                        slot = (qk * a + o) % 4
                        wait(act, st["mm"], nout * c + o + 1)
                        wait(act, st[f"stored{slot}"], (qk * 2 // 4) * 16 * p + 16 * ((qk * a + o) // 4))
                        nc.scalar.activation(QP[:, slot, 0, :], PS[:, 4 + (nout * a + o) % 4, :], ACT.Identity,
                                             bias=col(name, m)).then_inc(st["part1"].sem, 1)

        def act_mlp(act, st, w, b, b1):
            def chunk(c, last):
                for h in range(HB):
                    wait(act, st["m1"], 8 * c + h + 1)
                    wait(act, st["gl"], 8 * c + h - 1)
                    nc.scalar.activation(GF[:, h % 2, :], PS[:, 2 + h % 2, :], ACT.Gelu, bias=col(b1, h)
                                         ).then_inc(st["gelu"].sem, 1)
                if not last:
                    act_xf(act, st, c + 1, None, w, b)
            act_xf(act, st, 0, None, w, b)
            with act.Fori(0, NC - 1) as c:
                chunk(c, False)
            chunk(NC - 1, True)

        def out_view(h):
            return OU[:, :, h, :].rearrange("p (j i) w -> p j i w", i=TPC)

        BACK = PS[:, 7, :].rearrange("p (i j w) -> p j i w", i=TPC, j=4)[:, :, :, 0:OW]

        def act_cross(act, st):
            def unit(u, par, on):
                if on(7):
                    wait(act, st["otr"], u - 6)
                    nc.scalar.copy(out_view(u - 7), BACK).then_inc(st["ou"].sem, 1)
                if on(4):
                    h = u - 4
                    for j in range(4):
                        wait(act, st["st"], 4 * h + j + 1)
                        wait(act, st["pv"], 4 * h + j - 7)
                        nc.scalar.activation(PT[0:L, par, j * CH:(j + 1) * CH], PS[0:L, 4 + j % 2, :], ACT.Exp,
                                             scale=SCALE).then_inc(st["exped"].sem, 1)
            pipeline(unit)

        def act_self(act, st):
            def unit(u, m, on):
                par = m % 2
                for s in range(KT):
                    if s == 5 and on(2):
                        wait(act, st["pv"], 32 * (u - 2) + 32)
                        wait(act, st["otr"], u - 3)
                        nc.scalar.copy(OS[:, par, :], PS[:, 6, :]).then_inc(st["os"].sem, 1)
                    if s == 7 and on(2):
                        wait(act, st["otr"], u - 1)
                        nc.scalar.copy(out_view(u - 2), BACK).then_inc(st["ou"].sem, 1)
                    back, kt = self_lag(s, 12)
                    if on(back):
                        g = KT * (u - back) + kt
                        for j in range(4):
                            wait(act, st["st"], 4 * g + j + 1)
                            wait(act, st["pv"], 4 * g + j - 7)
                            nc.scalar.activation(PT[:, kt % 2, j * CH:(j + 1) * CH], PS[:, 4 + j % 2, :], ACT.Exp,
                                                 scale=SCALE).then_inc(st["exped"].sem, 1)
            pipeline_self(act, unit)

        def dve_stats(dve, st, c, s0):
            for t in range(TPC):
                nc.vector.bn_stats(bst[:, s0 + t, :], X[:, 4 * c + t, :]).then_inc(st["bn"].sem, 1)
            for t in range(TPC):
                wait_apart(dve, st["bn"], 4 * c + t + 1)
                nc.vector.bn_aggr(mv[:, s0 + t, :], bst[:, s0 + t, :]).then_inc(st["bn2"].sem, 1)

        def dve_norm(dve, st, c, a, s0):
            for t in range(TPC):
                nc.vector.tensor_scalar(XN[:, a, t, :], X[:, 4 * c + t, :], mv[:, s0 + t, 0:1],
                                        rstd[:, s0 + t:s0 + t + 1], ALU.subtract, ALU.mult
                                        ).then_inc(st["xn"].sem, 1)

        def dve_xl(dve, st, c, s):
            for ct in range(CT):
                wait(dve, st["xh"], 2 * c + ct + 1)
                nc.vector.tensor_tensor(XTL[:, s, ct, :], XF[:, s, ct, :], XTH[:, s, ct, :].bitcast(F32),
                                        ALU.subtract).then_inc(st["xl"].sem, 1)

        def dve_front(dve, st, norm, biases, tok, nout):
            qk = len(biases)
            with dve.Fori(0, 2) as p:
                if norm == "ln":
                    for a in range(2):
                        dve_stats(dve, st, 2 * p + a, 4 * a)
                    wait(dve, st["rs"], p + 1)
                for a in range(2):
                    c = 2 * p + a
                    wait(dve, st["tr"], 2 * c - 2)
                    if norm == "ln":
                        dve_norm(dve, st, c, a, 4 * a)
                    else:
                        ou = OU[:, bass.ds(4 * c, TPC), :, :]
                        nc.vector.reciprocal(rsum[:, a, :].rearrange("p (t h) -> p t h", t=TPC),
                                             ou[:, :, :, HD]).then_inc(st["bn"].sem, 4)
                        wait(dve, st["bn"], 4 * c + 4)
                        for t in range(TPC):
                            nc.vector.tensor_tensor(
                                XN[:, a, t, :].rearrange("p (h d) -> p h d", h=HEADS),
                                OU[:, 4 * c + t, :, 0:HD],
                                rsum[:, a, t * HEADS:(t + 1) * HEADS].rearrange("p (h o) -> p h o", o=1)
                                .to_broadcast([P, HEADS, HD]), ALU.mult).then_inc(st["xn"].sem, 1)
                for a in range(2):
                    dve_xl(dve, st, 2 * p + a, a)
                for a in range(2):
                    c = 2 * p + a
                    for o, (name, m) in enumerate(biases):
                        k = qk * c + o
                        wait(dve, st["part1"], k + 1)
                        wait(dve, st["part3"], k - 1)
                        nc.vector.scalar_tensor_tensor(RES[:, o % 2, :], PS[:, 4 + (nout * a + o) % 4, :],
                                                       col(name, m), QP[:, (qk * a + o) % 4, 0, :],
                                                       ALU.add, ALU.subtract).then_inc(st["ev"].sem, 1)
                    for t in range(TPC if tok else 0):
                        o = qk + t
                        wait(dve, st["mm"], nout * c + o + 1)
                        ps = PS[:, 4 + (nout * a + o) % 4, 0:D]
                        if tok == "v":
                            nc.vector.tensor_tensor(V[:, 4 * c + t, :], ps, row("sa_bv"), ALU.add
                                                    ).then_inc(st["ev"].sem, 1)
                        else:
                            nc.vector.tensor_tensor(X[:, 4 * c + t, :], ps, X[:, 4 * c + t, :], ALU.add
                                                    ).then_inc(st["ev"].sem, 1)

        def dve_mlp(dve, st):
            def chunk(c, last):
                for h in range(HB):
                    wait(dve, st["gh"], 8 * c + h + 1)
                    nc.vector.tensor_tensor(XTL[:, 1, h % 2, :], GF[:, h % 2, :], XTH[:, 1, h % 2, :].bitcast(F32),
                                            ALU.subtract).then_inc(st["gl"].sem, 1)
                    if h == 2 and not last:
                        dve_stats(dve, st, c + 1, 0)
                    if h == 5 and not last:
                        wait(dve, st["rs"], c + 2)
                        wait(dve, st["tr"], 2 * c + 2)
                        dve_norm(dve, st, c + 1, 0, 0)
                if not last:
                    dve_xl(dve, st, c + 1, 0)
                for t in range(TPC):
                    wait(dve, st["acc"], 4 * c + t + 1)
                    nc.vector.tensor_tensor(X[:, 4 * c + t, :], PS[:, 4 + t, 0:D], X[:, 4 * c + t, :], ALU.add
                                            ).then_inc(st["ev"].sem, 1)
            dve_stats(dve, st, 0, 0)
            wait(dve, st["rs"], 1)
            dve_norm(dve, st, 0, 0, 0)
            dve_xl(dve, st, 0, 0)
            with dve.Fori(0, NC - 1) as c:
                chunk(c, False)
            chunk(NC - 1, True)

        def dve_mrow(dve, st, h, par):
            wait(dve, st["mtr"], h + 1)
            wait(dve, st[f"mdma{par}"], 16 * half_of(h, par))
            nc.vector.tensor_copy(nrow[:, par, :], PS[0:3 * NT, 7, 0:P // 2].bitcast(BF16)
                                  ).then_inc(st["mrow"].sem, 1)

        def dve_cross(dve, st):
            def unit(u, par, on):
                if on(6):
                    wait(dve, st["pv"], 4 * (u - 5))
                    wait(dve, st["otr"], u - 7)
                    nc.vector.tensor_copy(OS[:, par, :], PS[:, 6, :]).then_inc(st["os"].sem, 1)
                for g in range(2):
                    if on(0):
                        wait(dve, st["smax"], 2 * u + g + 1)
                        if g == 0:
                            wait(dve, st["msplit"], 5 * (u - 1))
                        nc.vector.tensor_reduce(
                            nmax[:, par, 8 * g:8 * g + 8],
                            PS[:, 2 * g:2 * g + 2, :].rearrange("p k (i n) -> p (k i) n", i=4)[:, :, 0:L],
                            AX.X, ALU.max, negate=True).then_inc(st["maxed"].sem, 1)
                    if g == 0 and on(2):
                        dve_mrow(dve, st, u - 2, par)
            pipeline(unit)

        def dve_self(dve, st):
            def unit(u, m, on):
                par = m % 2
                for s in range(KT):
                    if s == 2 and on(1):
                        dve_mrow(dve, st, u - 1, 1 - par)
                    if on(0):
                        for i in (2 * s, 2 * s + 1):
                            wait(dve, st["smax"], 16 * u + i + 1)
                            if i == 0:
                                wait(dve, st["msplit"], 5 * (u - 1))
                            nc.vector.tensor_reduce(nmax[:, par, i:i + 1], PS[:, 2 * (i % 2):2 * (i % 2) + 2, :],
                                                    AX.XY, ALU.max, negate=True).then_inc(st["maxed"].sem, 1)
            pipeline_self(dve, unit)

        def pool_copy(out, in_):
            return nc.gpsimd.tensor_scalar(out, in_, 1.0, 0.0, ALU.mult, ALU.add)

        def pool_rstd(pool, st, n_stats, n_rs, width):
            wait_apart(pool, st["bn2"], n_stats)
            nc.gpsimd.tensor_scalar(var_eps[:, 0:width], mv[:, 0:width, 1], EPS, 1.0, ALU.add, ALU.mult
                                    ).then_inc(s_var, 1)
            return n_rs

        s_var = es.enter_context(nc.semaphore("s_var"))
        var_count = [0]

        def pool_front(pool, st, norm, qk, tok, nout, vbase):
            with pool.Fori(0, 2) as p:
                if norm == "ln":
                    pool_rstd(pool, st, 8 * p + 8, p, 8)
                    pool.wait_ge(s_var, p + vbase + 1)
                    pool.sem_inc(s_passed, 1)
                    nc.gpsimd.tensor_tensor(rstd[:], var_eps[:], half[:], ALU.pow).then_inc(st["rs"].sem, 1)
                for a in range(2):
                    c = 2 * p + a
                    for ct in range(CT):
                        wait_apart(pool, st["xf"], 2 * c + ct + 1)
                        wait_apart(pool, st["mm"], nout * (c - 1))
                        pool_copy(XTH[:, a, ct, :], XF[:, a, ct, :]).then_inc(st["xh"].sem, 1)
                for a in range(2):
                    c = 2 * p + a
                    for o in range(qk):
                        k, slot = qk * c + o, (qk * a + o) % 4
                        wait_apart(pool, st["ev"], nout * c + o + 1)
                        pool_copy(QP[:, slot, 1, :], RES[:, o % 2, :]).then_inc(st["part2"].sem, 1)
                        wait_apart(pool, st["part2"], k + 1)
                        nc.gpsimd.tensor_tensor(QP[:, slot, 2, :], RES[:, o % 2, :], QP[:, slot, 1, :],
                                                ALU.subtract).then_inc(st["part3"].sem, 1)
                    if tok and tok != "v":
                        for t in range(TPC):
                            wait_apart(pool, st["ev"], nout * c + t + 1)
                            nc.gpsimd.tensor_tensor(X[:, 4 * c + t, :], X[:, 4 * c + t, :], row(tok), ALU.add
                                                    ).then_inc(st["xr"].sem, 1)

        def pool_mlp(pool, st, b2, vbase):
            def norm(c, n):
                pool_rstd(pool, st, 4 * c + 4, c, 4)
                pool.wait_ge(s_var, c + vbase + 1)
                pool.sem_inc(s_passed, 1)
                nc.gpsimd.tensor_tensor(rstd[:, 0:4], var_eps[:, 0:4], half[:, 0:4], ALU.pow
                                        ).then_inc(st["rs"].sem, 1)

            def xh(c):
                for ct in range(CT):
                    wait_apart(pool, st["xf"], 2 * c + ct + 1)
                    wait_apart(pool, st["m1"], 8 * c)
                    pool_copy(XTH[:, 0, ct, :], XF[:, 0, ct, :]).then_inc(st["xh"].sem, 1)

            def chunk(c, last):
                for h in range(HB):
                    wait_apart(pool, st["gelu"], 8 * c + h + 1)
                    if h < 2:
                        wait_apart(pool, st["acc"], 4 * c)
                    else:
                        wait_apart(pool, st["m2"], 7 * c + h - 1)
                    pool_copy(XTH[:, 1, h % 2, :], GF[:, h % 2, :]).then_inc(st["gh"].sem, 1)
                    if h == 3 and not last:
                        norm(c + 1, 4)
                if not last:
                    xh(c + 1)
                for t in range(TPC):
                    wait_apart(pool, st["ev"], 4 * c + t + 1)
                    nc.gpsimd.tensor_tensor(X[:, 4 * c + t, :], X[:, 4 * c + t, :], row(b2), ALU.add
                                            ).then_inc(st["xr"].sem, 1)
            norm(0, 4)
            xh(0)
            with pool.Fori(0, NC - 1) as c:
                chunk(c, False)
            chunk(NC - 1, True)

        def pool_msplit(pool, st, h, par, ngroups):
            wait_apart(pool, st["maxed"], ngroups * (h + 1))
            wait_apart(pool, st["mtr"], h - 1)
            src = nmax
            for k in range(3):
                part = nparts[:, par, NT * k:NT * (k + 1)]
                pool_copy(part, src[:, par, :]).then_inc(st["msplit"].sem, 1)
                wait_apart(pool, st["msplit"], 5 * h + 2 * k + 1)
                if k < 2:
                    nc.gpsimd.tensor_tensor(nres[:, par, :], src[:, par, :], part, ALU.subtract
                                            ).then_inc(st["msplit"].sem, 1)
                    wait_apart(pool, st["msplit"], 5 * h + 2 * k + 2)
                    src = nres

        def pool_cross(pool, st, layer):
            def unit(u, par, on):
                if on(4):
                    h = u - 4
                    wait_apart(pool, st["pv"], 4 * (h - 1))
                    nc.gpsimd.tensor_copy(VS[0:L, par, :, 0, 0:HD], VC[:, layer, :, bass.ds(h * HD, HD)]
                                          ).then_inc(st["vs"].sem, 1)
                if on(0):
                    pool_msplit(pool, st, u, par, 2)
            pipeline(unit)

        def pool_self(pool, st):
            Vv = V[:, :, :].rearrange("p (b k) c -> p b k c", b=B)

            def unit(u, m, on):
                par = m % 2
                if on(1):
                    h = u - 1
                    wait_apart(pool, st["pv"], 32 * (h - 1))
                    nc.gpsimd.tensor_copy(VS[:, 1 - par, :, :, 0:HD], Vv[:, :, :, bass.ds(h * HD, HD)]
                                          ).then_inc(st["vs"].sem, 1)
                if on(0):
                    pool_msplit(pool, st, u, par, NT)
            pipeline_self(pool, unit)

        def sp_store_parts(sp, st, dests, nout):
            qk = len(dests)
            with sp.Fori(0, 2) as p:
                for a in range(2):
                    c = 2 * p + a
                    for o, (dst, m) in enumerate(dests):
                        slot = (qk * a + o) % 4
                        wait(sp, st["part3"], qk * c + o + 1)
                        sp.dma_start(dst[m * P:(m + 1) * P, :, bass.ds(c * CH, CH)],
                                     QP[:, slot, :, :]).then_inc(st[f"stored{slot}"].sem, 16)

        def load_q(sp, st, h, par, slot, src):
            parts = src[bass.ds(h * HD, HD), :, :].rearrange("(g d) t n -> g (d t) n", g=1)
            sp.dma_start(STK[0:96, slot, :], parts.to_broadcast([2, 48, T])).then_inc(st[f"stack{par}"].sem, 16)
            sp.dma_start(STK[96:SK, slot, :], src[bass.ds(h * HD, HD), 0, :]).then_inc(st[f"stack{par}"].sem, 16)

        def load_k(sp, st, h, par, slot, src):
            for g in range(2):
                sp.dma_start(STK[48 * g:48 * g + 48, slot, :], src[bass.ds(h * HD, HD), g:g + 1, :]
                             .to_broadcast([HD, 3, T])).then_inc(st[f"stack{par}"].sem, 16)
            sp.dma_start(STK[96:SK, slot, :], src[bass.ds(h * HD, HD), 2, :]).then_inc(st[f"stack{par}"].sem, 16)

        def store_mrow(sp, st, h, par, slot):
            wait(sp, st["mrow"], h + 1)
            sp.dma_start(STK[SK:SKM, slot, :],
                         nrow[:, par, :]
                         ).then_inc(st[f"mdma{par}"].sem, 16)

        def sp_cross(sp, st, src):
            def load(h, par):
                wait(sp, st["st"], 4 * (h - 7))
                wait(sp, st[f"stack{par}"], 32 * half_of(h, par))
                load_q(sp, st, h, par, h % 8, src)

            def unit(u, par, on):
                if on(2):
                    store_mrow(sp, st, u - 2, par, (u - 2) % 8)
                if on(-4):
                    load(u + 4, par)
            for h in range(4):
                load(h, h % 2)
            pipeline(unit, last=HEADS + 2)

        def sp_self(sp, st):
            def load(h, m):
                par = m % 2
                wait(sp, st["st"], 32 * (h - 3))
                wait(sp, st[f"stack{par}"], 80 * half_of(h, par))
                load_q(sp, st, h, par, m, q_parts[1])
                load_k(sp, st, h, par, m + 4, k_parts)

            def unit(u, m, on):
                if on(1):
                    store_mrow(sp, st, u - 1, (m + 1) % 2, (m - 1) % 4)
                if on(-2):
                    load(u + 2, (m + 2) % 4)
            load(0, 0)
            load(1, 1)
            pipeline_self(sp, unit)

        block = es.enter_context(nc.Block())
        qk0 = [("zero", 0), ("zero", 1)]
        qk1 = [("sa_bq", 0), ("sa_bq", 1), ("sa_bk", 0), ("sa_bk", 1)]
        qk2 = [("ca_bq", 0), ("ca_bq", 1)]

        @block.sync
        def _(sp):
            for counting in sems.values():
                sp.sem_inc(counting, CREDIT)
            sp.dma_start(colv[:], cols_d).then_inc(ld["vec"], 16)
            sp.dma_start(CX[:], ctx_d.rearrange("b t c -> t b c")).then_inc(ld["ctx"], 16)
            sp.dma_start(X[:], x_d.rearrange("b (t p) c -> p (b t) c", p=P)).then_inc(ld["x"], 16)
            sp.dma_start(RAW[:, 0:2, :], w_d[:, 0:2, :]).then_inc(ld["wq"], 16)
            sp.dma_start(WCA[:, 0, :], wkv_d[0:P, :]).then_inc(ld["wc"], 16)
            sp.dma_start(WCB[:, 0, :], wkv_d[P:CTX, :]).then_inc(ld["wc"], 16)
            for i, w in enumerate((wck_d, wcv_d)):
                sp.dma_start(WCA[:, 1, i * D:(i + 1) * D], w[0:P, :]).then_inc(ld["wc"], 16)
                sp.dma_start(WCB[:, 1, i * D:(i + 1) * D], w[P:CTX, :]).then_inc(ld["wc"], 16)
            sp.dma_start(RAW[:, 2:NWB, :], w_d[:, 2:NWB, :]).then_inc(ld["w"], 16)
            sp.dma_start(rowv[:], rows_d.rearrange("(o r) c -> o r c", o=1).to_broadcast([P, len(ROWS), D])
                         ).then_inc(ld["vec"], 16)
            for i in range(4):
                wait(sp, cx["c_p3"], i + 1)
                sp.dma_start(kc_parts[i // 2][(i % 2) * P:(i % 2 + 1) * P, :, :],
                             KP[:, i, :, :]).then_inc(cx["c_store"].sem, 16)
            wait(sp, cx["c_store"], 64)
            sp.wait_ge(s_const2, 3)
            for layer in range(2):
                for g in range(GROUPS):
                    rows = slice(48 * (g // 3) + g % 3, 48 * (g // 3) + 48, 3) if g < 6 else slice(96, SK)
                    sp.dma_start(KSC[rows, layer, :, :],
                                 kc_parts[layer][:, g // 3, :].rearrange("(h d) n -> d h n", d=HD)
                                 ).then_inc(cx["c_stack"].sem, 16)
            sp_store_parts(sp, A0, [(q_parts[0], 0), (q_parts[0], 1)], 2)
            join(sp, A0, "stored0 stored1 stored2 stored3")
            join(sp, sp0, "w_low")
            sp_cross(sp, C0, q_parts[0])
            join(sp, C0, ALL_C)
            sp.dma_start(RAW[:, 0:8, :], wm_d).then_inc(ld["mlp1"], 16)
            sp_store_parts(sp, A1, [(q_parts[1], 0), (q_parts[1], 1), (k_parts, 0), (k_parts, 1)], 8)
            join(sp, A1, "stored0 stored1 stored2 stored3")
            join(sp, sp1, "w_low")
            join(sp, ones_set, "ones_rows")
            sp_self(sp, C1)
            sp_store_parts(sp, A2, [(q_parts[2], 0), (q_parts[2], 1)], 2)
            join(sp, A2, "stored0 stored1 stored2 stored3")
            join(sp, C1, ALL_C)
            sp_cross(sp, C2, q_parts[2])
            for c in range(NC):
                wait(sp, M1["xr"], 4 * c + 4)
                b, h = c // 2, c % 2
                sp.dma_start(out_d[b, h * CH:(h + 1) * CH, :].rearrange("(t p) c -> p t c", p=P),
                             X[:, 4 * c:4 * c + 4, :]).then_inc(s_out, 16)
            sp.wait_ge(s_out, 16 * NC)

        @block.tensor
        def _(pe):
            pe.wait_ge(s_const, 3)
            pe.wait_ge(ld["ctx"], 16)
            for layer in (1, 0):
                src = CX if layer else CN
                if layer == 0:
                    wait(pe, cx["c_n"], 2)
                for k, (c0, cn) in enumerate(((0, P), (P, CTX - P))):
                    for b in range(B):
                        last = nc.tensor.transpose(PS[0:cn, 2 * layer + k, b * L:(b + 1) * L],
                                                   src[:, b, c0:c0 + cn], identf[0:L, 0:L])
                    last.then_inc(cx["c_tr"].sem, 1)
            pe.wait_ge(ld["wc"], 96)
            wait(pe, cx["c_yt"], 4)
            for i in range(4):
                layer, m = i // 2, i % 2
                nc.tensor.matmul(PS[:, 4 + i, 0:B * L], WCA[:, layer, m * P:(m + 1) * P], YT[:, 2 * layer, :],
                                 start=True, stop=False)
                nc.tensor.matmul(PS[:, 4 + i, 0:B * L], WCB[:, layer, m * P:(m + 1) * P],
                                 YT[0:CTX - P, 2 * layer + 1, :], start=False, stop=True
                                 ).then_inc(cx["c_mm"].sem, 1)
            for i in range(4):
                layer, b = i // 2, i % 2
                nc.tensor.matmul(PS[0:L, i, 0:D], YT[:, 2 * layer, b * L:(b + 1) * L], WCA[:, layer, D:2 * D],
                                 start=True, stop=False)
                nc.tensor.matmul(PS[0:L, i, 0:D], YT[0:CTX - P, 2 * layer + 1, b * L:(b + 1) * L],
                                 WCB[:, layer, D:2 * D], start=False, stop=True).then_inc(cx["c_mm"].sem, 1)
            join(pe, cx, "c_r c_v")
            wait(pe, sp0["w_low"], 2)
            pe_front(pe, A0, [(WB_Q0, 0), (WB_Q0, 1)], [], 2)
            join(pe, A0, "xf ev")
            join(pe, cx, "c_stack")
            pe.wait_ge(s_const2, 4)
            pe_cross(pe, C0, 0)
            join(pe, C0, "maxed exped os ou")
            join(pe, sp0, "w_low")
            pe_front(pe, P0, [], [WB_P0], 4)
            join(pe, P0, "xf ev")
            pe_mlp(pe, M0)
            join(pe, M0, "xf gelu ev")
            pe_front(pe, A1, [(WB_SQ, 0), (WB_SQ, 1), (WB_SK, 0), (WB_SK, 1)], [WB_SV], 8)
            join(pe, A1, "xf ev")
            pe_self(pe, C1)
            join(pe, C1, "maxed exped os ou")
            pe_front(pe, P1, [], [WB_SO], 4)
            join(pe, P1, "xf ev")
            pe_front(pe, A2, [(WB_CQ, 0), (WB_CQ, 1)], [], 2)
            join(pe, A2, "xf ev")
            pe_cross(pe, C2, 1)
            join(pe, C2, "maxed exped os ou")
            pe_front(pe, P2, [], [WB_CO], 4)
            join(pe, P2, "xf ev")
            join(pe, sp1, "w_low")
            pe_mlp(pe, M1)

        @block.scalar
        def _(act):
            act.wait_ge(ld["vec"], 32)
            for layer in (1, 0):
                for k, cn in enumerate((P, CTX - P)):
                    i = 2 * layer + k
                    wait(act, cx["c_tr"], (3 if layer == 0 else 1) + k)
                    if layer:
                        y = nc.scalar.copy(YT[0:cn, i, :], PS[0:cn, i, 0:B * L])
                    else:
                        y = nc.scalar.activation(YT[0:cn, i, :], PS[0:cn, i, 0:B * L], ACT.Identity,
                                                 scale=col("l0_ln2_w", k)[0:cn], bias=col("l0_ln2_b", k)[0:cn])
                    y.then_inc(cx["c_yt"].sem, 1)
            for i in range(4):
                wait(act, cx["c_mm"], i + 1)
                nc.scalar.activation(KP[:, i, 0, :], PS[:, 4 + i, 0:B * L], ACT.Identity,
                                     bias=col("ca_bk" if i > 1 else "zero", i % 2)).then_inc(cx["c_p1"].sem, 1)
            act_front(act, A0, "l0_ln1_w", "l0_ln1_b", qk0, 2)
            join(act, A0, "xl part3 stored0 stored1 stored2 stored3")
            join(act, cx, "c_store")
            act_cross(act, C0)
            join(act, C0, "pv otr")
            act_front(act, P0, None, None, [], 4)
            join(act, P0, "xl")
            act_mlp(act, M0, "l0_ln3_w", "l0_ln3_b", "l0_b1")
            join(act, M0, "xl gl")
            act_front(act, A1, "l1_ln1_w", "l1_ln1_b", qk1, 8)
            join(act, A1, "xl part3 stored0 stored1 stored2 stored3")
            join(act, P0, "xn")
            act_self(act, C1)
            join(act, C1, "pv otr")
            act_front(act, P1, None, None, [], 4)
            join(act, P1, "xl")
            act_front(act, A2, "l1_ln2_w", "l1_ln2_b", qk2, 2)
            join(act, A2, "xl part3 stored0 stored1 stored2 stored3")
            act_cross(act, C2)
            join(act, C2, "pv otr")
            act_front(act, P2, None, None, [], 4)
            join(act, P2, "xl")
            act_mlp(act, M1, "l1_ln3_w", "l1_ln3_b", "l1_b1")

        @block.vector
        def _(dve):
            dve.wait_ge(s_const, 3)
            dve.wait_ge(ld["vec"], 32)
            nc.vector.tensor_copy(identb[:], identf[:]).then_inc(s_const2, 1)
            dve.wait_ge(ld["ctx"], 16)
            for b in range(B):
                nc.vector.bn_stats(bst[0:L, b, :], CX[:, b, :]).then_inc(cx["c_bn"].sem, 1)
            for b in range(B):
                wait(dve, cx["c_bn"], b + 1)
                nc.vector.bn_aggr(mv[0:L, b, :], bst[0:L, b, :]).then_inc(cx["c_bn2"].sem, 1)
            wait(dve, cx["c_rs"], 1)
            for b in range(B):
                nc.vector.tensor_scalar(CN[:, b, :], CX[:, b, :], mv[0:L, b, 0:1], rstd[0:L, b:b + 1],
                                        ALU.subtract, ALU.mult).then_inc(cx["c_n"].sem, 1)

            def split_low(st, n, blk):
                wait(dve, st["w_high"], n + 1)
                raw = RAW[:, blk if st is sp0 else blk - WB_W1, :]
                nc.vector.tensor_tensor(WL[:, blk, :], raw, WH[:, blk, :].bitcast(F32), ALU.subtract
                                        ).then_inc(st["w_low"].sem, 1)
            for blk in range(2):
                split_low(sp0, blk, blk)
            for i in range(4):
                wait(dve, cx["c_p1"], i + 1)
                nc.vector.scalar_tensor_tensor(KR[:, i, :], PS[:, 4 + i, 0:B * L],
                                               col("ca_bk" if i > 1 else "zero", i % 2), KP[:, i, 0, :],
                                               ALU.add, ALU.subtract).then_inc(cx["c_r"].sem, 1)
            for i in range(4):
                wait(dve, cx["c_r"], i + 1)
                nc.vector.tensor_copy(KP[:, i, 1, :], KR[:, i, :]).then_inc(cx["c_p2"].sem, 1)
            for i in range(4):
                wait(dve, cx["c_p2"], i + 1)
                nc.vector.tensor_tensor(KP[:, i, 2, :], KR[:, i, :], KP[:, i, 1, :], ALU.subtract
                                        ).then_inc(cx["c_p3"].sem, 1)
            for i in range(4):
                wait(dve, cx["c_mm"], 5 + i)
                if i < 2:
                    v = nc.vector.tensor_copy(VC[:, 0, i, :], PS[0:L, i, 0:D])
                else:
                    v = nc.vector.tensor_tensor(VC[:, 1, i - 2, :], PS[0:L, i, 0:D], row("ca_bv")[0:L], ALU.add)
                v.then_inc(cx["c_v"].sem, 1)
            dve.wait_ge(ld["x"], 16)
            dve_front(dve, A0, "ln", qk0, None, 2)
            for blk in range(2, NWB):
                split_low(sp0, blk, blk)
            join(dve, A0, "xh part3 stored0 stored1 stored2 stored3")
            dve_cross(dve, C0)
            join(dve, C0, "ou")
            dve_front(dve, P0, "sum", [], "x", 4)
            join(dve, P0, "xr")
            dve_mlp(dve, M0)
            join(dve, M0, "xr acc")
            dve_front(dve, A1, "ln", qk1, "v", 8)
            for k in range(8):
                split_low(sp1, k, WB_W1 + k)
            dve_self(dve, C1)
            join(dve, C1, "ou")
            dve_front(dve, P1, "sum", [], "x", 4)
            join(dve, P1, "xr")
            dve_front(dve, A2, "ln", qk2, None, 2)
            join(dve, A2, "part3 stored0 stored1 stored2 stored3")
            dve_cross(dve, C2)
            join(dve, C2, "ou")
            dve_front(dve, P2, "sum", [], "x", 4)
            join(dve, P2, "xr")
            dve_mlp(dve, M1)

        @block.gpsimd
        def _(pool):
            nc.gpsimd.memset(identf[:], 0.0).then_inc(s_const, 1)
            nc.gpsimd.memset(half[:], -0.5).then_inc(s_const, 1)
            pool.wait_ge(s_const, 1)
            nc.gpsimd.affine_select(out=identf[:], in_=identf[:], compare_op=ALU.not_equal, fill=1.0, base=0,
                                    pattern=[[-1, P]], channel_multiplier=1).then_inc(s_const, 1)
            wait(pool, cx["c_bn2"], 2)
            nc.gpsimd.tensor_scalar(var_eps[0:L, 0:2], mv[0:L, 0:2, 1], EPS, 1.0, ALU.add, ALU.mult).then_inc(s_var, 1)
            pool.wait_ge(s_var, 1)
            pool.wait_ge(s_const, 3)
            nc.gpsimd.tensor_tensor(rstd[0:L, 0:2], var_eps[0:L, 0:2], half[0:L, 0:2], ALU.pow
                                    ).then_inc(cx["c_rs"].sem, 1)
            nc.gpsimd.memset(VS[:], 0.0).then_inc(s_const2, 1)
            pool.wait_ge(s_const2, 2)
            nc.gpsimd.memset(KSC[96:P, :, :, :], 1.0).then_inc(s_const2, 1)
            pool.wait_ge(s_const2, 3)
            nc.gpsimd.memset(VS[:, :, :, :, HD:HD + 1], 1.0).then_inc(s_const2, 1)
            pool.wait_ge(ld["vec"], 32)
            pool.wait_ge(ld["wq"], 16)
            for blk in range(2):
                pool_copy(WH[:, blk, :], RAW[:, blk, :]).then_inc(sp0["w_high"].sem, 1)
            pool_front(pool, A0, "ln", 2, None, 2, 1)
            pool.wait_ge(ld["w"], 16)
            for blk in range(2, NWB):
                pool_copy(WH[:, blk, :], RAW[:, blk, :]).then_inc(sp0["w_high"].sem, 1)
            pool.wait_ge(s_const2, 4)
            join(pool, cx, "c_v")
            pool_cross(pool, C0, 0)
            pool_front(pool, P0, "sum", 0, "l0_bproj", 4, 0)
            join(pool, P0, "mm")
            pool_mlp(pool, M0, "l0_b2", 3)
            join(pool, M0, "m1 acc")
            join(pool, C0, ALL_C)
            pool_front(pool, A1, "ln", 4, "v", 8, 7)
            pool.wait_ge(ld["mlp1"], 16)
            for k in range(8):
                pool_copy(WH[:, WB_W1 + k, :], RAW[:, k, :]).then_inc(sp1["w_high"].sem, 1)
            join(pool, sp1, "w_low")
            nc.gpsimd.memset(STK[96:P, 4:8, :], 1.0).then_inc(ones_set["ones_rows"].sem, 1)
            join(pool, ones_set, "ones_rows")
            join(pool, A1, "ev")
            pool_self(pool, C1)
            pool_front(pool, P1, "sum", 0, "sa_bo", 4, 0)
            join(pool, P1, "mm")
            pool_front(pool, A2, "ln", 2, None, 2, 9)
            pool_cross(pool, C2, 1)
            join(pool, A2, "mm")
            pool_front(pool, P2, "sum", 0, "ca_bo", 4, 0)
            join(pool, P2, "mm")
            pool_mlp(pool, M1, "l1_b2", 11)


def kernel(**inputs):
    import numpy as np
    import concourse.bacc as bacc
    from concourse.bass_utils import run_bass_kernel_spmd

    a = {k: np.asarray(v) for k, v in inputs.items()}
    l0, l1 = "L0_xattn_", "L1_xattn_"

    def square(w):
        k, n = w.shape
        return w.reshape(k // P, P, n).transpose(1, 0, 2).reshape(P, -1, 512)

    weights = np.concatenate(
        [square(a[l0 + "Wq"]), square(a[l0 + "Wproj"])]
        + [square(a[l1 + n].T) for n in ("sa_wq", "sa_wk", "sa_wv", "sa_wo", "ca_wq", "ca_wo")]
        + [square(a[l0 + "W1"]), square(a[l0 + "W2"])], axis=1)
    weights_mlp1 = np.concatenate([square(a[l1 + "mlp_w1"].T), square(a[l1 + "mlp_w2"].T)], axis=1)

    named = {"l0_ln1_w": l0 + "ln1_w", "l0_ln1_b": l0 + "ln1_b", "l0_ln3_w": l0 + "ln3_w", "l0_ln3_b": l0 + "ln3_b",
             "l1_ln1_w": l1 + "ln1_g", "l1_ln1_b": l1 + "ln1_b", "l1_ln2_w": l1 + "ln2_g", "l1_ln2_b": l1 + "ln2_b",
             "l1_ln3_w": l1 + "ln3_g", "l1_ln3_b": l1 + "ln3_b", "l0_ln2_w": l0 + "ln2_w", "l0_ln2_b": l0 + "ln2_b",
             "sa_bq": l1 + "sa_bq", "sa_bk": l1 + "sa_bk", "ca_bq": l1 + "ca_bq", "ca_bk": l1 + "ca_bk",
             "l0_b1": l0 + "b1", "l1_b1": l1 + "mlp_b1"}
    cols = np.zeros((P, NCOLS), np.float32)
    for name, (at, width) in COLS.items():
        if name in named:
            v = a[named[name]]
            for i in range(width):
                part = v[i * P:(i + 1) * P]
                cols[:len(part), at + i] = part
    rows = np.stack([a[n] for n in (l0 + "bproj", l0 + "b2", l1 + "sa_bv", l1 + "sa_bo", l1 + "ca_bo",
                                    l1 + "mlp_b2", l1 + "ca_bv")])
    arrays = {"x": a["x"], "ctx": a["ctx_768"], "weights": weights, "weights_mlp1": weights_mlp1,
              "wkv": a[l0 + "Wkv"], "wck": a[l1 + "ca_wk"].T, "wcv": a[l1 + "ca_wv"].T, "cols": cols, "rows": rows}
    arrays = {k: np.ascontiguousarray(v) for k, v in arrays.items()}

    nc = bacc.Bacc("TRN2", target_bir_lowering=False, num_devices=1, dynamic_dma_scratch_size=1024)
    args = [nc.dram_tensor(k, v.shape, mybir.dt.from_np(v.dtype), kind="ExternalInput").ap()
            for k, v in arrays.items()]
    out = nc.dram_tensor("out", (B, S, D), F32, kind="ExternalOutput").ap()
    build(nc, *args, out)
    r = run_bass_kernel_spmd(nc, [arrays], core_ids=[0])
    return r.results[0]["out"]
```

```python
from contextlib import ExitStack

import concourse.bass as bass
from concourse import mybir

F32, F32R, BF16 = mybir.dt.float32, mybir.dt.float32r, mybir.dt.bfloat16
ALU, ACT, AX = mybir.AluOpType, mybir.ActivationFunctionType, mybir.AxisListType

P = 128
B, S, D, CTX, L = 2, 1024, 256, 192, 77
HEADS, HD, HID = 16, 16, 1024
T = B * S
NT = T // P
CH = 512
NC = T // CH
TPC = CH // P
CT = D // P
KT = S // P
HB = HID // P
EPS = 1e-5
SCALE = HD ** -0.5
GROUPS = 7
SK = GROUPS * HD
SKM = SK + 3
VW = 32
OW = HD + 1
CREDIT = 64

COLS, ROWS = {}, {}
for _n, _w in (("l0_ln1_w", 2), ("l0_ln1_b", 2), ("l0_ln3_w", 2), ("l0_ln3_b", 2), ("l1_ln1_w", 2),
               ("l1_ln1_b", 2), ("l1_ln2_w", 2), ("l1_ln2_b", 2), ("l1_ln3_w", 2), ("l1_ln3_b", 2),
               ("l0_ln2_w", 2), ("l0_ln2_b", 2), ("sa_bq", 2), ("sa_bk", 2), ("ca_bq", 2), ("ca_bk", 2),
               ("l0_b1", 8), ("l1_b1", 8), ("zero", 2)):
    COLS[_n] = (sum(w for _, w in COLS.values()), _w)
NCOLS = sum(w for _, w in COLS.values())
for _n in ("l0_bproj", "l0_b2", "sa_bv", "sa_bo", "ca_bo", "l1_b2", "ca_bv"):
    ROWS[_n] = len(ROWS)

WB_Q0, WB_P0, WB_SQ, WB_SK, WB_SV, WB_SO, WB_CQ, WB_CO, WB_W1, WB_W2 = 0, 1, 2, 3, 4, 5, 6, 7, 8, 12
NWB = 16


class Tally:

    def __init__(self, sem, start, total):
        self.sem, self.start, self.total = sem, start, total

    def at(self, n):
        return self.sem, n + self.start

    @property
    def end(self):
        return self.start + self.total


class Stage(dict):
    prev = w = b = None
    two = True
    nout = qk = 0

    def slot(self, c):
        return c % 2 if self.two else 0

    def freed(self, c, ct):
        return 2 * c + ct - (3 if self.two and c > 0 else 1)


def build(nc, x_d, ctx_d, w_d, wm_d, wkv_d, wck_d, wcv_d, cols_d, rows_d, out_d):
    es = ExitStack()
    with es:
        def sb(name, shape, dt):
            return es.enter_context(nc.sbuf_tensor(name, shape, dt))

        def scratch(name, n):
            return nc.dram_tensor(name, [D, 3, n], BF16, kind="Internal").ap()
        q_parts = [scratch("q_parts_l0", T), scratch("q_parts_self", T), scratch("q_parts_cross", T)]
        k_parts = scratch("k_parts_self", T)
        kc_parts = [scratch("kc_parts_l0", B * L), scratch("kc_parts_l1", B * L)]

        X = sb("X", [P, NT, D], F32)
        WH = sb("WH", [P, NWB, 512], F32R)
        WL = sb("WL", [P, NWB, 512], F32R)
        XTH = sb("XTH", [P, 2, CT, CH], F32R)
        XTL = sb("XTL", [P, 2, CT, CH], F32R)
        XN = sb("XN", [P, 2, TPC, D], F32)
        SCR = sb("SCR", [P, 6144], F32)
        STK = sb("STK", [P, 8, T], BF16)
        V = sb("V", [P, NT, D], F32)
        VS = sb("VS", [P, 2, B, KT, VW], F32)
        OU = sb("OU", [P, NT, HEADS, OW], F32)
        KSC = sb("KSC", [P, 2, HEADS, B * L], BF16)
        VC = sb("VC", [L, 2, B, D], F32)
        colv = sb("colv", [P, NCOLS], F32)
        rowv = sb("rowv", [P, len(ROWS), D], F32)
        identf = sb("identf", [P, P], F32)
        identb = sb("identb", [P, P], BF16)
        bst = sb("bst", [P, NT, 6], F32)
        mv = sb("mv", [P, NT, 2], F32)
        var_eps = sb("var_eps", [P, NT], F32)
        rstd = sb("rstd", [P, NT], F32)
        half = sb("half", [P, NT], F32)
        rsum = sb("rsum", [P, 2, TPC * HEADS], F32)
        nmax = sb("nmax", [P, 2, NT], F32)
        nres = sb("nres", [P, 2, NT], F32)
        nparts = sb("nparts", [P, 2, 3 * NT], BF16)
        nrow = sb("nrow", [3 * NT, 2, P], BF16)
        PS = es.enter_context(nc.psum_tensor("PS", [P, 8, 512], F32))

        XF = SCR[:, 0:2048].rearrange("p (a c n) -> p a c n", a=2, c=CT)
        RES = SCR[:, 2048:3072].rearrange("p (r n) -> p r n", r=2)
        QP = SCR[:, 3072:6144].bitcast(BF16).rearrange("p (s t n) -> p s t n", s=4, t=3)
        GF = SCR[:, 2048:3072].rearrange("p (r n) -> p r n", r=2)
        PT = SCR[:, 0:4096].rearrange("p (s n) -> p s n", s=2)
        OS = SCR[:, 4096:5120].rearrange("p (s n) -> p s n", s=2)
        RAW = STK[:, :, :].rearrange("p s n -> p (s n)").bitcast(F32).rearrange("p (b n) -> p b n", b=NWB)
        Vf = V[:, :, :].rearrange("p t c -> p (t c)")
        RAW2 = Vf.rearrange("p (b n) -> p b n", b=8)
        WCA = RAW[:, 8:10, :]
        WCB = RAW[0:CTX - P, 10:12, :]
        OUf = OU[:, :, :, :].rearrange("p t h w -> p (t h w)")
        CX = OUf[0:L, 0:384].rearrange("p (b c) -> p b c", b=B)
        CN = OUf[0:L, 384:768].rearrange("p (b c) -> p b c", b=B)
        YT = OUf[:, 768:768 + 4 * B * L].rearrange("p (k n) -> p k n", k=4)
        KR = OUf[:, 1408:1408 + 4 * B * L].rearrange("p (k n) -> p k n", k=4)
        KP = OUf[:, 2048:2048 + 6 * B * L].bitcast(BF16).rearrange("p (k t n) -> p k t n", k=4, t=3)

        def whl(w, blk, ct, off, n):
            return w[:, blk, ct * D + off:ct * D + off + n]

        def w1(w, ct, h):
            f = ct * HID + h * P
            return w[:, WB_W1 + f // 512, f % 512:f % 512 + P]

        def w2(w, h):
            f = h * D
            return w[:, WB_W2 + f // 512, f % 512:f % 512 + D]

        def col(name, i):
            return colv[:, COLS[name][0] + i:COLS[name][0] + i + 1]

        def row(name):
            return rowv[:, ROWS[name], :]

        sems, starts = {}, {}

        def stage(**totals):
            out = Stage()
            for name, total in totals.items():
                if name not in sems:
                    sems[name] = es.enter_context(nc.semaphore(name))
                    starts[name] = CREDIT
                out[name] = Tally(sems[name], starts[name], total)
                starts[name] += total
            return out

        ld = {n: es.enter_context(nc.semaphore("ld_" + n)) for n in ("x0", "x1", "x2", "x3", "ctx", "wq", "w", "wc", "cols", "rows", "mlp0", "mlp1")}
        s_const = es.enter_context(nc.semaphore("s_const"))
        s_const2 = es.enter_context(nc.semaphore("s_const2"))
        s_ones = es.enter_context(nc.semaphore("s_ones"))
        s_credit = es.enter_context(nc.semaphore("s_credit"))
        s_passed = es.enter_context(nc.semaphore("s_passed"))
        s_out = es.enter_context(nc.semaphore("s_out"))

        def front(nout, qk, prev=None, w=None, b=None):
            t = dict(bn=NT, bn2=NT if qk else 0, var=NC if qk else 0, rs=NC if qk else 0, xn=NT, tr=NC * CT,
                     xf=NC * CT, xh=NC * CT, xl=NC * CT, mm=nout * NC, ev=nout * NC)
            if qk:
                t |= dict(part1=qk * NC, part2=qk * NC, part3=qk * NC)
                t |= {f"stored{s}": 16 * qk * NC // 4 for s in range(4)}
            else:
                t |= dict(xb=NT)
            st = stage(**t)
            st.nout, st.qk, st.prev, st.w, st.b = nout, qk, prev, w, b
            return st

        def mlp(prev, w, b):
            st = stage(bn=NT, bn2=NT, var=NC, rs=NC, xn=NT, tr=NC * CT, xf=NC * CT, xh=NC * CT, xl=NC * CT,
                       m1=HB * NC, gelu=HB * NC, gh=HB * NC, gl=HB * NC, m2=(HB - 1) * NC, ev=NT, acc=NT, xb=NT)
            st.two, st.prev, st.w, st.b = False, prev, w, b
            return st

        def attention(keys_steps, loads, groups):
            n = HEADS
            return stage(stack0=loads * n // 2, stack1=loads * n // 2, smax=groups * n, maxed=groups * n,
                         msplit=5 * n, mtr=n, mrow=n, mdma0=8 * n, mdma1=8 * n,
                         st=4 * keys_steps * n, exped=4 * keys_steps * n, vs=n, pv=4 * keys_steps * n,
                         os=n, otr=n, ou=n)

        cx = stage(c_bn=2, c_bn2=2, c_var=1, c_rs=1, c_n=2, c_tr=4, c_yt=4, c_mm=8, c_p1=4, c_r=4, c_p2=4, c_p3=4,
                   c_v=4, c_store=16 * 4, c_stack=16 * 14)
        split0 = stage(w_high=NWB, low_dve=5, low_pool=NWB - 5)
        A0 = front(2, 2, None, "l0_ln1_w", "l0_ln1_b")
        C0 = attention(1, 32, 2)
        P0 = front(4, 0)
        M0 = mlp(P0, "l0_ln3_w", "l0_ln3_b")
        A1 = front(8, 4, M0, "l1_ln1_w", "l1_ln1_b")
        ones_set = stage(ones_rows=32)
        C1 = attention(KT, 80, NT)
        P1 = front(4, 0)
        A2 = front(2, 2, P1, "l1_ln2_w", "l1_ln2_b")
        split1 = stage(w_high=8, low_pool=8)
        C2 = attention(1, 32, 2)
        P2 = front(4, 0)
        M1 = mlp(P2, "l1_ln3_w", "l1_ln3_b")

        def join(eng, st, names):
            for name in names.split():
                eng.wait_ge(st[name].sem, st[name].end)

        ALL_C = "stack0 stack1 smax maxed msplit mtr mrow mdma0 mdma1 st exped vs pv os otr ou"


        def pe_transposes(pe, st, c):
            s = st.slot(c)
            pe.wait_ge(*st["xn"].at(4 * c + 4))
            for ct in range(CT):
                pe.wait_ge(*st["xf"].at(st.freed(c, ct)))
                for t in range(TPC):
                    last = nc.tensor.transpose(PS[:, 2 * s + ct, t * P:(t + 1) * P],
                                               XN[:, s, t, ct * P:(ct + 1) * P], identf[:])
                last.then_inc(st["tr"].sem, 1)

        def split_mm(out, pairs):
            n = len(pairs)
            for k, (lh, ll, rh, rl) in enumerate(pairs):
                nc.tensor.matmul(out, lh, rh, start=(k == 0), stop=False)
                nc.tensor.matmul(out, ll, rh, start=False, stop=False)
                last = nc.tensor.matmul(out, lh, rl, start=False, stop=(k == n - 1))
            return last

        def pe_front(pe, st, tform, tokform, nxt=None):
            outs = [(blk, m, None) for blk, m in tform] + [(blk, None, t) for blk in tokform for t in range(TPC)]
            for c in range(NC):
                a = c % 2
                pe.wait_ge(*st["xl"].at(2 * c + 2))
                for o, (blk, m, t) in enumerate(outs):
                    k = len(outs) * c + o
                    pe.wait_ge(*st["ev"].at(k - 3))
                    if m is not None:
                        out = PS[:, 4 + k % 4, :]
                        pairs = [(whl(WH, blk, ct, m * P, P), whl(WL, blk, ct, m * P, P),
                                  XTH[:, a, ct, :], XTL[:, a, ct, :]) for ct in range(CT)]
                    else:
                        out = PS[:, 4 + k % 4, 0:D]
                        pairs = [(XTH[:, a, ct, t * P:(t + 1) * P], XTL[:, a, ct, t * P:(t + 1) * P],
                                  whl(WH, blk, ct, 0, D), whl(WL, blk, ct, 0, D)) for ct in range(CT)]
                    split_mm(out, pairs).then_inc(st["mm"].sem, 1)
                    if o == len(outs) // 2 - 1:
                        if c < NC - 2:
                            pe_transposes(pe, st, c + 2)
                        elif nxt and (nxt.two or c == NC - 2):
                            pe_transposes(pe, nxt, c - NC + 2)

        def pe_mlp(pe, st, nxt=None):
            def m1(c, h):
                pe.wait_ge(*st["gelu"].at(8 * c + h - 1))
                split_mm(PS[:, 2 + h % 2, :], [(w1(WH, ct, h), w1(WL, ct, h), XTH[:, 0, ct, :], XTL[:, 0, ct, :])
                                               for ct in range(CT)]).then_inc(st["m1"].sem, 1)

            def m2(c, h):
                pe.wait_ge(*st["gh"].at(8 * c + h + 1))
                for t in range(TPC):
                    if h == 0:
                        pe.wait_ge(*st["ev"].at(4 * c + t - 3))
                    g = XTH[:, 1, h % 2, t * P:(t + 1) * P]
                    nc.tensor.matmul(PS[:, 4 + t, 0:D], g, w2(WH, h), start=(h == 0), stop=False)
                    nc.tensor.matmul(PS[:, 4 + t, 0:D], g, w2(WL, h), start=False, stop=False)
                pe.wait_ge(*st["gl"].at(8 * c + h + 1))
                for t in range(TPC):
                    mm = nc.tensor.matmul(PS[:, 4 + t, 0:D], XTL[:, 1, h % 2, t * P:(t + 1) * P], w2(WH, h),
                                          start=False, stop=(h == HB - 1))
                    if h == HB - 1:
                        mm.then_inc(st["acc"].sem, 1)
                    elif t == TPC - 1:
                        mm.then_inc(st["m2"].sem, 1)

            def chunk(c, last):
                pe.wait_ge(*st["xl"].at(2 * c + 2))
                m1(c, 0)
                for h in range(1, HB):
                    m1(c, h)
                    if h < HB - 1:
                        m2(c, h - 1)
                if not last:
                    pe_transposes(pe, st, c + 1)
                elif nxt:
                    pe_transposes(pe, nxt, 0)
                m2(c, HB - 2)
                m2(c, HB - 1)

            for c in range(NC):
                chunk(c, c == NC - 1)
            if nxt:
                join(pe, st, "gelu")
                pe_transposes(pe, nxt, 1)

        def pe_mrow(pe, st, h, par, out):
            pe.wait_ge(*st["msplit"].at(5 * h + 5))
            pe.wait_ge(*st["mrow"].at(h))
            pe.wait_ge(*st["ou"].at(out))
            pe.sem_inc(s_passed, 1)
            nc.tensor.transpose(PS[0:3 * NT, 7, 0:P // 2].bitcast(BF16), nparts[:, par, :], identb[:]
                                ).then_inc(st["mtr"].sem, 1)

        def pe_ot(pe, st, h, par):
            pe.wait_ge(*st["os"].at(h + 1))
            pe.wait_ge(*st["ou"].at(h))
            for i in range(TPC):
                last = nc.tensor.transpose(PS[:, 7, i * P:(i + 1) * P], OS[:, par, i * P:(i + 1) * P], identf[:])
            last.then_inc(st["otr"].sem, 1)

        def pe_cross(pe, st, layer):
            def smax(h, par, g):
                if g == 0:
                    pe.wait_ge(*st[f"stack{par}"].at(32 * half_of(h, par) + 32))
                pe.wait_ge(*st["maxed"].at(2 * h + g - 1))
                for i in range(8):
                    tile = 8 * g + i
                    b = g
                    last = nc.tensor.matmul(PS[:, 2 * g + i // 4, (i % 4) * P:(i % 4) * P + L],
                                            STK[0:SK, h % 8, tile * P:(tile + 1) * P],
                                            KSC[0:SK, layer, h, b * L:(b + 1) * L], start=True, stop=True)
                last.then_inc(st["smax"].sem, 1)

            def score(h, par, j):
                if j == 0:
                    pe.wait_ge(*st[f"mdma{par}"].at(16 * half_of(h, par) + 16))
                pe.wait_ge(*st["exped"].at(4 * h + j - 1))
                b = j // 2
                nc.tensor.matmul(PS[0:L, 4 + j % 2, :], KSC[0:SKM, layer, h, b * L:(b + 1) * L],
                                 STK[0:SKM, h % 8, j * CH:(j + 1) * CH], start=True, stop=True
                                 ).then_inc(st["st"].sem, 1)

            def values(h, par, j):
                if j == 0:
                    pe.wait_ge(*st["vs"].at(h + 1))
                    pe.wait_ge(*st["os"].at(h))
                pe.wait_ge(*st["exped"].at(4 * h + j + 1))
                nc.tensor.matmul(PS[32 * j:32 * j + VW, 6, :], VS[0:L, par, j // 2, 0, :],
                                 PT[0:L, par, j * CH:(j + 1) * CH], start=True, stop=True
                                 ).then_inc(st["pv"].sem, 1)

            def unit(u, par, on):
                for g in range(2):
                    if on(0):
                        smax(u, par, g)
                    for j in (2 * g, 2 * g + 1):
                        if on(4):
                            score(u - 4, par, j)
                        if on(5):
                            values(u - 5, 1 - par, j)
                    if g == 0 and on(2):
                        pe_mrow(pe, st, u - 2, par, u - 6)
                if on(6):
                    pe.wait_ge(*st["mrow"].at(heads_until(u - 1)))
                    pe_ot(pe, st, u - 6, par)

            pipeline(unit)

        def heads_until(n):
            return min(n, HEADS) if isinstance(n, int) else n

        def half_of(h, par):
            return (h - par) // 2

        def pipeline(unit, first=0, last=HEADS + 8):
            for u in range(first, last):
                unit(u, u % 2, lambda k, u=u: 0 <= u - k < HEADS)

        def self_lag(s, lag):
            g = s - lag
            return -(g // KT), g % KT

        def pipeline_self(eng, unit):
            for u in range(2):
                unit(u, u % 4, lambda k, u=u: 0 <= u - k < HEADS)
            with eng.Fori(0, 3) as i:
                for k in range(2, 6):
                    unit(4 * i + k, k % 4, lambda k: True)
            for u in range(14, HEADS + 3):
                unit(u, u % 4, lambda k, u=u: 0 <= u - k < HEADS)

        def score_banks(drain):
            return (4, 5, 0, 1) if drain else (4, 5, 4, 5)

        SELF_STEP = [(dict(m="max", s="score", v="values")[w[0]], int(w[1]))
                     for w in "m0 s0 m1 s1 v0 v1 v2 v3 s2 m2 s3 m3".split()]

        def pe_self(pe, st):
            def smax(h, m, i, n):
                if i == 0 and n == 0:
                    pe.wait_ge(*st[f"stack{m % 2}"].at(80 * half_of(h, m % 2) + 80))
                if n == 0:
                    pe.wait_ge(*st["maxed"].at(16 * h + i - 1))
                b = i // KT
                mm = nc.tensor.matmul(PS[:, 2 * (i % 2) + n, :], STK[0:SK, m, i * P:(i + 1) * P],
                                      STK[0:SK, m + 4, b * S + n * CH:b * S + (n + 1) * CH],
                                      start=True, stop=True)
                if n == 1:
                    mm.then_inc(st["smax"].sem, 1)

            def score(h, m, kt, j, drain, first):
                if kt == 0 and j == 0:
                    pe.wait_ge(*st[f"mdma{m % 2}"].at(16 * half_of(h, m % 2) + 16))
                banks = score_banks(drain)
                if drain and kt == 4 and j == 2:
                    join(pe, st, "maxed")
                pe.wait_ge(*st["exped"].at(32 * h + 4 * kt + j + 1 - (2 if first else len(set(banks)))))
                b = j // 2
                nc.tensor.matmul(PS[:, banks[j], :], STK[0:SKM, m + 4, b * S + kt * P:b * S + (kt + 1) * P],
                                 STK[0:SKM, m, j * CH:(j + 1) * CH], start=True, stop=True
                                 ).then_inc(st["st"].sem, 1)

            def values(h, par, kt, j):
                if kt == 0 and j == 0:
                    pe.wait_ge(*st["vs"].at(h + 1))
                    pe.wait_ge(*st["os"].at(h))
                pe.wait_ge(*st["exped"].at(32 * h + 4 * kt + j + 1))
                nc.tensor.matmul(PS[32 * j:32 * j + VW, 6, :], VS[:, par, j // 2, kt, :],
                                 PT[:, kt % 2, j * CH:(j + 1) * CH], start=(kt == 0), stop=(kt == KT - 1)
                                 ).then_inc(st["pv"].sem, 1)

            def unit(u, m, on):
                par = m % 2
                for s in range(KT):
                    if s == 2 and on(1):
                        pe_mrow(pe, st, u - 1, 1 - par, u - 2)
                    back, kt = self_lag(s, 12)
                    vback, vkt = self_lag(s, 13)
                    for what, j in SELF_STEP:
                        if what == "max" and on(0):
                            smax(u, m, 2 * s + j // 2, j % 2)
                        if what == "score" and on(back):
                            draining = isinstance(u, int) and u >= HEADS
                            score(u - back, (m - back) % 4, kt, j, draining, u is HEADS and s == 0)
                        if what == "values" and on(vback):
                            values(u - vback, (m - vback) % 2, vkt, j)
                    if s == 6 and on(2):
                        pe.wait_ge(*st["mrow"].at(heads_until(u)))
                        pe_ot(pe, st, u - 2, par)

            pipeline_self(pe, unit)

        def act_xf(act, st, c):
            s = st.slot(c)
            for ct in range(CT):
                act.wait_ge(*st["tr"].at(2 * c + ct + 1))
                act.wait_ge(*st["xl"].at(st.freed(c, ct)))
                if st.w is None:
                    i = nc.scalar.copy(XF[:, s, ct, :], PS[:, 2 * s + ct, :])
                else:
                    i = nc.scalar.activation(XF[:, s, ct, :], PS[:, 2 * s + ct, :], ACT.Identity,
                                             scale=col(st.w, ct), bias=col(st.b, ct))
                i.then_inc(st["xf"].sem, 1)

        def act_front(act, st, biases, nxt=None):
            for c in range(NC):
                for o, (name, m) in enumerate(biases):
                    k = st.qk * c + o
                    act.wait_ge(*st["mm"].at(st.nout * c + o + 1))
                    act.wait_ge(*st[f"stored{k % 4}"].at(16 * (k // 4)))
                    nc.scalar.activation(QP[:, k % 4, 0, :], PS[:, 4 + (st.nout * c + o) % 4, :], ACT.Identity,
                                         bias=col(name, m)).then_inc(st["part1"].sem, 1)
                    if o == st.nout // 2 - 1 and c < NC - 2:
                        act_xf(act, st, c + 2)
                if not biases:
                    if c < NC - 2:
                        act_xf(act, st, c + 2)
                    elif nxt and (nxt.two or c == NC - 2):
                        act_xf(act, nxt, c - NC + 2)

        def act_mlp(act, st, b1, nxt=None):
            def chunk(c, last):
                for h in range(HB):
                    act.wait_ge(*st["m1"].at(8 * c + h + 1))
                    act.wait_ge(*st["gl"].at(8 * c + h - 1))
                    nc.scalar.activation(GF[:, h % 2, :], PS[:, 2 + h % 2, :], ACT.Gelu, bias=col(b1, h)
                                         ).then_inc(st["gelu"].sem, 1)
                if not last:
                    act_xf(act, st, c + 1)
                elif nxt:
                    act_xf(act, nxt, 0)
            for c in range(NC):
                chunk(c, c == NC - 1)
            if nxt:
                act_xf(act, nxt, 1)

        def out_view(h):
            return OU[:, :, h, :].rearrange("p (j i) w -> p j i w", i=TPC)

        BACK = PS[:, 7, :].rearrange("p (i j w) -> p j i w", i=TPC, j=4)[:, :, :, 0:OW]

        def act_cross(act, st, split, loaded):
            def unit(u, par, on):
                if u >= 8 and u < 16:
                    if u == 8:
                        act.wait_ge(*loaded)
                    nc.scalar.copy(WH[:, u, :], RAW2[:, u - 8, :]).then_inc(split["w_high"].sem, 1)
                if on(7):
                    act.wait_ge(*st["otr"].at(u - 6))
                    nc.scalar.copy(out_view(u - 7), BACK).then_inc(st["ou"].sem, 1)
                if on(4):
                    h = u - 4
                    for j in range(4):
                        act.wait_ge(*st["st"].at(4 * h + j + 1))
                        act.wait_ge(*st["pv"].at(4 * h + j - 7))
                        nc.scalar.activation(PT[0:L, par, j * CH:(j + 1) * CH], PS[0:L, 4 + j % 2, :], ACT.Exp,
                                             scale=SCALE).then_inc(st["exped"].sem, 1)
            pipeline(unit)

        def act_self(act, st):
            def unit(u, m, on):
                par = m % 2
                for s in range(KT):
                    if s == 5 and on(2):
                        act.wait_ge(*st["pv"].at(32 * (u - 2) + 32))
                        act.wait_ge(*st["otr"].at(u - 3))
                        nc.scalar.copy(OS[:, par, :], PS[:, 6, :]).then_inc(st["os"].sem, 1)
                    if s == 7 and on(2):
                        act.wait_ge(*st["otr"].at(u - 1))
                        nc.scalar.copy(out_view(u - 2), BACK).then_inc(st["ou"].sem, 1)
                    back, kt = self_lag(s, 12)
                    if on(back):
                        g = KT * (u - back) + kt
                        for j in range(4):
                            act.wait_ge(*st["st"].at(4 * g + j + 1))
                            act.wait_ge(*st["pv"].at(4 * g + j - 7))
                            nc.scalar.activation(PT[:, kt % 2, j * CH:(j + 1) * CH],
                                                 PS[:, score_banks(isinstance(u, int) and u >= HEADS)[j], :], ACT.Exp,
                                                 scale=SCALE).then_inc(st["exped"].sem, 1)
            pipeline_self(act, unit)

        def dve_stats(dve, st, c):
            s0 = 4 * c
            if st is A0:
                dve.wait_ge(ld[f"x{c}"], 16)
            else:
                dve.wait_ge(*st.prev["ev"].at(4 * c + 4))
            for t in range(TPC):
                nc.vector.bn_stats(bst[:, s0 + t, :], X[:, 4 * c + t, :]).then_inc(st["bn"].sem, 1)
            for t in range(TPC):
                dve.wait_ge(*st["bn"].at(4 * c + t + 1))
                dve.sem_inc(s_passed, 1)
                nc.vector.bn_aggr(mv[:, s0 + t, :], bst[:, s0 + t, :]).then_inc(st["bn2"].sem, 1)

        def dve_norm(dve, st, c):
            a = st.slot(c)
            dve.wait_ge(*st["tr"].at(2 * c - 2 if st.two and c > 0 else 2 * c))
            if st.w is not None:
                dve.wait_ge(*st["rs"].at(c + 1))
                for t in range(TPC):
                    nc.vector.tensor_scalar(XN[:, a, t, :], X[:, 4 * c + t, :], mv[:, 4 * c + t, 0:1],
                                            rstd[:, 4 * c + t:4 * c + t + 1], ALU.subtract, ALU.mult
                                            ).then_inc(st["xn"].sem, 1)
            else:
                nc.vector.reciprocal(rsum[:, a, :].rearrange("p (t h) -> p t h", t=TPC),
                                     OU[:, 4 * c:4 * c + 4, :, HD]).then_inc(st["bn"].sem, 4)
                dve.wait_ge(*st["bn"].at(4 * c + 4))
                for t in range(TPC):
                    nc.vector.tensor_tensor(
                        XN[:, a, t, :].rearrange("p (h d) -> p h d", h=HEADS), OU[:, 4 * c + t, :, 0:HD],
                        rsum[:, a, t * HEADS:(t + 1) * HEADS].rearrange("p (h o) -> p h o", o=1)
                        .to_broadcast([P, HEADS, HD]), ALU.mult).then_inc(st["xn"].sem, 1)

        def dve_xl(dve, st, c):
            s = st.slot(c)
            for ct in range(CT):
                dve.wait_ge(*st["xh"].at(2 * c + ct + 1))
                nc.vector.tensor_tensor(XTL[:, s, ct, :], XF[:, s, ct, :], XTH[:, s, ct, :].bitcast(F32),
                                        ALU.subtract).then_inc(st["xl"].sem, 1)

        def stats_ahead(st, nxt, c):
            if c == NC - 2:
                return (0, 1) if nxt.two else (0,)
            return (2,) if nxt.two else ()

        def dve_front(dve, st, biases, tok, nxt=None, after={}):
            for c in range(NC):
                if c < NC - 2:
                    dve_norm(dve, st, c + 2)
                elif nxt and (nxt.two or c == NC - 2):
                    for k in stats_ahead(st, nxt, c):
                        dve_stats(dve, nxt, k)
                    dve_norm(dve, nxt, c - 2)
                if c < NC - 1:
                    dve_xl(dve, st, c + 1)
                elif nxt:
                    dve_xl(dve, nxt, 0)
                if c == 0 and st.w:
                    dve_stats(dve, st, 3)
                for o, (name, m) in enumerate(biases):
                    k = st.qk * c + o
                    dve.wait_ge(*st["part1"].at(k + 1))
                    dve.wait_ge(*st["part3"].at(k - 1))
                    nc.vector.scalar_tensor_tensor(RES[:, k % 2, :], PS[:, 4 + (st.nout * c + o) % 4, :],
                                                   col(name, m), QP[:, k % 4, 0, :],
                                                   ALU.add, ALU.subtract).then_inc(st["ev"].sem, 1)
                for t in range(TPC if tok else 0):
                    k = st.nout * c + st.qk + t
                    dve.wait_ge(*st["mm"].at(k + 1))
                    ps = PS[:, 4 + k % 4, 0:D]
                    if tok == "v":
                        nc.vector.tensor_tensor(V[:, 4 * c + t, :], ps, row("sa_bv"), ALU.add
                                                ).then_inc(st["ev"].sem, 1)
                    else:
                        dve.wait_ge(*st["xb"].at(4 * c + t + 1))
                        nc.vector.tensor_tensor(X[:, 4 * c + t, :], ps, X[:, 4 * c + t, :], ALU.add
                                                ).then_inc(st["ev"].sem, 1)
                if c in after:
                    after[c]()

        def dve_mlp(dve, st, nxt=None):
            def chunk(c, last):
                for h in range(HB):
                    dve.wait_ge(*st["gh"].at(8 * c + h + 1))
                    nc.vector.tensor_tensor(XTL[:, 1, h % 2, :], GF[:, h % 2, :], XTH[:, 1, h % 2, :].bitcast(F32),
                                            ALU.subtract).then_inc(st["gl"].sem, 1)
                    if h == 2 and not last:
                        dve_stats(dve, st, c + 1)
                    if h == 5 and not last:
                        dve_norm(dve, st, c + 1)
                    if last and nxt and h in (1, 2, 3):
                        dve_stats(dve, nxt, h - 1)
                    if last and nxt and h in (5, 6):
                        dve_norm(dve, nxt, h - 5)
                if not last:
                    dve_xl(dve, st, c + 1)
                elif nxt:
                    dve_xl(dve, nxt, 0)
                for t in range(TPC):
                    dve.wait_ge(*st["acc"].at(4 * c + t + 1))
                    dve.wait_ge(*st["xb"].at(4 * c + t + 1))
                    nc.vector.tensor_tensor(X[:, 4 * c + t, :], PS[:, 4 + t, 0:D], X[:, 4 * c + t, :], ALU.add
                                            ).then_inc(st["ev"].sem, 1)
            join(dve, st.prev, "ev")
            for c in range(NC):
                chunk(c, c == NC - 1)

        def dve_mrow(dve, st, h, par):
            dve.wait_ge(*st["mtr"].at(h + 1))
            dve.wait_ge(*st[f"mdma{par}"].at(16 * half_of(h, par)))
            nc.vector.tensor_copy(nrow[:, par, :], PS[0:3 * NT, 7, 0:P // 2].bitcast(BF16)
                                  ).then_inc(st["mrow"].sem, 1)

        def dve_cross(dve, st):
            def unit(u, par, on):
                if on(6):
                    dve.wait_ge(*st["pv"].at(4 * (u - 5)))
                    dve.wait_ge(*st["otr"].at(u - 7))
                    nc.vector.tensor_copy(OS[:, par, :], PS[:, 6, :]).then_inc(st["os"].sem, 1)
                for g in range(2):
                    if on(0):
                        dve.wait_ge(*st["smax"].at(2 * u + g + 1))
                        if g == 0:
                            dve.wait_ge(*st["msplit"].at(5 * (u - 1)))
                        nc.vector.tensor_reduce(
                            nmax[:, par, 8 * g:8 * g + 8],
                            PS[:, 2 * g:2 * g + 2, :].rearrange("p k (i n) -> p (k i) n", i=4)[:, :, 0:L],
                            AX.X, ALU.max, negate=True).then_inc(st["maxed"].sem, 1)
                    if g == 0 and on(2):
                        dve_mrow(dve, st, u - 2, par)
            pipeline(unit)

        def dve_self(dve, st):
            def unit(u, m, on):
                par = m % 2
                for s in range(KT):
                    if s == 2 and on(1):
                        dve_mrow(dve, st, u - 1, 1 - par)
                    if on(0):
                        for i in (2 * s, 2 * s + 1):
                            dve.wait_ge(*st["smax"].at(16 * u + i + 1))
                            if i == 0:
                                dve.wait_ge(*st["msplit"].at(5 * (u - 1)))
                            nc.vector.tensor_reduce(nmax[:, par, i:i + 1], PS[:, 2 * (i % 2):2 * (i % 2) + 2, :],
                                                    AX.XY, ALU.max, negate=True).then_inc(st["maxed"].sem, 1)
            pipeline_self(dve, unit)

        def pool_copy(out, in_):
            return nc.gpsimd.tensor_scalar(out, in_, 1.0, 0.0, ALU.mult, ALU.add)

        def pool_rstd(pool, st, c):
            at = slice(4 * c, 4 * c + 4)
            pool.wait_ge(*st["bn2"].at(4 * c + 4))
            pool.sem_inc(s_passed, 1)
            nc.gpsimd.tensor_scalar(var_eps[:, at], mv[:, at, 1], EPS, 1.0, ALU.add, ALU.mult
                                    ).then_inc(st["var"].sem, 1)
            pool.wait_ge(*st["var"].at(c + 1))
            pool.sem_inc(s_passed, 1)
            nc.gpsimd.tensor_tensor(rstd[:, at], var_eps[:, at], half[:, at], ALU.pow).then_inc(st["rs"].sem, 1)

        def pool_xh(pool, st, c):
            s = st.slot(c)
            for ct in range(CT):
                pool.wait_ge(*st["xf"].at(2 * c + ct + 1))
                pool.sem_inc(s_passed, 1)
                if not st.two:
                    if isinstance(c, int) and c == 0:
                        pool.wait_ge(*st.prev["mm"].at(12))
                        pool.sem_inc(s_passed, 1)
                    else:
                        pool.wait_ge(*st["m1"].at(8 * c))
                        pool.sem_inc(s_passed, 1)
                elif c == 0 and st is A1:
                    pool.wait_ge(*st.prev["m1"].at(32))
                    pool.sem_inc(s_passed, 1)
                elif c == 1 and st is A1:
                    pool.wait_ge(*st.prev["acc"].at(NT))
                    pool.sem_inc(s_passed, 1)
                elif c == 0 and st.prev:
                    pool.wait_ge(*st.prev["mm"].at(12))
                    pool.sem_inc(s_passed, 1)
                elif c > 0:
                    pool.wait_ge(*st["mm"].at(st.nout * (c - 1)))
                    pool.sem_inc(s_passed, 1)
                pool_copy(XTH[:, s, ct, :], XF[:, s, ct, :]).then_inc(st["xh"].sem, 1)

        def pool_front(pool, st, nxt=None):
            for c in range(NC):
                if c >= NC - 2 and nxt:
                    for k in stats_ahead(st, nxt, c):
                        pool_rstd(pool, nxt, k)
                if c < NC - 1:
                    pool_xh(pool, st, c + 1)
                if c == 0 and st.w:
                    pool_rstd(pool, st, 3)
                if c == NC - 1 and nxt:
                    pool_xh(pool, nxt, 0)
                for o in range(st.qk):
                    k = st.qk * c + o
                    pool.wait_ge(*st["ev"].at(st.nout * c + o + 1))
                    pool.sem_inc(s_passed, 1)
                    pool_copy(QP[:, k % 4, 1, :], RES[:, k % 2, :]).then_inc(st["part2"].sem, 1)
                    pool.wait_ge(*st["part2"].at(k + 1))
                    pool.sem_inc(s_passed, 1)
                    nc.gpsimd.tensor_tensor(QP[:, k % 4, 2, :], RES[:, k % 2, :], QP[:, k % 4, 1, :],
                                            ALU.subtract).then_inc(st["part3"].sem, 1)

        def pool_mlp(pool, st, b2, nxt=None):
            def chunk(c, last):
                for h in range(HB):
                    pool.wait_ge(*st["gelu"].at(8 * c + h + 1))
                    pool.sem_inc(s_passed, 1)
                    if h < 2:
                        pool.wait_ge(*st["acc"].at(4 * c))
                        pool.sem_inc(s_passed, 1)
                    else:
                        pool.wait_ge(*st["m2"].at(7 * c + h - 1))
                        pool.sem_inc(s_passed, 1)
                    pool_copy(XTH[:, 1, h % 2, :], GF[:, h % 2, :]).then_inc(st["gh"].sem, 1)
                    if 1 <= h <= TPC:
                        if h == 1:
                            pool.wait_ge(*st["xn"].at(4 * c + 4))
                            pool.sem_inc(s_passed, 1)
                        nc.gpsimd.tensor_tensor(X[:, 4 * c + h - 1, :], X[:, 4 * c + h - 1, :], row(b2), ALU.add
                                                ).then_inc(st["xb"].sem, 1)
                    if h == 3 and not last:
                        pool_rstd(pool, st, c + 1)
                    if last and nxt and h in (3, 4, 5):
                        pool_rstd(pool, nxt, h - 3)
                if not last:
                    pool_xh(pool, st, c + 1)
                elif nxt:
                    pool_xh(pool, nxt, 0)
            pool.wait_ge(*st.prev["mm"].at(NT))
            pool.sem_inc(s_passed, 1)
            for c in range(NC):
                chunk(c, c == NC - 1)

        def pool_msplit(pool, st, h, par, ngroups):
            pool.wait_ge(*st["maxed"].at(ngroups * (h + 1)))
            pool.sem_inc(s_passed, 1)
            pool.wait_ge(*st["mtr"].at(h - 1))
            pool.sem_inc(s_passed, 1)
            src = nmax
            for k in range(3):
                part = nparts[:, par, NT * k:NT * (k + 1)]
                pool_copy(part, src[:, par, :]).then_inc(st["msplit"].sem, 1)
                pool.wait_ge(*st["msplit"].at(5 * h + 2 * k + 1))
                pool.sem_inc(s_passed, 1)
                if k < 2:
                    nc.gpsimd.tensor_tensor(nres[:, par, :], src[:, par, :], part, ALU.subtract
                                            ).then_inc(st["msplit"].sem, 1)
                    pool.wait_ge(*st["msplit"].at(5 * h + 2 * k + 2))
                    pool.sem_inc(s_passed, 1)
                    src = nres

        def pool_bias(st, bias, tiles):
            for t in tiles:
                nc.gpsimd.tensor_tensor(X[:, t, :], X[:, t, :], row(bias), ALU.add).then_inc(st["xb"].sem, 1)

        def pool_cross(pool, st, layer, split, high_before, Pj, bias):
            def unit(u, par, on):
                if on(4):
                    h = u - 4
                    pool.wait_ge(*st["pv"].at(4 * (h - 1)))
                    pool.sem_inc(s_passed, 1)
                    nc.gpsimd.tensor_copy(VS[0:L, par, :, 0, 0:HD], VC[:, layer, :, bass.ds(h * HD, HD)]
                                          ).then_inc(st["vs"].sem, 1)
                if on(0):
                    pool_msplit(pool, st, u, par, 2)
                if u >= 8 and u < 16:
                    pool.wait_ge(*split["w_high"].at(high_before + u - 7))
                    pool.sem_inc(s_passed, 1)
                    nc.gpsimd.tensor_tensor(WL[:, u, :], RAW2[:, u - 8, :], WH[:, u, :].bitcast(F32), ALU.subtract
                                            ).then_inc(split["low_pool"].sem, 1)
                if HEADS <= u < HEADS + 4:
                    pool_bias(Pj, bias, range(4 * (u - HEADS), 4 * (u - HEADS) + 4))
            pipeline(unit)

        def pool_self(pool, st):
            Vv = V[:, :, :].rearrange("p (b k) c -> p b k c", b=B)

            def unit(u, m, on):
                par = m % 2
                if on(1):
                    h = u - 1
                    pool.wait_ge(*st["pv"].at(32 * (h - 1)))
                    pool.sem_inc(s_passed, 1)
                    nc.gpsimd.tensor_copy(VS[:, 1 - par, :, :, 0:HD], Vv[:, :, :, bass.ds(h * HD, HD)]
                                          ).then_inc(st["vs"].sem, 1)
                if on(0):
                    pool_msplit(pool, st, u, par, NT)
            pipeline_self(pool, unit)

        def sp_store_parts(sp, st, dests, ks):
            for k in ks:
                c = k // st.qk
                dst, m = dests[k % st.qk]
                sp.wait_ge(*st["part3"].at(k + 1))
                sp.dma_start(dst[m * P:(m + 1) * P, :, c * CH:(c + 1) * CH], QP[:, k % 4, :, :]
                             ).then_inc(st[f"stored{k % 4}"].sem, 16)

        def load_q(sp, st, h, par, slot, src):
            parts = src[bass.ds(h * HD, HD), :, :].rearrange("(g d) t n -> g (d t) n", g=1)
            sp.dma_start(STK[0:96, slot, :], parts.to_broadcast([2, 48, T])).then_inc(st[f"stack{par}"].sem, 16)
            sp.dma_start(STK[96:SK, slot, :], src[bass.ds(h * HD, HD), 0, :]).then_inc(st[f"stack{par}"].sem, 16)

        def load_k(sp, st, h, par, slot, src):
            for g in range(2):
                sp.dma_start(STK[48 * g:48 * g + 48, slot, :], src[bass.ds(h * HD, HD), g:g + 1, :]
                             .to_broadcast([HD, 3, T])).then_inc(st[f"stack{par}"].sem, 16)
            sp.dma_start(STK[96:SK, slot, :], src[bass.ds(h * HD, HD), 2, :]).then_inc(st[f"stack{par}"].sem, 16)

        def store_mrow(sp, st, h, par, slot):
            sp.wait_ge(*st["mrow"].at(h + 1))
            sp.dma_start(STK[SK:SKM, slot, :],
                         nrow[:, par, :]
                         ).then_inc(st[f"mdma{par}"].sem, 16)

        def sp_cross(sp, st, src, A, stores, load_weights):
            def load(h, par):
                sp.wait_ge(*st["st"].at(4 * (h - 7)))
                sp.wait_ge(*st[f"stack{par}"].at(32 * half_of(h, par)))
                load_q(sp, st, h, par, h % 8, src)

            def unit(u, par, on):
                if on(2):
                    store_mrow(sp, st, u - 2, par, (u - 2) % 8)
                if 2 <= u < 6:
                    load_weights(u - 2)
                if u == 4:
                    join(sp, A, "stored1 stored3")
                if on(-4):
                    load(u + 4, par)
            load(0, 0)
            stores()
            for h in range(1, 4):
                load(h, h % 2)
            pipeline(unit, last=HEADS + 2)

        def sp_self(sp, st, stores):
            def load(h, m):
                par = m % 2
                sp.wait_ge(*st["st"].at(32 * (h - 3)))
                sp.wait_ge(*st[f"stack{par}"].at(80 * half_of(h, par)))
                load_q(sp, st, h, par, m, q_parts[1])
                load_k(sp, st, h, par, m + 4, k_parts)

            def unit(u, m, on):
                if on(1):
                    store_mrow(sp, st, u - 1, (m + 1) % 2, (m - 1) % 4)
                if on(-2):
                    load(u + 2, (m + 2) % 4)
            load(0, 0)
            stores()
            load(1, 1)
            join(sp, A1, "stored2 stored3")
            pipeline_self(sp, unit)

        block = es.enter_context(nc.Block())
        qk0 = [("zero", 0), ("zero", 1)]
        qk1 = [("sa_bq", 0), ("sa_bk", 0), ("sa_bq", 1), ("sa_bk", 1)]
        qk2 = [("ca_bq", 0), ("ca_bq", 1)]

        @block.sync
        def _(sp):
            for counting in sems.values():
                sp.sem_inc(counting, CREDIT)
            def load_x(c):
                b, h = c // 2, c % 2
                sp.dma_start(X[:, 4 * c:4 * c + 4, :], x_d[b, h * CH:(h + 1) * CH, :].rearrange("(t p) c -> p t c", p=P)
                             ).then_inc(ld[f"x{c}"], 16)
            sp.dma_start(colv[:], cols_d).then_inc(ld["cols"], 16)
            sp.dma_start(CX[:], ctx_d.rearrange("b t c -> t b c")).then_inc(ld["ctx"], 16)
            load_x(0)
            sp.dma_start(RAW[:, 0:2, :], w_d[:, 0:2, :]).then_inc(ld["wq"], 16)
            load_x(1)
            sp.dma_start(WCA[:, 0, :], wkv_d[0:P, :]).then_inc(ld["wc"], 16)
            sp.dma_start(WCB[:, 0, :], wkv_d[P:CTX, :]).then_inc(ld["wc"], 16)
            for i, w in enumerate((wck_d, wcv_d)):
                sp.dma_start(WCA[:, 1, i * D:(i + 1) * D], w[0:P, :]).then_inc(ld["wc"], 16)
                sp.dma_start(WCB[:, 1, i * D:(i + 1) * D], w[P:CTX, :]).then_inc(ld["wc"], 16)
            load_x(2)
            load_x(3)
            sp.dma_start(rowv[:], rows_d.rearrange("(o r) c -> o r c", o=1).to_broadcast([P, len(ROWS), D])
                         ).then_inc(ld["rows"], 16)
            sp.dma_start(RAW[:, 2:8, :], w_d[:, 2:8, :]).then_inc(ld["w"], 16)
            q_dests = [(q_parts[0], 0), (q_parts[0], 1)]
            sp_store_parts(sp, A0, q_dests, range(2))
            def store_context(layer):
                for i in (2 * layer, 2 * layer + 1):
                    sp.wait_ge(*cx["c_p3"].at(i + 1))
                    sp.dma_start(kc_parts[layer][(i % 2) * P:(i % 2 + 1) * P, :, :],
                                 KP[:, i, :, :]).then_inc(cx["c_store"].sem, 16)
                sp.wait_ge(*cx["c_store"].at(32 * layer + 32))
            def stack_context(layer):
                for g in range(GROUPS):
                    rows = slice(48 * (g // 3) + g % 3, 48 * (g // 3) + 48, 3) if g < 6 else slice(96, SK)
                    sp.dma_start(KSC[rows, layer, :, :],
                                 kc_parts[layer][:, g // 3, :].rearrange("(h d) n -> d h n", d=HD)
                                 ).then_inc(cx["c_stack"].sem, 16)
            sp_store_parts(sp, A0, q_dests, range(2, 4))
            store_context(0)
            sp.wait_ge(s_ones, 1)
            stack_context(0)
            store_context(1)
            sp_store_parts(sp, A0, q_dests, range(4, 7))
            join(sp, A0, "stored0 stored2")
            join(sp, split0, "low_dve")
            sp.wait_ge(*split0["low_pool"].at(3))
            join(sp, cx, "c_mm")
            sp_cross(sp, C0, q_parts[0], A0, lambda: sp_store_parts(sp, A0, q_dests, range(7, 8)),
                     lambda k: sp.dma_start(RAW2[:, 2 * k:2 * k + 2, :], w_d[:, 8 + 2 * k:10 + 2 * k, :]
                                            ).then_inc(ld["mlp0"], 16))
            stack_context(1)
            join(sp, C0, "st")
            ones = KSC[SK:SKM, :, :, :].rearrange("p l h n -> p (l h n)")[:, 0:2 * T].rearrange("p (s n) -> p s n", s=2)
            for k in range(2):
                sp.dma_start(STK[SK:SKM, 4 + 2 * k:6 + 2 * k, :], ones).then_inc(ones_set["ones_rows"].sem, 16)
            qk_dests = [(q_parts[1], 0), (k_parts, 0), (q_parts[1], 1), (k_parts, 1)]
            sp_store_parts(sp, A1, qk_dests, range(14))
            join(sp, A1, "stored0 stored1")
            join(sp, C0, "smax st")
            join(sp, ones_set, "ones_rows")
            sp_self(sp, C1, lambda: sp_store_parts(sp, A1, qk_dests, range(14, 16)))
            join(sp, C1, "vs")
            sp.dma_start(RAW2, wm_d).then_inc(ld["mlp1"], 16)
            qc_dests = [(q_parts[2], 0), (q_parts[2], 1)]
            sp_store_parts(sp, A2, qc_dests, range(7))
            join(sp, A2, "stored0 stored2")
            join(sp, C1, "st")
            sp_cross(sp, C2, q_parts[2], A2, lambda: sp_store_parts(sp, A2, qc_dests, range(7, 8)),
                     lambda k: None)
            for c in range(NC):
                sp.wait_ge(*M1["ev"].at(4 * c + 4))
                b, h = c // 2, c % 2
                sp.dma_start(out_d[b, h * CH:(h + 1) * CH, :].rearrange("(t p) c -> p t c", p=P),
                             X[:, 4 * c:4 * c + 4, :]).then_inc(s_out, 16)
            sp.wait_ge(s_out, 16 * NC)

        @block.tensor
        def _(pe):
            pe.wait_ge(s_const, 3)
            pe.wait_ge(ld["ctx"], 16)
            for layer in (1, 0):
                src = CX if layer else CN
                if layer == 0:
                    pe.wait_ge(*cx["c_n"].at(2))
                for k, (c0, cn) in enumerate(((0, P), (P, CTX - P))):
                    for b in range(B):
                        last = nc.tensor.transpose(PS[0:cn, 4 + 2 * layer + k, b * L:(b + 1) * L],
                                                   src[:, b, c0:c0 + cn], identf[0:L, 0:L])
                    last.then_inc(cx["c_tr"].sem, 1)
            pe_transposes(pe, A0, 0)
            pe.wait_ge(ld["wc"], 96)
            pe.wait_ge(*cx["c_yt"].at(4))
            for i in range(4):
                layer, m = i // 2, i % 2
                nc.tensor.matmul(PS[:, 4 + i, 0:B * L], WCA[:, layer, m * P:(m + 1) * P], YT[:, 2 * layer, :],
                                 start=True, stop=False)
                nc.tensor.matmul(PS[:, 4 + i, 0:B * L], WCB[:, layer, m * P:(m + 1) * P],
                                 YT[0:CTX - P, 2 * layer + 1, :], start=False, stop=True
                                 ).then_inc(cx["c_mm"].sem, 1)
            pe_transposes(pe, A0, 1)
            for i in range(4):
                layer, b = i // 2, i % 2
                pe.wait_ge(*cx["c_r"].at(i + 1))
                nc.tensor.matmul(PS[0:L, 4 + i, 0:D], YT[:, 2 * layer, b * L:(b + 1) * L], WCA[:, layer, D:2 * D],
                                 start=True, stop=False)
                nc.tensor.matmul(PS[0:L, 4 + i, 0:D], YT[0:CTX - P, 2 * layer + 1, b * L:(b + 1) * L],
                                 WCB[:, layer, D:2 * D], start=False, stop=True).then_inc(cx["c_mm"].sem, 1)
            join(pe, cx, "c_v")
            pe.wait_ge(*split0["low_dve"].at(2))
            pe_front(pe, A0, [(WB_Q0, 0), (WB_Q0, 1)], [])
            join(pe, A0, "xf ev")
            pe.wait_ge(*cx["c_stack"].at(16 * GROUPS))
            pe.wait_ge(s_const2, 2)
            pe.wait_ge(s_ones, 2)

            def project(C, Pj, blk, nxt):
                join(pe, C, "maxed exped os ou")
                pe_transposes(pe, Pj, 0)
                pe_transposes(pe, Pj, 1)
                pe_front(pe, Pj, [], [blk], nxt)

            pe_cross(pe, C0, 0)
            join(pe, split0, "low_dve")
            pe.wait_ge(*split0["low_pool"].at(3))
            project(C0, P0, WB_P0, M0)
            join(pe, split0, "low_pool")
            pe_mlp(pe, M0, A1)
            pe_front(pe, A1, [(WB_SQ, 0), (WB_SK, 0), (WB_SQ, 1), (WB_SK, 1)], [WB_SV])
            join(pe, A1, "xf ev")
            pe_self(pe, C1)
            project(C1, P1, WB_SO, A2)
            pe_front(pe, A2, [(WB_CQ, 0), (WB_CQ, 1)], [])
            join(pe, A2, "xf ev")
            join(pe, cx, "c_stack")
            pe_cross(pe, C2, 1)
            project(C2, P2, WB_CO, M1)
            join(pe, split1, "low_pool")
            pe_mlp(pe, M1)

        @block.scalar
        def _(act):
            act.wait_ge(ld["cols"], 16)

            def high(blk):
                nc.scalar.copy(WH[:, blk, :], RAW[:, blk, :]).then_inc(split0["w_high"].sem, 1)
            for layer in (1, 0):
                for k, cn in enumerate((P, CTX - P)):
                    i = 2 * layer + k
                    act.wait_ge(*cx["c_tr"].at((3 if layer == 0 else 1) + k))
                    if layer:
                        y = nc.scalar.copy(YT[0:cn, i, :], PS[0:cn, 4 + i, 0:B * L])
                    else:
                        y = nc.scalar.activation(YT[0:cn, i, :], PS[0:cn, 4 + i, 0:B * L], ACT.Identity,
                                                 scale=col("l0_ln2_w", k)[0:cn], bias=col("l0_ln2_b", k)[0:cn])
                    y.then_inc(cx["c_yt"].sem, 1)
            act.wait_ge(ld["wq"], 16)
            high(0)
            high(1)
            act_xf(act, A0, 0)
            for i in range(4):
                act.wait_ge(*cx["c_mm"].at(i + 1))
                nc.scalar.activation(KP[:, i, 0, :], PS[:, 4 + i, 0:B * L], ACT.Identity,
                                     bias=col("ca_bk" if i > 1 else "zero", i % 2)).then_inc(cx["c_p1"].sem, 1)
            act_xf(act, A0, 1)
            act_front(act, A0, qk0)
            act.wait_ge(ld["w"], 16)
            for blk in range(2, 8):
                high(blk)
            join(act, A0, "xl part3 stored0 stored1 stored2 stored3")
            join(act, cx, "c_store")

            def project(C, Pj, nxt):
                join(act, C, "pv otr")
                act_xf(act, Pj, 0)
                act_xf(act, Pj, 1)
                act_front(act, Pj, [], nxt)

            act_cross(act, C0, split0, (ld["mlp0"], 64))
            project(C0, P0, M0)
            act_mlp(act, M0, "l0_b1", A1)
            act_front(act, A1, qk1)
            join(act, A1, "xl part3 stored0 stored1 stored2 stored3")
            join(act, P0, "xn")
            act_self(act, C1)
            project(C1, P1, A2)
            act_front(act, A2, qk2)
            join(act, A2, "xl part3 stored0 stored1 stored2 stored3")
            join(act, P1, "xn")
            join(act, M0, "acc")
            act_cross(act, C2, split1, (ld["mlp1"], 16))
            project(C2, P2, M1)
            act_mlp(act, M1, "l1_b1")

        @block.vector
        def _(dve):
            nc.vector.memset(KSC[96:P, :, :, :], 1.0).then_inc(s_ones, 1)
            dve.wait_ge(ld["ctx"], 16)
            for b in range(B):
                nc.vector.bn_stats(bst[0:L, b, :], CX[:, b, :]).then_inc(cx["c_bn"].sem, 1)
            for b in range(B):
                dve.wait_ge(*cx["c_bn"].at(b + 1))
                nc.vector.bn_aggr(mv[0:L, b, :], bst[0:L, b, :]).then_inc(cx["c_bn2"].sem, 1)
            dve.wait_ge(*cx["c_rs"].at(1))
            for b in range(B):
                nc.vector.tensor_scalar(CN[:, b, :], CX[:, b, :], mv[0:L, b, 0:1], rstd[0:L, b:b + 1],
                                        ALU.subtract, ALU.mult).then_inc(cx["c_n"].sem, 1)

            dve.wait_ge(s_const, 4)
            nc.vector.tensor_copy(identb[:], identf[:]).then_inc(s_ones, 1)

            def low(blk):
                dve.wait_ge(*split0["w_high"].at(blk + 1))
                nc.vector.tensor_tensor(WL[:, blk, :], RAW[:, blk, :], WH[:, blk, :].bitcast(F32), ALU.subtract
                                        ).then_inc(split0["low_dve"].sem, 1)

            dve_stats(dve, A0, 0)
            dve_norm(dve, A0, 0)
            dve_stats(dve, A0, 1)
            dve_norm(dve, A0, 1)
            dve_stats(dve, A0, 2)
            low(0)
            low(1)
            dve.wait_ge(ld["cols"], 16)
            for i in range(4):
                dve.wait_ge(*cx["c_p1"].at(i + 1))
                nc.vector.scalar_tensor_tensor(KR[:, i, :], PS[:, 4 + i, 0:B * L],
                                               col("ca_bk" if i > 1 else "zero", i % 2), KP[:, i, 0, :],
                                               ALU.add, ALU.subtract).then_inc(cx["c_r"].sem, 1)
            dve_xl(dve, A0, 0)
            dve.wait_ge(ld["rows"], 16)
            for i in range(4):
                dve.wait_ge(*cx["c_mm"].at(5 + i))
                if i < 2:
                    v = nc.vector.tensor_copy(VC[:, 0, i, :], PS[0:L, 4 + i, 0:D])
                else:
                    v = nc.vector.tensor_tensor(VC[:, 1, i - 2, :], PS[0:L, 4 + i, 0:D], row("ca_bv")[0:L], ALU.add)
                v.then_inc(cx["c_v"].sem, 1)

            def context_parts():
                for i in range(4):
                    dve.wait_ge(*cx["c_r"].at(i + 1))
                    nc.vector.tensor_copy(KP[:, i, 1, :], KR[:, i, :]).then_inc(cx["c_p2"].sem, 1)
                for i in range(4):
                    dve.wait_ge(*cx["c_p2"].at(i + 1))
                    nc.vector.tensor_tensor(KP[:, i, 2, :], KR[:, i, :], KP[:, i, 1, :], ALU.subtract
                                            ).then_inc(cx["c_p3"].sem, 1)
            dve_front(dve, A0, qk0, None, None, {0: context_parts})
            for blk in range(2, 5):
                low(blk)
            join(dve, A0, "xh part3 stored0 stored1 stored2 stored3")

            def project(C, Pj, nxt):
                join(dve, C, "ou")
                for c in range(2):
                    dve_norm(dve, Pj, c)
                dve_xl(dve, Pj, 0)
                dve_front(dve, Pj, [], "x", nxt)

            dve_cross(dve, C0)
            project(C0, P0, M0)
            dve_mlp(dve, M0, A1)
            join(dve, split0, "low_pool")
            dve_front(dve, A1, qk1, "v")
            dve_self(dve, C1)
            project(C1, P1, A2)
            dve_front(dve, A2, qk2, None)
            join(dve, A2, "part3 stored0 stored1 stored2 stored3")
            dve_cross(dve, C2)
            project(C2, P2, M1)
            dve_mlp(dve, M1)

        @block.gpsimd
        def _(pool):
            nc.gpsimd.memset(identf[:], 0.0).then_inc(s_const, 1)
            nc.gpsimd.memset(half[:], -0.5).then_inc(s_const, 1)
            pool.wait_ge(s_const, 1)
            nc.gpsimd.affine_select(out=identf[:], in_=identf[:], compare_op=ALU.not_equal, fill=1.0, base=0,
                                    pattern=[[-1, P]], channel_multiplier=1).then_inc(s_const, 2)
            nc.gpsimd.memset(VS[:], 0.0).then_inc(s_const2, 1)
            pool.wait_ge(s_const2, 1)
            nc.gpsimd.memset(VS[:, :, :, :, HD:HD + 1], 1.0).then_inc(s_const2, 1)
            pool.wait_ge(*cx["c_bn2"].at(2))
            nc.gpsimd.tensor_scalar(var_eps[0:L, 0:2], mv[0:L, 0:2, 1], EPS, 1.0, ALU.add, ALU.mult
                                    ).then_inc(cx["c_var"].sem, 1)
            join(pool, cx, "c_var")
            pool.wait_ge(s_const, 4)
            nc.gpsimd.tensor_tensor(rstd[0:L, 0:2], var_eps[0:L, 0:2], half[0:L, 0:2], ALU.pow
                                    ).then_inc(cx["c_rs"].sem, 1)
            join(pool, cx, "c_n")
            pool_rstd(pool, A0, 0)
            pool_rstd(pool, A0, 1)
            pool_rstd(pool, A0, 2)
            pool_xh(pool, A0, 0)
            pool_front(pool, A0)
            for blk in range(5, 8):
                pool.wait_ge(*split0["w_high"].at(blk + 1))
                nc.gpsimd.tensor_tensor(WL[:, blk, :], RAW[:, blk, :], WH[:, blk, :].bitcast(F32), ALU.subtract
                                        ).then_inc(split0["low_pool"].sem, 1)
            pool.wait_ge(s_const2, 2)
            pool.wait_ge(ld["rows"], 16)
            join(pool, cx, "c_v")

            def project(Pj, nxt):
                pool_xh(pool, Pj, 0)
                pool_front(pool, Pj, nxt)

            join(pool, A0, "xn")
            pool_cross(pool, C0, 0, split0, 8, P0, "l0_bproj")
            project(P0, M0)
            pool_mlp(pool, M0, "l0_b2", A1)
            pool_front(pool, A1)
            join(pool, A1, "ev")
            pool_self(pool, C1)
            join(pool, A1, "xn")
            pool_bias(P1, "sa_bo", range(NT))
            project(P1, A2)
            pool_front(pool, A2)
            join(pool, M0, "acc")
            join(pool, A2, "xn")
            pool_cross(pool, C2, 1, split1, 0, P2, "ca_bo")
            project(P2, M1)
            pool_mlp(pool, M1, "l1_b2")


def kernel(**inputs):
    import numpy as np
    import concourse.bacc as bacc
    from concourse.bass_utils import run_bass_kernel_spmd

    a = {k: np.asarray(v) for k, v in inputs.items()}
    l0, l1 = "L0_xattn_", "L1_xattn_"

    def square(w):
        k, n = w.shape
        return w.reshape(k // P, P, n).transpose(1, 0, 2).reshape(P, -1, 512)

    weights = np.concatenate(
        [square(a[l0 + "Wq"]), square(a[l0 + "Wproj"])]
        + [square(a[l1 + n].T) for n in ("sa_wq", "sa_wk", "sa_wv", "sa_wo", "ca_wq", "ca_wo")]
        + [square(a[l0 + "W1"]), square(a[l0 + "W2"])], axis=1)
    weights_mlp1 = np.concatenate([square(a[l1 + "mlp_w1"].T), square(a[l1 + "mlp_w2"].T)], axis=1)

    named = {"l0_ln1_w": l0 + "ln1_w", "l0_ln1_b": l0 + "ln1_b", "l0_ln3_w": l0 + "ln3_w", "l0_ln3_b": l0 + "ln3_b",
             "l1_ln1_w": l1 + "ln1_g", "l1_ln1_b": l1 + "ln1_b", "l1_ln2_w": l1 + "ln2_g", "l1_ln2_b": l1 + "ln2_b",
             "l1_ln3_w": l1 + "ln3_g", "l1_ln3_b": l1 + "ln3_b", "l0_ln2_w": l0 + "ln2_w", "l0_ln2_b": l0 + "ln2_b",
             "sa_bq": l1 + "sa_bq", "sa_bk": l1 + "sa_bk", "ca_bq": l1 + "ca_bq", "ca_bk": l1 + "ca_bk",
             "l0_b1": l0 + "b1", "l1_b1": l1 + "mlp_b1"}
    cols = np.zeros((P, NCOLS), np.float32)
    for name, (at, width) in COLS.items():
        if name in named:
            v = a[named[name]]
            for i in range(width):
                part = v[i * P:(i + 1) * P]
                cols[:len(part), at + i] = part
    rows = np.stack([a[n] for n in (l0 + "bproj", l0 + "b2", l1 + "sa_bv", l1 + "sa_bo", l1 + "ca_bo",
                                    l1 + "mlp_b2", l1 + "ca_bv")])
    arrays = {"x": a["x"], "ctx": a["ctx_768"], "weights": weights, "weights_mlp1": weights_mlp1,
              "wkv": a[l0 + "Wkv"], "wck": a[l1 + "ca_wk"].T, "wcv": a[l1 + "ca_wv"].T, "cols": cols, "rows": rows}
    arrays = {k: np.ascontiguousarray(v) for k, v in arrays.items()}

    nc = bacc.Bacc("TRN2", target_bir_lowering=False, num_devices=1, dynamic_dma_scratch_size=1024)
    args = [nc.dram_tensor(k, v.shape, mybir.dt.from_np(v.dtype), kind="ExternalInput").ap()
            for k, v in arrays.items()]
    out = nc.dram_tensor("out", (B, S, D), F32, kind="ExternalOutput").ap()
    build(nc, *args, out)
    r = run_bass_kernel_spmd(nc, [arrays], core_ids=[0])
    return r.results[0]["out"]
```

```python
from contextlib import ExitStack

import concourse.bass as bass
from concourse import mybir

F32, F32R, BF16 = mybir.dt.float32, mybir.dt.float32r, mybir.dt.bfloat16
ALU, ACT, AX = mybir.AluOpType, mybir.ActivationFunctionType, mybir.AxisListType

P = 128
B, S, D, CTX, L = 2, 1024, 256, 192, 77
HEADS, HD, HID = 16, 16, 1024
T = B * S
NT = T // P
CH = 512
NC = T // CH
TPC = CH // P
CT = D // P
KT = S // P
HB = HID // P
EPS = 1e-5
SCALE = HD ** -0.5
GROUPS = 7
SK = GROUPS * HD
SKM = SK + 3
VW = 32
OW = HD + 1
CREDIT = 64

COLS, ROWS = {}, {}
for _n, _w in (("l0_ln1_w", 2), ("l0_ln1_b", 2), ("l0_ln3_w", 2), ("l0_ln3_b", 2), ("l1_ln1_w", 2),
               ("l1_ln1_b", 2), ("l1_ln2_w", 2), ("l1_ln2_b", 2), ("l1_ln3_w", 2), ("l1_ln3_b", 2),
               ("l0_ln2_w", 2), ("l0_ln2_b", 2), ("sa_bq", 2), ("sa_bk", 2), ("ca_bq", 2), ("ca_bk", 2),
               ("l0_b1", 8), ("l1_b1", 8), ("zero", 2)):
    COLS[_n] = (sum(w for _, w in COLS.values()), _w)
NCOLS = sum(w for _, w in COLS.values())
for _n in ("l0_bproj", "l0_b2", "sa_bv", "sa_bo", "ca_bo", "l1_b2", "ca_bv"):
    ROWS[_n] = len(ROWS)

WB_Q0, WB_P0, WB_SQ, WB_SK, WB_SV, WB_SO, WB_CQ, WB_CO, WB_W1, WB_W2 = 0, 1, 2, 3, 4, 5, 6, 7, 8, 12
NWB = 16


class Tally:

    def __init__(self, sem, start, total):
        self.sem, self.start, self.total = sem, start, total

    def at(self, n):
        return self.sem, n + self.start

    @property
    def end(self):
        return self.start + self.total


class Stage(dict):
    prev = w = b = None
    two = True
    nout = qk = 0

    def slot(self, c):
        return c % 2 if self.two else 0

    def place(self, c, o):
        if self.nout > 4 and c >= NC - 2:
            half = self.nout // 2
            return self.nout * (NC - 2) + half * (c - NC + 2) + o + (half if o >= half else 0)
        return self.nout * c + o

    def freed(self, c, ct):
        return 2 * c + ct - (3 if self.two and c > 0 else 1)


def build(nc, x_d, ctx_d, w_d, wm_d, wkv_d, wck_d, wcv_d, cols_d, rows_d, out_d):
    es = ExitStack()
    with es:
        def sb(name, shape, dt):
            return es.enter_context(nc.sbuf_tensor(name, shape, dt))

        def scratch(name, n):
            return nc.dram_tensor(name, [D, 3, n], BF16, kind="Internal").ap()
        q_parts = [scratch("q_parts_l0", T), scratch("q_parts_self", T), scratch("q_parts_cross", T)]
        k_parts = scratch("k_parts_self", T)
        kc_parts = [scratch("kc_parts_l0", B * L), scratch("kc_parts_l1", B * L)]

        X = sb("X", [P, NT, D], F32)
        WH = sb("WH", [P, NWB, 512], F32R)
        WL = sb("WL", [P, NWB, 512], F32R)
        XTH = sb("XTH", [P, 2, CT, CH], F32R)
        XTL = sb("XTL", [P, 2, CT, CH], F32R)
        XN = sb("XN", [P, 2, TPC, D], F32)
        SCR = sb("SCR", [P, 6144], F32)
        STK = sb("STK", [P, 8, T], BF16)
        V = sb("V", [P, NT, D], F32)
        VS = sb("VS", [P, 2, B, KT, VW], F32)
        OU = sb("OU", [P, NT, HEADS, OW], F32)
        KSC = sb("KSC", [P, 2, HEADS, B * L], BF16)
        VC = sb("VC", [L, 2, B, D], F32)
        colv = sb("colv", [P, NCOLS], F32)
        rowv = sb("rowv", [P, len(ROWS), D], F32)
        identf = sb("identf", [P, P], F32)
        identb = sb("identb", [P, P], BF16)
        bst = sb("bst", [P, NT, 6], F32)
        mv = sb("mv", [P, NT, 2], F32)
        var_eps = sb("var_eps", [P, NT], F32)
        rstd = sb("rstd", [P, NT], F32)
        half = sb("half", [P, NT], F32)
        unused = sb("unused", [P, 2], F32)
        rsum = sb("rsum", [P, 2, TPC * HEADS], F32)
        nmax = sb("nmax", [P, 2, NT], F32)
        nres = sb("nres", [P, 2, NT], F32)
        nparts = sb("nparts", [P, 2, 3 * NT], BF16)
        nrow = sb("nrow", [3 * NT, 2, P], BF16)
        PS = es.enter_context(nc.psum_tensor("PS", [P, 8, 512], F32))

        XF = SCR[:, 0:2048].rearrange("p (a c n) -> p a c n", a=2, c=CT)
        RES = SCR[:, 2048:3072].rearrange("p (r n) -> p r n", r=2)
        QP = SCR[:, 3072:6144].bitcast(BF16).rearrange("p (s t n) -> p s t n", s=4, t=3)
        GF = SCR[:, 2048:3072].rearrange("p (r n) -> p r n", r=2)
        PT = SCR[:, 0:4096].rearrange("p (s n) -> p s n", s=2)
        OS = SCR[:, 4096:5120].rearrange("p (s n) -> p s n", s=2)
        RAW = STK[:, :, :].rearrange("p s n -> p (s n)").bitcast(F32).rearrange("p (b n) -> p b n", b=NWB)
        Vf = V[:, :, :].rearrange("p t c -> p (t c)")
        RAW2 = Vf.rearrange("p (b n) -> p b n", b=8)
        WCA = RAW[:, 8:10, :]
        WCB = RAW[0:CTX - P, 10:12, :]
        OUf = OU[:, :, :, :].rearrange("p t h w -> p (t h w)")
        CX = OUf[0:L, 0:384].rearrange("p (b c) -> p b c", b=B)
        CN = OUf[0:L, 384:768].rearrange("p (b c) -> p b c", b=B)
        YT = OUf[:, 768:768 + 4 * B * L].rearrange("p (k n) -> p k n", k=4)
        KR = OUf[:, 1408:1408 + 4 * B * L].rearrange("p (k n) -> p k n", k=4)
        KP = OUf[:, 2048:2048 + 6 * B * L].bitcast(BF16).rearrange("p (k t n) -> p k t n", k=4, t=3)

        def whl(w, blk, ct, off, n):
            return w[:, blk, ct * D + off:ct * D + off + n]

        def w1(w, ct, h):
            f = ct * HID + h * P
            return w[:, WB_W1 + f // 512, f % 512:f % 512 + P]

        def w2(w, h):
            f = h * D
            return w[:, WB_W2 + f // 512, f % 512:f % 512 + D]

        def col(name, i):
            return colv[:, COLS[name][0] + i:COLS[name][0] + i + 1]

        def row(name):
            return rowv[:, ROWS[name], :]

        sems, starts = {}, {}

        def stage(**totals):
            out = Stage()
            for name, total in totals.items():
                if name not in sems:
                    sems[name] = es.enter_context(nc.semaphore(name))
                    starts[name] = CREDIT
                out[name] = Tally(sems[name], starts[name], total)
                starts[name] += total
            return out

        ld = {n: es.enter_context(nc.semaphore("ld_" + n)) 
              for n in ("x0", "x1", "x2", "x3", "ctx", "wq", "w", "wc", "cols", "rows", "mlp0", "mlp1")}
        s_const = es.enter_context(nc.semaphore("s_const"))
        s_vs_const = es.enter_context(nc.semaphore("s_vs_const"))
        s_ones = es.enter_context(nc.semaphore("s_ones"))
        s_passed = es.enter_context(nc.semaphore("s_passed"))
        s_out = es.enter_context(nc.semaphore("s_out"))

        def front(nout, qk, prev=None, w=None, b=None):
            t = dict(bn=NT, bn2=NT if qk else 0, var=NC if qk else 0, rs=NC if qk else 0, xn=NT,
                     xn_pool=0 if qk else NT, tr=NC * CT, xf=NC * CT, xh=NC * CT, xl=NC * CT if qk else 0,
                     mm=nout * NC, ev=nout * NC)
            if qk:
                t |= dict(part1=qk * NC, part2=qk * NC, part3=qk * NC)
                t |= {f"stored{s}": 16 * qk * NC // 4 for s in range(4)}
            else:
                t |= dict(xb=NT)
            st = stage(**t)
            st.nout, st.qk, st.prev, st.w, st.b = nout, qk, prev, w, b
            return st

        def mlp(prev, w, b):
            st = stage(bn=NT, bn2=NT, var=NC, rs=NC, xn=NT, tr=NC * CT, xf=NC * CT, xh=NC * CT, xl=NC * CT,
                       m1=HB * NC, gelu=HB * NC, gh=HB * NC, gl=HB * NC, m2=(HB - 1) * NC, ev=NT, acc=NT, xb=NT)
            st.two, st.prev, st.w, st.b = False, prev, w, b
            return st

        def attention(keys_steps, loads, groups):
            n = HEADS
            ways = 4 if keys_steps == 1 else 2
            stacks = {f"stack{k}": loads * n // ways for k in range(ways)}
            return stage(**stacks, smax=groups * n, maxed=groups * n,
                         msplit=5 * n, mtr=n, mrow=n, mdma0=8 * n, mdma1=8 * n,
                         st=4 * keys_steps * n, exped=4 * keys_steps * n, vs=n, pv=4 * keys_steps * n,
                         os=n, otr=n, ou=n)

        cx = stage(c_bn=2, c_bn2=2, c_var=1, c_rs=1, c_n=2, c_tr=4, c_yt=4, c_mm=8, c_p1=4, c_r=4, c_p2=4, c_p3=4,
                   c_v=4, c_store0=32, c_store1=32, c_stack=16 * 14)
        split0 = stage(w_high=NWB, w_low=NWB)
        A0 = front(2, 2, None, "l0_ln1_w", "l0_ln1_b")
        C0 = attention(1, 32, 2)
        P0 = front(4, 0)
        M0 = mlp(P0, "l0_ln3_w", "l0_ln3_b")
        A1 = front(8, 4, M0, "l1_ln1_w", "l1_ln1_b")
        ones_set = stage(ones_rows=32)
        C1 = attention(KT, 80, NT)
        P1 = front(4, 0)
        A2 = front(2, 2, P1, "l1_ln2_w", "l1_ln2_b")
        split1 = stage(w_high=8, w_low=8)
        C2 = attention(1, 32, 2)
        P2 = front(4, 0)
        M1 = mlp(P2, "l1_ln3_w", "l1_ln3_b")

        def join(eng, st, names):
            for name in names.split():
                eng.wait_ge(st[name].sem, st[name].end)


        def pe_transposes(pe, st, c):
            s = st.slot(c)
            pe.wait_ge(*st["xn"].at(4 * c + 4))
            if st.w is None:
                pe.wait_ge(*st["xn_pool"].at(4 * c + 4))
            for ct in range(CT):
                pe.wait_ge(*st["xf"].at(st.freed(c, ct)))
                for t in range(TPC):
                    last = nc.tensor.transpose(PS[:, 2 * s + ct, t * P:(t + 1) * P],
                                               XN[:, s, t, ct * P:(ct + 1) * P], identf[:])
                last.then_inc(st["tr"].sem, 1)

        def split_mm(out, pairs):
            n = len(pairs)
            for k, (lh, ll, rh, rl) in enumerate(pairs):
                nc.tensor.matmul(out, lh, rh, start=(k == 0), stop=False)
                nc.tensor.matmul(out, ll, rh, start=False, stop=False)
                last = nc.tensor.matmul(out, lh, rl, start=False, stop=(k == n - 1))
            return last

        def parts_of_chunks(st):
            outs = range(st.nout)
            if st.nout <= 4:
                return [(c, outs) for c in range(NC)]
            return [(0, outs), (1, outs), (2, outs[:4]), (3, outs[:4]), (2, outs[4:]), (3, outs[4:])]

        def pe_front(pe, st, tform, tokform, nxt=None):
            outs = [(blk, m, None) for blk, m in tform] + [(blk, None, t) for blk in tokform for t in range(TPC)]
            for c, which in parts_of_chunks(st):
                a = c % 2
                pe.wait_ge(*st["xl" if st.w else "xf"].at(2 * c + 2))
                for o in which:
                    blk, m, t = outs[o]
                    k = st.place(c, o)
                    pe.wait_ge(*st["ev"].at(k - 3))
                    if m is not None:
                        out = PS[:, 4 + k % 4, :]
                        pairs = [(whl(WH, blk, ct, m * P, P), whl(WL, blk, ct, m * P, P),
                                  XTH[:, a, ct, :], XTL[:, a, ct, :]) for ct in range(CT)]
                    else:
                        out = PS[:, 4 + k % 4, 0:D]
                        pairs = [(XTH[:, a, ct, t * P:(t + 1) * P], XTL[:, a, ct, t * P:(t + 1) * P],
                                  whl(WH, blk, ct, 0, D), whl(WL, blk, ct, 0, D)) for ct in range(CT)]
                    split_mm(out, pairs).then_inc(st["mm"].sem, 1)
                    if o == len(outs) // 2 - 1:
                        if c < NC - 2:
                            pe_transposes(pe, st, c + 2)
                        elif nxt and nxt.two and c == NC - 1:
                            pe_transposes(pe, nxt, 1)
                if nxt and c == NC - 2:
                    pe_transposes(pe, nxt, 0)

        def pe_mlp(pe, st, nxt=None):
            def m1(c, h):
                pe.wait_ge(*st["gelu"].at(8 * c + h - 1))
                split_mm(PS[:, 2 + h % 2, :], [(w1(WH, ct, h), w1(WL, ct, h), XTH[:, 0, ct, :], XTL[:, 0, ct, :])
                                               for ct in range(CT)]).then_inc(st["m1"].sem, 1)

            def m2(c, h):
                pe.wait_ge(*st["gh"].at(8 * c + h + 1))
                for t in range(TPC):
                    if h == 0:
                        pe.wait_ge(*st["ev"].at(4 * c + t - 3))
                    g = XTH[:, 1, h % 2, t * P:(t + 1) * P]
                    nc.tensor.matmul(PS[:, 4 + t, 0:D], g, w2(WH, h), start=(h == 0), stop=False)
                    nc.tensor.matmul(PS[:, 4 + t, 0:D], g, w2(WL, h), start=False, stop=False)
                pe.wait_ge(*st["gl"].at(8 * c + h + 1))
                for t in range(TPC):
                    mm = nc.tensor.matmul(PS[:, 4 + t, 0:D], XTL[:, 1, h % 2, t * P:(t + 1) * P], w2(WH, h),
                                          start=False, stop=(h == HB - 1))
                    if h == HB - 1:
                        mm.then_inc(st["acc"].sem, 1)
                    elif t == TPC - 1:
                        mm.then_inc(st["m2"].sem, 1)

            def chunk(c, last):
                pe.wait_ge(*st["xl"].at(2 * c + 2))
                m1(c, 0)
                for h in range(1, HB):
                    m1(c, h)
                    if h < HB - 1:
                        m2(c, h - 1)
                if not last:
                    pe_transposes(pe, st, c + 1)
                elif nxt:
                    pe_transposes(pe, nxt, 0)
                m2(c, HB - 2)
                m2(c, HB - 1)

            for c in range(NC):
                chunk(c, c == NC - 1)
            if nxt:
                join(pe, st, "gelu")
                pe_transposes(pe, nxt, 1)

        def pe_mrow(pe, st, h, par, out):
            pe.wait_ge(*st["msplit"].at(5 * h + 5))
            pe.wait_ge(*st["mrow"].at(h))
            pe.wait_ge(*st["ou"].at(out))
            pe.sem_inc(s_passed, 1)
            nc.tensor.transpose(PS[0:3 * NT, 7, 0:P // 2].bitcast(BF16), nparts[:, par, :], identb[:]
                                ).then_inc(st["mtr"].sem, 1)

        def pe_ot(pe, st, h, par):
            pe.wait_ge(*st["os"].at(h + 1))
            pe.wait_ge(*st["ou"].at(h))
            for i in range(TPC):
                last = nc.tensor.transpose(PS[:, 7, i * P:(i + 1) * P], OS[:, par, i * P:(i + 1) * P], identf[:])
            last.then_inc(st["otr"].sem, 1)

        def order(text):
            return [(dict(m="max", s="score", v="values", r="rows")[w[0]], int(w[1])) for w in text.split()]

        CROSS_STEP = order("m0 s0 s1 v0 v1 v2 v3 r0 s2 m1 s3")

        def pe_cross(pe, st, layer):
            def smax(h, par, g):
                if g == 0:
                    pe.wait_ge(*st[f"stack{h % 4}"].at(32 * (h // 4) + 32))
                pe.wait_ge(*st["maxed"].at(2 * h + g - 1))
                for i in range(8):
                    tile = 8 * g + i
                    b = g
                    last = nc.tensor.matmul(PS[:, 2 * g + i // 4, (i % 4) * P:(i % 4) * P + L],
                                            STK[0:SK, h % 8, tile * P:(tile + 1) * P],
                                            KSC[0:SK, layer, h, b * L:(b + 1) * L], start=True, stop=True)
                last.then_inc(st["smax"].sem, 1)

            def score(h, par, j):
                if j == 0:
                    pe.wait_ge(*st[f"mdma{par}"].at(16 * half_of(h, par) + 16))
                pe.wait_ge(*st["exped"].at(4 * h + j - 1))
                b = j // 2
                nc.tensor.matmul(PS[0:L, 4 + j % 2, :], KSC[0:SKM, layer, h, b * L:(b + 1) * L],
                                 STK[0:SKM, h % 8, j * CH:(j + 1) * CH], start=True, stop=True
                                 ).then_inc(st["st"].sem, 1)

            def values(h, par, j):
                if j == 0:
                    pe.wait_ge(*st["vs"].at(h + 1))
                    pe.wait_ge(*st["os"].at(h))
                pe.wait_ge(*st["exped"].at(4 * h + j + 1))
                nc.tensor.matmul(PS[32 * j:32 * j + VW, 6, :], VS[0:L, par, j // 2, 0, :],
                                 PT[0:L, par, j * CH:(j + 1) * CH], start=True, stop=True
                                 ).then_inc(st["pv"].sem, 1)

            def unit(u, par, on):
                for what, j in CROSS_STEP:
                    if what == "max" and on(0):
                        smax(u, par, j)
                    if what == "rows" and on(2):
                        pe_mrow(pe, st, u - 2, par, u - 6)
                    if what == "score" and on(4):
                        score(u - 4, par, j)
                    if what == "values" and on(5):
                        values(u - 5, 1 - par, j)
                if on(6):
                    pe.wait_ge(*st["mrow"].at(heads_until(u - 1)))
                    pe_ot(pe, st, u - 6, par)

            pipeline(unit)

        def heads_until(n):
            return min(n, HEADS) if isinstance(n, int) else n

        def half_of(h, par):
            return (h - par) // 2

        def pipeline(unit, first=0, last=HEADS + 8):
            for u in range(first, last):
                unit(u, u % 2, lambda k, u=u: 0 <= u - k < HEADS)

        def self_lag(s, lag):
            g = s - lag
            return -(g // KT), g % KT

        def pipeline_self(eng, unit):
            for u in range(2):
                unit(u, u % 4, lambda k, u=u: 0 <= u - k < HEADS)
            with eng.Fori(0, 3) as i:
                for k in range(2, 6):
                    unit(4 * i + k, k % 4, lambda k: True)
            for u in range(14, HEADS + 3):
                unit(u, u % 4, lambda k, u=u: 0 <= u - k < HEADS)

        def score_banks(drain):
            return (4, 5, 0, 1) if drain else (4, 5, 4, 5)

        SELF_STEP = order("m0 s0 m1 s1 v0 v1 v2 v3 s2 m2 s3 m3")

        def pe_self(pe, st):
            def smax(h, m, i, n):
                if i == 0 and n == 0:
                    pe.wait_ge(*st[f"stack{m % 2}"].at(80 * half_of(h, m % 2) + 80))
                if n == 0:
                    pe.wait_ge(*st["maxed"].at(16 * h + i - 1))
                b = i // KT
                mm = nc.tensor.matmul(PS[:, 2 * (i % 2) + n, :], STK[0:SK, m, i * P:(i + 1) * P],
                                      STK[0:SK, m + 4, b * S + n * CH:b * S + (n + 1) * CH],
                                      start=True, stop=True)
                if n == 1:
                    mm.then_inc(st["smax"].sem, 1)

            def score(h, m, kt, j, drain, first):
                if kt == 0 and j == 0:
                    pe.wait_ge(*st[f"mdma{m % 2}"].at(16 * half_of(h, m % 2) + 16))
                banks = score_banks(drain)
                if drain and kt == 4 and j == 2:
                    join(pe, st, "maxed")
                pe.wait_ge(*st["exped"].at(32 * h + 4 * kt + j + 1 - (2 if first else len(set(banks)))))
                b = j // 2
                nc.tensor.matmul(PS[:, banks[j], :], STK[0:SKM, m + 4, b * S + kt * P:b * S + (kt + 1) * P],
                                 STK[0:SKM, m, j * CH:(j + 1) * CH], start=True, stop=True
                                 ).then_inc(st["st"].sem, 1)

            def values(h, par, kt, j):
                if kt == 0 and j == 0:
                    pe.wait_ge(*st["vs"].at(h + 1))
                    pe.wait_ge(*st["os"].at(h))
                pe.wait_ge(*st["exped"].at(32 * h + 4 * kt + j + 1))
                nc.tensor.matmul(PS[32 * j:32 * j + VW, 6, :], VS[:, par, j // 2, kt, :],
                                 PT[:, kt % 2, j * CH:(j + 1) * CH], start=(kt == 0), stop=(kt == KT - 1)
                                 ).then_inc(st["pv"].sem, 1)

            def unit(u, m, on):
                par = m % 2
                for s in range(KT):
                    if s == 2 and on(1):
                        pe_mrow(pe, st, u - 1, 1 - par, u - 2)
                    back, kt = self_lag(s, 12)
                    vback, vkt = self_lag(s, 13)
                    for what, j in SELF_STEP:
                        if what == "max" and on(0):
                            smax(u, m, 2 * s + j // 2, j % 2)
                        if what == "score" and on(back):
                            draining = isinstance(u, int) and u >= HEADS
                            score(u - back, (m - back) % 4, kt, j, draining, isinstance(u, int) and u == HEADS and s == 0)
                        if what == "values" and on(vback):
                            values(u - vback, (m - vback) % 2, vkt, j)
                    if s == 6 and on(2):
                        pe.wait_ge(*st["mrow"].at(heads_until(u)))
                        pe_ot(pe, st, u - 2, par)

            pipeline_self(pe, unit)

        def act_high(act, st, c):
            for ct in range(CT):
                act.wait_ge(*st["tr"].at(2 * c + ct + 1))
                act.wait_ge(*st["mm"].at(max(st.nout * (c - 1), 0)))
                nc.scalar.copy(XTH[:, c % 2, ct, :], PS[:, 2 * (c % 2) + ct, :]).then_inc(st["xh"].sem, 1)

        def act_xf(act, st, c):
            s = st.slot(c)
            for ct in range(CT):
                act.wait_ge(*st["tr"].at(2 * c + ct + 1))
                act.wait_ge(*st["xl"].at(st.freed(c, ct)))
                nc.scalar.activation(XF[:, s, ct, :], PS[:, 2 * s + ct, :], ACT.Identity,
                                     scale=col(st.w, ct), bias=col(st.b, ct)).then_inc(st["xf"].sem, 1)

        def act_part2(act, st, k):
            act.wait_ge(*st["ev"].at(st.place(k // st.qk, k % st.qk) + 1))
            nc.scalar.copy(QP[:, k % 4, 1, :], RES[:, k % 2, :]).then_inc(st["part2"].sem, 1)

        def act_xh(act, st, c):
            for ct in range(CT):
                act.wait_ge(*st["xf"].at(2 * c + ct + 1))
                if c > 1:
                    act.wait_ge(*st["mm"].at(st.nout * (c - 1)))
                elif st is A1:
                    join(act, M0, "acc" if c else "m1")
                elif st is A2:
                    act.wait_ge(*P1["mm"].at(16 if c else 12))
                nc.scalar.copy(XTH[:, c % 2, ct, :], XF[:, c % 2, ct, :]).then_inc(st["xh"].sem, 1)

        def act_front(act, st, biases, nxt=None, after={}):
            for c in range(NC):
                for o, (name, m) in enumerate(biases):
                    k = st.qk * c + o
                    act.wait_ge(*st["mm"].at(st.place(c, o) + 1))
                    act.wait_ge(*st[f"stored{k % 4}"].at(16 * (k // 4)))
                    nc.scalar.activation(QP[:, k % 4, 0, :], PS[:, 4 + st.place(c, o) % 4, :], ACT.Identity,
                                         bias=col(name, m)).then_inc(st["part1"].sem, 1)
                    if o > 0:
                        act_part2(act, st, k - 1)
                    if o == st.nout // 2 - 1 and c < NC - 2:
                        act_xf(act, st, c + 2)
                    if o == st.qk - 1:
                        act_part2(act, st, k)
                if biases and c < NC - 2:
                    act_xh(act, st, c + 2)
                if c in after:
                    after[c]()
                if not biases:
                    if c < NC - 2:
                        act_high(act, st, c + 2)
                    elif c == NC - 2:
                        if not nxt.two:
                            nc.scalar.activation(unused[:, 1:2], half[:, 0:1], ACT.Gelu)
                        join(act, st, "xf")
                        act_xf(act, nxt, 0)
                        if nxt.two:
                            act_xh(act, nxt, 0)
                    elif nxt.two:
                        act_xf(act, nxt, 1)
                        act_xh(act, nxt, 1)

        def act_mlp(act, st, b1, nxt=None):
            def chunk(c, last):
                for h in range(HB):
                    act.wait_ge(*st["m1"].at(8 * c + h + 1))
                    act.wait_ge(*st["gl"].at(8 * c + h - 1))
                    nc.scalar.activation(GF[:, h % 2, :], PS[:, 2 + h % 2, :], ACT.Gelu, bias=col(b1, h)
                                         ).then_inc(st["gelu"].sem, 1)
                if not last:
                    act_xf(act, st, c + 1)
                elif nxt:
                    act_xf(act, nxt, 0)
                    act_xh(act, nxt, 0)
            for c in range(NC):
                chunk(c, c == NC - 1)
            if nxt:
                act_xf(act, nxt, 1)
                act_xh(act, nxt, 1)

        def out_view(h):
            return OU[:, :, h, :].rearrange("p (j i) w -> p j i w", i=TPC)

        BACK = PS[:, 7, :].rearrange("p (i j w) -> p j i w", i=TPC, j=4)[:, :, :, 0:OW]

        def act_cross(act, st):
            def unit(u, par, on):
                if on(7):
                    act.wait_ge(*st["otr"].at(u - 6))
                    nc.scalar.copy(out_view(u - 7), BACK).then_inc(st["ou"].sem, 1)
                if on(4):
                    h = u - 4
                    for j in range(4):
                        act.wait_ge(*st["st"].at(4 * h + j + 1))
                        act.wait_ge(*st["pv"].at(4 * h + j - 7))
                        nc.scalar.activation(PT[0:L, par, j * CH:(j + 1) * CH], PS[0:L, 4 + j % 2, :], ACT.Exp,
                                             scale=SCALE).then_inc(st["exped"].sem, 1)
            pipeline(unit)

        def act_self(act, st):
            def unit(u, m, on):
                par = m % 2
                for s in range(KT):
                    if s == 5 and on(2):
                        act.wait_ge(*st["pv"].at(32 * (u - 2) + 32))
                        act.wait_ge(*st["otr"].at(u - 3))
                        nc.scalar.copy(OS[:, par, :], PS[:, 6, :]).then_inc(st["os"].sem, 1)
                    if s == 7 and on(2):
                        act.wait_ge(*st["otr"].at(u - 1))
                        nc.scalar.copy(out_view(u - 2), BACK).then_inc(st["ou"].sem, 1)
                    back, kt = self_lag(s, 12)
                    if on(back):
                        g = KT * (u - back) + kt
                        for j in range(4):
                            act.wait_ge(*st["st"].at(4 * g + j + 1))
                            act.wait_ge(*st["pv"].at(4 * g + j - 7))
                            nc.scalar.activation(PT[:, kt % 2, j * CH:(j + 1) * CH],
                                                 PS[:, score_banks(isinstance(u, int) and u >= HEADS)[j], :], ACT.Exp,
                                                 scale=SCALE).then_inc(st["exped"].sem, 1)
            pipeline_self(act, unit)

        def dve_stats(dve, st, c):
            s0 = 4 * c
            if st is A0:
                dve.wait_ge(ld[f"x{c}"], 16)
            else:
                dve.wait_ge(*st.prev["ev"].at(4 * c + 4))
            for t in range(TPC):
                nc.vector.bn_stats(bst[:, s0 + t, :], X[:, 4 * c + t, :]).then_inc(st["bn"].sem, 1)
            for t in range(TPC):
                dve.wait_ge(*st["bn"].at(4 * c + t + 1))
                dve.sem_inc(s_passed, 1)
                nc.vector.bn_aggr(mv[:, s0 + t, :], bst[:, s0 + t, :]).then_inc(st["bn2"].sem, 1)

        def divided(c, t):
            return (XN[:, c % 2, t, :].rearrange("p (h d) -> p h d", h=HEADS), OU[:, 4 * c + t, :, 0:HD],
                    rsum[:, c % 2, t * HEADS:(t + 1) * HEADS].rearrange("p (h o) -> p h o", o=1)
                    .to_broadcast([P, HEADS, HD]))

        def dve_norm(dve, st, c):
            a = st.slot(c)
            dve.wait_ge(*st["tr"].at(2 * c - 2 if st.two and c > 0 else 2 * c))
            if st.w is not None:
                dve.wait_ge(*st["rs"].at(c + 1))
                for t in range(TPC):
                    nc.vector.tensor_scalar(XN[:, a, t, :], X[:, 4 * c + t, :], mv[:, 4 * c + t, 0:1],
                                            rstd[:, 4 * c + t:4 * c + t + 1], ALU.subtract, ALU.mult
                                            ).then_inc(st["xn"].sem, 1)
            else:
                nc.vector.reciprocal(rsum[:, a, :].rearrange("p (t h) -> p t h", t=TPC),
                                     OU[:, 4 * c:4 * c + 4, :, HD]).then_inc(st["bn"].sem, 4)
                dve.wait_ge(*st["bn"].at(4 * c + 4))
                for t in range(TPC // 2):
                    nc.vector.tensor_tensor(*divided(c, t), ALU.mult).then_inc(st["xn"].sem, 2)

        def dve_xl(dve, st, c):
            s = st.slot(c)
            for ct in range(CT):
                dve.wait_ge(*st["xh"].at(2 * c + ct + 1))
                if st.w:
                    nc.vector.tensor_tensor(XTL[:, s, ct, :], XF[:, s, ct, :], XTH[:, s, ct, :].bitcast(F32),
                                            ALU.subtract).then_inc(st["xl"].sem, 1)
                else:
                    nc.vector.tensor_tensor(XTL[:, s, ct, :], PS[:, 2 * s + ct, :], XTH[:, s, ct, :].bitcast(F32),
                                            ALU.subtract).then_inc(st["xf"].sem, 1)

        def stats_ahead(nxt, c):
            return (c - 1,) if c == 1 or nxt.two and c > 1 else ()

        def dve_front(dve, st, biases, tok, nxt=None, after={}):
            for c in range(NC):
                if c < NC - 2 and (st.w or c == 0):
                    dve_norm(dve, st, c + 2)
                if c < NC - 1:
                    dve_xl(dve, st, c + 1)
                if c == 0 and not st.w:
                    dve_norm(dve, st, 3)
                if nxt and (c == NC - 2 or c == NC - 1 and nxt.two):
                    dve_norm(dve, nxt, c - NC + 2)
                if nxt:
                    for k in stats_ahead(nxt, c):
                        dve_stats(dve, nxt, k)
                if c == 0 and st.w:
                    dve_stats(dve, st, 3)
                for o, (name, m) in enumerate(biases):
                    k = st.qk * c + o
                    dve.wait_ge(*st["part1"].at(k + 1))
                    dve.wait_ge(*st["part3"].at(k - 1))
                    nc.vector.scalar_tensor_tensor(RES[:, k % 2, :], PS[:, 4 + st.place(c, o) % 4, :],
                                                   col(name, m), QP[:, k % 4, 0, :],
                                                   ALU.add, ALU.subtract).then_inc(st["ev"].sem, 1)
                if not tok or st.nout > 4 and c == NC - 2:
                    tiles = []
                elif st.nout > 4 and c == NC - 1:
                    tiles = [(v, t) for v in (c - 1, c) for t in range(TPC)]
                else:
                    tiles = [(c, t) for t in range(TPC)]
                for v, t in tiles:
                    k = st.place(v, st.qk + t)
                    dve.wait_ge(*st["mm"].at(k + 1))
                    ps = PS[:, 4 + k % 4, 0:D]
                    if tok == "v":
                        nc.vector.tensor_tensor(V[:, 4 * v + t, :], ps, row("sa_bv"), ALU.add
                                                ).then_inc(st["ev"].sem, 1)
                    else:
                        dve.wait_ge(*st["xb"].at(4 * v + t + 1))
                        nc.vector.tensor_tensor(X[:, 4 * v + t, :], ps, X[:, 4 * v + t, :], ALU.add
                                                ).then_inc(st["ev"].sem, 1)
                        if v == NC - 1 and t == 1:
                            dve_xl(dve, nxt, 0)
                if c in after:
                    after[c]()

        def dve_mlp(dve, st, nxt=None):
            def chunk(c, last):
                for h in range(HB):
                    dve.wait_ge(*st["gh"].at(8 * c + h + 1))
                    nc.vector.tensor_tensor(XTL[:, 1, h % 2, :], GF[:, h % 2, :], XTH[:, 1, h % 2, :].bitcast(F32),
                                            ALU.subtract).then_inc(st["gl"].sem, 1)
                    if h == 2 and not last:
                        dve_stats(dve, st, c + 1)
                    if h == 5 and not last:
                        dve_norm(dve, st, c + 1)
                    if last and nxt and h in (1, 2, 3):
                        dve_stats(dve, nxt, h - 1)
                    if last and nxt and h in (5, 6):
                        dve_norm(dve, nxt, h - 5)
                if not last:
                    dve_xl(dve, st, c + 1)
                elif nxt:
                    dve_xl(dve, nxt, 0)
                for t in range(TPC):
                    dve.wait_ge(*st["acc"].at(4 * c + t + 1))
                    dve.wait_ge(*st["xb"].at(4 * c + t + 1))
                    nc.vector.tensor_tensor(X[:, 4 * c + t, :], PS[:, 4 + t, 0:D], X[:, 4 * c + t, :], ALU.add
                                            ).then_inc(st["ev"].sem, 1)
            join(dve, st.prev, "ev")
            for c in range(NC):
                chunk(c, c == NC - 1)

        def dve_mrow(dve, st, h, par):
            dve.wait_ge(*st["mtr"].at(h + 1))
            dve.wait_ge(*st[f"mdma{par}"].at(16 * half_of(h, par)))
            nc.vector.tensor_copy(nrow[:, par, :], PS[0:3 * NT, 7, 0:P // 2].bitcast(BF16)
                                  ).then_inc(st["mrow"].sem, 1)

        def dve_cross(dve, st):
            def unit(u, par, on):
                if on(6):
                    dve.wait_ge(*st["pv"].at(4 * (u - 5)))
                    dve.wait_ge(*st["otr"].at(u - 7))
                    nc.vector.tensor_copy(OS[:, par, :], PS[:, 6, :]).then_inc(st["os"].sem, 1)
                for g in range(2):
                    if on(0):
                        dve.wait_ge(*st["smax"].at(2 * u + g + 1))
                        if g == 0:
                            dve.wait_ge(*st["msplit"].at(5 * (u - 1)))
                        nc.vector.tensor_reduce(
                            nmax[:, par, 8 * g:8 * g + 8],
                            PS[:, 2 * g:2 * g + 2, :].rearrange("p k (i n) -> p (k i) n", i=4)[:, :, 0:L],
                            AX.X, ALU.max, negate=True).then_inc(st["maxed"].sem, 1)
                    if g == 0 and on(2):
                        dve_mrow(dve, st, u - 2, par)
            pipeline(unit)

        def dve_self(dve, st):
            def unit(u, m, on):
                par = m % 2
                for s in range(KT):
                    if s == 2 and on(1):
                        dve_mrow(dve, st, u - 1, 1 - par)
                    if on(0):
                        for i in (2 * s, 2 * s + 1):
                            dve.wait_ge(*st["smax"].at(16 * u + i + 1))
                            if i == 0:
                                dve.wait_ge(*st["msplit"].at(5 * (u - 1)))
                            nc.vector.tensor_reduce(nmax[:, par, i:i + 1], PS[:, 2 * (i % 2):2 * (i % 2) + 2, :],
                                                    AX.XY, ALU.max, negate=True).then_inc(st["maxed"].sem, 1)
            pipeline_self(dve, unit)

        def pool_copy(out, in_):
            return nc.gpsimd.tensor_scalar(out, in_, 1.0, 0.0, ALU.mult, ALU.add)

        def pool_rstd(pool, st, c):
            at = slice(4 * c, 4 * c + 4)
            pool.wait_ge(*st["bn2"].at(4 * c + 4))
            pool.sem_inc(s_passed, 1)
            nc.gpsimd.tensor_scalar(var_eps[:, at], mv[:, at, 1], EPS, 1.0, ALU.add, ALU.mult
                                    ).then_inc(st["var"].sem, 1)
            pool.wait_ge(*st["var"].at(c + 1))
            pool.sem_inc(s_passed, 1)
            nc.gpsimd.tensor_tensor(rstd[:, at], var_eps[:, at], half[:, at], ALU.pow).then_inc(st["rs"].sem, 1)

        def pool_xh(pool, st, c):
            for ct in range(CT):
                pool.wait_ge(*st["xf"].at(2 * c + ct + 1))
                pool.sem_inc(s_passed, 1)
                if c == 0:
                    pool.wait_ge(*st.prev["mm"].at(12))
                else:
                    pool.wait_ge(*st["m1"].at(8 * c))
                pool_copy(XTH[:, 0, ct, :], XF[:, 0, ct, :]).then_inc(st["xh"].sem, 1)

        def pool_divide(pool, st, c):
            pool.wait_ge(*st["bn"].at(4 * c + 4))
            pool.wait_ge(*st["tr"].at(2 * c - 2 if c else 0))
            for t in range(TPC // 2, TPC):
                nc.gpsimd.tensor_tensor(*divided(c, t), ALU.mult).then_inc(st["xn_pool"].sem, 2)

        def pool_front(pool, st, nxt=None):
            for c in range(NC):
                if nxt:
                    for k in stats_ahead(nxt, c):
                        pool_rstd(pool, nxt, k)
                if st.w is None and c == 0:
                    pool_divide(pool, st, 2)
                    pool_divide(pool, st, 3)
                if c == 0 and st.w:
                    pool_rstd(pool, st, 3)
                if c == NC - 1 and nxt:
                    if not nxt.two:
                        pool_xh(pool, nxt, 0)
                for o in range(st.qk):
                    k = st.qk * c + o
                    pool.wait_ge(*st["part2"].at(k + 1))
                    pool.sem_inc(s_passed, 1)
                    nc.gpsimd.tensor_tensor(QP[:, k % 4, 2, :], RES[:, k % 2, :], QP[:, k % 4, 1, :],
                                            ALU.subtract).then_inc(st["part3"].sem, 1)

        def pool_mlp(pool, st, b2, nxt=None):
            def chunk(c, last):
                for h in range(HB):
                    pool.wait_ge(*st["gelu"].at(8 * c + h + 1))
                    pool.sem_inc(s_passed, 1)
                    if h < 2:
                        pool.wait_ge(*st["acc"].at(4 * c))
                        pool.sem_inc(s_passed, 1)
                    else:
                        pool.wait_ge(*st["m2"].at(7 * c + h - 1))
                        pool.sem_inc(s_passed, 1)
                    pool_copy(XTH[:, 1, h % 2, :], GF[:, h % 2, :]).then_inc(st["gh"].sem, 1)
                    if 1 <= h <= TPC:
                        if h == 1:
                            pool.wait_ge(*st["xn"].at(4 * c + 4))
                            pool.sem_inc(s_passed, 1)
                        nc.gpsimd.tensor_tensor(X[:, 4 * c + h - 1, :], X[:, 4 * c + h - 1, :], row(b2), ALU.add
                                                ).then_inc(st["xb"].sem, 1)
                    if h == 3 and not last:
                        pool_rstd(pool, st, c + 1)
                    if last and nxt and h in (3, 4, 5):
                        pool_rstd(pool, nxt, h - 3)
                if not last:
                    pool_xh(pool, st, c + 1)
            pool.wait_ge(*st.prev["mm"].at(NT))
            pool.sem_inc(s_passed, 1)
            for c in range(NC):
                chunk(c, c == NC - 1)

        def pool_msplit(pool, st, h, par, ngroups):
            pool.wait_ge(*st["maxed"].at(ngroups * (h + 1)))
            pool.sem_inc(s_passed, 1)
            pool.wait_ge(*st["mtr"].at(h - 1))
            pool.sem_inc(s_passed, 1)
            src = nmax
            for k in range(3):
                part = nparts[:, par, NT * k:NT * (k + 1)]
                pool_copy(part, src[:, par, :]).then_inc(st["msplit"].sem, 1)
                pool.wait_ge(*st["msplit"].at(5 * h + 2 * k + 1))
                pool.sem_inc(s_passed, 1)
                if k < 2:
                    nc.gpsimd.tensor_tensor(nres[:, par, :], src[:, par, :], part, ALU.subtract
                                            ).then_inc(st["msplit"].sem, 1)
                    pool.wait_ge(*st["msplit"].at(5 * h + 2 * k + 2))
                    pool.sem_inc(s_passed, 1)
                    src = nres

        def pool_bias(st, bias, tiles):
            for t in tiles:
                nc.gpsimd.tensor_tensor(X[:, t, :], X[:, t, :], row(bias), ALU.add).then_inc(st["xb"].sem, 1)

        def pool_cross(pool, st, layer, Pj, bias):
            def unit(u, par, on):
                if on(4):
                    h = u - 4
                    pool.wait_ge(*st["pv"].at(4 * (h - 1)))
                    pool.sem_inc(s_passed, 1)
                    nc.gpsimd.tensor_copy(VS[0:L, par, :, 0, 0:HD], VC[:, layer, :, bass.ds(h * HD, HD)]
                                          ).then_inc(st["vs"].sem, 1)
                if on(0):
                    pool_msplit(pool, st, u, par, 2)
                if HEADS <= u < HEADS + 4:
                    pool_bias(Pj, bias, range(4 * (u - HEADS), 4 * (u - HEADS) + 4))
            pipeline(unit)

        def pool_self(pool, st):
            Vv = V[:, :, :].rearrange("p (b k) c -> p b k c", b=B)

            def unit(u, m, on):
                par = m % 2
                if on(1):
                    h = u - 1
                    pool.wait_ge(*st["pv"].at(32 * (h - 1)))
                    pool.sem_inc(s_passed, 1)
                    nc.gpsimd.tensor_copy(VS[:, 1 - par, :, :, 0:HD], Vv[:, :, :, bass.ds(h * HD, HD)]
                                          ).then_inc(st["vs"].sem, 1)
                if on(0):
                    pool_msplit(pool, st, u, par, NT)
            pipeline_self(pool, unit)

        def sp_store_parts(sp, st, dests, ks):
            for k in ks:
                c = k // st.qk
                dst, m = dests[k % st.qk]
                sp.wait_ge(*st["part3"].at(k + 1))
                sp.dma_start(dst[m * P:(m + 1) * P, :, c * CH:(c + 1) * CH], QP[:, k % 4, :, :]
                             ).then_inc(st[f"stored{k % 4}"].sem, 16)

        def load_q(sp, st, way, h, slot, src):
            parts = src[bass.ds(h * HD, HD), :, :].rearrange("(g d) t n -> g (d t) n", g=1)
            sp.dma_start(STK[0:96, slot, :], parts.to_broadcast([2, 48, T])).then_inc(st[f"stack{way}"].sem, 16)
            sp.dma_start(STK[96:SK, slot, :], src[bass.ds(h * HD, HD), 0, :]).then_inc(st[f"stack{way}"].sem, 16)

        def load_k(sp, st, way, h, slot, src):
            for g in range(2):
                sp.dma_start(STK[48 * g:48 * g + 48, slot, :], src[bass.ds(h * HD, HD), g:g + 1, :]
                             .to_broadcast([HD, 3, T])).then_inc(st[f"stack{way}"].sem, 16)
            sp.dma_start(STK[96:SK, slot, :], src[bass.ds(h * HD, HD), 2, :]).then_inc(st[f"stack{way}"].sem, 16)

        def store_mrow(sp, st, h, par, slot):
            sp.wait_ge(*st["mrow"].at(h + 1))
            sp.dma_start(STK[SK:SKM, slot, :],
                         nrow[:, par, :]
                         ).then_inc(st[f"mdma{par}"].sem, 16)

        def sp_cross(sp, st, src, A, stores):
            def load(h, par):
                sp.wait_ge(*st["st"].at(4 * (h - 7)))
                sp.wait_ge(*st[f"stack{h % 4}"].at(32 * (h // 4)))
                load_q(sp, st, h % 4, h, h % 8, src)

            def unit(u, par, on):
                if on(2):
                    store_mrow(sp, st, u - 2, par, (u - 2) % 8)
                if u == 4:
                    join(sp, A, "stored1 stored3")
                if on(-4):
                    load(u + 4, par)
            load(0, 0)
            stores()
            for h in range(1, 4):
                load(h, h % 2)
            pipeline(unit, last=HEADS + 2)

        def sp_self(sp, st, stores):
            def load(h, m):
                par = m % 2
                sp.wait_ge(*st["st"].at(32 * (h - 3)))
                sp.wait_ge(*st[f"stack{par}"].at(80 * half_of(h, par)))
                load_q(sp, st, par, h, m, q_parts[1])
                load_k(sp, st, par, h, m + 4, k_parts)

            def unit(u, m, on):
                if on(1):
                    store_mrow(sp, st, u - 1, (m + 1) % 2, (m - 1) % 4)
                if on(-2):
                    load(u + 2, (m + 2) % 4)
            load(0, 0)
            stores()
            load(1, 1)
            join(sp, A1, "stored2 stored3")
            pipeline_self(sp, unit)

        block = es.enter_context(nc.Block())
        qk0 = [("zero", 0), ("zero", 1)]
        qk1 = [("sa_bq", 0), ("sa_bk", 0), ("sa_bq", 1), ("sa_bk", 1)]
        qk2 = [("ca_bq", 0), ("ca_bq", 1)]

        @block.sync
        def _(sp):
            for counting in sems.values():
                sp.sem_inc(counting, CREDIT)
            def load_x(c):
                b, h = c // 2, c % 2
                sp.dma_start(X[:, 4 * c:4 * c + 4, :], x_d[b, h * CH:(h + 1) * CH, :].rearrange("(t p) c -> p t c", p=P)
                             ).then_inc(ld[f"x{c}"], 16)
            sp.dma_start(colv[:], cols_d).then_inc(ld["cols"], 16)
            sp.dma_start(CX[:], ctx_d.rearrange("b t c -> t b c")).then_inc(ld["ctx"], 16)
            load_x(0)
            sp.dma_start(RAW[:, 0:2, :], w_d[:, 0:2, :]).then_inc(ld["wq"], 16)
            load_x(1)
            sp.dma_start(WCA[:, 0, :], wkv_d[0:P, :]).then_inc(ld["wc"], 16)
            sp.dma_start(WCB[:, 0, :], wkv_d[P:CTX, :]).then_inc(ld["wc"], 16)
            for i, w in enumerate((wck_d, wcv_d)):
                sp.dma_start(WCA[:, 1, i * D:(i + 1) * D], w[0:P, :]).then_inc(ld["wc"], 16)
                sp.dma_start(WCB[:, 1, i * D:(i + 1) * D], w[P:CTX, :]).then_inc(ld["wc"], 16)
            load_x(2)
            load_x(3)
            sp.dma_start(rowv[:], rows_d.rearrange("(o r) c -> o r c", o=1).to_broadcast([P, len(ROWS), D])
                         ).then_inc(ld["rows"], 16)
            sp.dma_start(RAW[:, 2:8, :], w_d[:, 2:8, :]).then_inc(ld["w"], 16)
            sp.dma_start(RAW2, w_d[:, 8:NWB, :]).then_inc(ld["mlp0"], 16)
            q_dests = [(q_parts[0], 0), (q_parts[0], 1)]
            sp_store_parts(sp, A0, q_dests, range(2))
            def store_context(layer):
                for i in (2 * layer, 2 * layer + 1):
                    sp.wait_ge(*cx["c_p3"].at(i + 1))
                    sp.dma_start(kc_parts[layer][(i % 2) * P:(i % 2 + 1) * P, :, :],
                                 KP[:, i, :, :]).then_inc(cx[f"c_store{layer}"].sem, 16)
            def stack_context(layer):
                sp.wait_ge(*cx[f"c_store{layer}"].at(32))
                for g in range(GROUPS):
                    rows = slice(48 * (g // 3) + g % 3, 48 * (g // 3) + 48, 3) if g < 6 else slice(96, SK)
                    sp.dma_start(KSC[rows, layer, :, :],
                                 kc_parts[layer][:, g // 3, :].rearrange("(h d) n -> d h n", d=HD)
                                 ).then_inc(cx["c_stack"].sem, 16)
            store_context(0)
            store_context(1)
            sp.wait_ge(s_ones, 1)
            stack_context(0)
            sp_store_parts(sp, A0, q_dests, range(2, 7))
            join(sp, A0, "stored0 stored2")
            sp.wait_ge(*split0["w_low"].at(8))
            join(sp, cx, "c_mm")
            sp_cross(sp, C0, q_parts[0], A0, lambda: sp_store_parts(sp, A0, q_dests, range(7, 8)))
            stack_context(1)
            join(sp, C0, "st")
            ones = KSC[SK:SKM, :, :, :].rearrange("p l h n -> p (l h n)")[:, 0:2 * T].rearrange("p (s n) -> p s n", s=2)
            for k in range(2):
                sp.dma_start(STK[SK:SKM, 4 + 2 * k:6 + 2 * k, :], ones).then_inc(ones_set["ones_rows"].sem, 16)
            qk_dests = [(q_parts[1], 0), (k_parts, 0), (q_parts[1], 1), (k_parts, 1)]
            sp_store_parts(sp, A1, qk_dests, range(14))
            join(sp, A1, "stored0 stored1")
            join(sp, C0, "smax st")
            join(sp, ones_set, "ones_rows")
            sp_self(sp, C1, lambda: sp_store_parts(sp, A1, qk_dests, range(14, 16)))
            join(sp, C1, "vs")
            sp.dma_start(RAW2, wm_d).then_inc(ld["mlp1"], 16)
            qc_dests = [(q_parts[2], 0), (q_parts[2], 1)]
            sp_store_parts(sp, A2, qc_dests, range(7))
            join(sp, A2, "stored0 stored2")
            join(sp, C1, "st")
            sp_cross(sp, C2, q_parts[2], A2, lambda: sp_store_parts(sp, A2, qc_dests, range(7, 8)))
            for c in range(NC):
                sp.wait_ge(*M1["ev"].at(4 * c + 4))
                b, h = c // 2, c % 2
                sp.dma_start(out_d[b, h * CH:(h + 1) * CH, :].rearrange("(t p) c -> p t c", p=P),
                             X[:, 4 * c:4 * c + 4, :]).then_inc(s_out, 16)
            sp.wait_ge(s_out, 16 * NC)

        @block.tensor
        def _(pe):
            pe.wait_ge(s_const, 3)
            pe.wait_ge(ld["ctx"], 16)
            for layer in (1, 0):
                src = CX if layer else CN
                if layer == 0:
                    pe.wait_ge(*cx["c_n"].at(2))
                for k, (c0, cn) in enumerate(((0, P), (P, CTX - P))):
                    for b in range(B):
                        last = nc.tensor.transpose(PS[0:cn, 4 + 2 * layer + k, b * L:(b + 1) * L],
                                                   src[:, b, c0:c0 + cn], identf[0:L, 0:L])
                    last.then_inc(cx["c_tr"].sem, 1)
            pe_transposes(pe, A0, 0)
            pe.wait_ge(ld["wc"], 96)
            pe.wait_ge(*cx["c_yt"].at(4))
            for i in range(4):
                layer, m = i // 2, i % 2
                nc.tensor.matmul(PS[:, 4 + i, 0:B * L], WCA[:, layer, m * P:(m + 1) * P], YT[:, 2 * layer, :],
                                 start=True, stop=False)
                nc.tensor.matmul(PS[:, 4 + i, 0:B * L], WCB[:, layer, m * P:(m + 1) * P],
                                 YT[0:CTX - P, 2 * layer + 1, :], start=False, stop=True
                                 ).then_inc(cx["c_mm"].sem, 1)
            pe_transposes(pe, A0, 1)
            for i in range(4):
                layer, b = i // 2, i % 2
                pe.wait_ge(*cx["c_r"].at(i + 1))
                nc.tensor.matmul(PS[0:L, 4 + i, 0:D], YT[:, 2 * layer, b * L:(b + 1) * L], WCA[:, layer, D:2 * D],
                                 start=True, stop=False)
                nc.tensor.matmul(PS[0:L, 4 + i, 0:D], YT[0:CTX - P, 2 * layer + 1, b * L:(b + 1) * L],
                                 WCB[:, layer, D:2 * D], start=False, stop=True).then_inc(cx["c_mm"].sem, 1)
            join(pe, cx, "c_v")
            pe.wait_ge(*split0["w_low"].at(2))
            pe_front(pe, A0, [(WB_Q0, 0), (WB_Q0, 1)], [])
            join(pe, A0, "xf ev")
            pe.wait_ge(*cx["c_stack"].at(16 * GROUPS))
            pe.wait_ge(s_vs_const, 2)
            pe.wait_ge(s_ones, 2)

            def project(C, Pj, blk, nxt):
                join(pe, C, "maxed exped os ou")
                pe_transposes(pe, Pj, 0)
                pe_transposes(pe, Pj, 1)
                pe_front(pe, Pj, [], [blk], nxt)

            pe_cross(pe, C0, 0)
            pe.wait_ge(*split0["w_low"].at(8))
            project(C0, P0, WB_P0, M0)
            join(pe, split0, "w_low")
            pe_mlp(pe, M0, A1)
            pe_front(pe, A1, [(WB_SQ, 0), (WB_SK, 0), (WB_SQ, 1), (WB_SK, 1)], [WB_SV])
            join(pe, A1, "xf ev")
            pe_self(pe, C1)
            project(C1, P1, WB_SO, A2)
            pe_front(pe, A2, [(WB_CQ, 0), (WB_CQ, 1)], [])
            join(pe, A2, "xf ev")
            join(pe, cx, "c_stack")
            pe_cross(pe, C2, 1)
            project(C2, P2, WB_CO, M1)
            join(pe, split1, "w_low")
            pe_mlp(pe, M1)

        @block.scalar
        def _(act):
            act.wait_ge(ld["cols"], 16)

            def high(blk):
                nc.scalar.copy(WH[:, blk, :], RAW[:, blk, :]).then_inc(split0["w_high"].sem, 1)
            for layer in (1, 0):
                for k, cn in enumerate((P, CTX - P)):
                    i = 2 * layer + k
                    act.wait_ge(*cx["c_tr"].at((3 if layer == 0 else 1) + k))
                    if layer:
                        y = nc.scalar.copy(YT[0:cn, i, :], PS[0:cn, 4 + i, 0:B * L])
                    else:
                        y = nc.scalar.activation(YT[0:cn, i, :], PS[0:cn, 4 + i, 0:B * L], ACT.Identity,
                                                 scale=col("l0_ln2_w", k)[0:cn], bias=col("l0_ln2_b", k)[0:cn])
                    y.then_inc(cx["c_yt"].sem, 1)
            act.wait_ge(ld["wq"], 16)
            high(0)
            high(1)
            act_xf(act, A0, 0)
            act_xh(act, A0, 0)
            for i in range(4):
                act.wait_ge(*cx["c_mm"].at(i + 1))
                nc.scalar.activation(KP[:, i, 0, :], PS[:, 4 + i, 0:B * L], ACT.Identity,
                                     bias=col("ca_bk" if i > 1 else "zero", i % 2)).then_inc(cx["c_p1"].sem, 1)
            act_xf(act, A0, 1)
            act_xh(act, A0, 1)

            def act_mlp_weights(split, loaded):
                act.wait_ge(loaded, 16)
                for k in range(8):
                    nc.scalar.copy(WH[:, WB_W1 + k, :], RAW2[:, k, :]).then_inc(split["w_high"].sem, 1)

            def highs():
                act.wait_ge(ld["w"], 16)
                for blk in range(2, 8):
                    high(blk)
            act_front(act, A0, qk0, None, {0: highs})
            act_mlp_weights(split0, ld["mlp0"])
            join(act, A0, "xl part3 stored0 stored1 stored2 stored3")
            join(act, cx, "c_store0 c_store1")

            def project(C, Pj, nxt):
                join(act, C, "pv otr")
                act_high(act, Pj, 0)
                act_high(act, Pj, 1)
                act_front(act, Pj, [], nxt)

            act_cross(act, C0)
            project(C0, P0, M0)
            act_mlp(act, M0, "l0_b1", A1)
            act_front(act, A1, qk1)
            join(act, A1, "xl part3 stored0 stored1 stored2 stored3")
            join(act, P0, "xn xn_pool")
            act_self(act, C1)
            project(C1, P1, A2)
            act_front(act, A2, qk2)
            join(act, M0, "acc")
            act_mlp_weights(split1, ld["mlp1"])
            join(act, A2, "xl part3 stored0 stored1 stored2 stored3")
            join(act, P1, "xn xn_pool")
            act_cross(act, C2)
            project(C2, P2, M1)
            act_mlp(act, M1, "l1_b1")

        @block.vector
        def _(dve):
            nc.vector.memset(KSC[96:P, :, :, :], 1.0).then_inc(s_ones, 1)
            dve.wait_ge(ld["ctx"], 16)
            for b in range(B):
                nc.vector.bn_stats(bst[0:L, b, :], CX[:, b, :]).then_inc(cx["c_bn"].sem, 1)
            for b in range(B):
                dve.wait_ge(*cx["c_bn"].at(b + 1))
                nc.vector.bn_aggr(mv[0:L, b, :], bst[0:L, b, :]).then_inc(cx["c_bn2"].sem, 1)
            dve.wait_ge(*cx["c_rs"].at(1))
            for b in range(B):
                nc.vector.tensor_scalar(CN[:, b, :], CX[:, b, :], mv[0:L, b, 0:1], rstd[0:L, b:b + 1],
                                        ALU.subtract, ALU.mult).then_inc(cx["c_n"].sem, 1)

            dve.wait_ge(s_const, 4)
            nc.vector.tensor_copy(identb[:], identf[:]).then_inc(s_ones, 1)

            def low(blk):
                dve.wait_ge(*split0["w_high"].at(blk + 1))
                nc.vector.tensor_tensor(WL[:, blk, :], RAW[:, blk, :], WH[:, blk, :].bitcast(F32), ALU.subtract
                                        ).then_inc(split0["w_low"].sem, 1)

            dve_stats(dve, A0, 0)
            dve_norm(dve, A0, 0)
            dve_stats(dve, A0, 1)
            dve_norm(dve, A0, 1)
            dve_stats(dve, A0, 2)
            low(0)
            low(1)
            dve.wait_ge(ld["cols"], 16)
            for i in range(4):
                dve.wait_ge(*cx["c_p1"].at(i + 1))
                nc.vector.scalar_tensor_tensor(KR[:, i, :], PS[:, 4 + i, 0:B * L],
                                               col("ca_bk" if i > 1 else "zero", i % 2), KP[:, i, 0, :],
                                               ALU.add, ALU.subtract).then_inc(cx["c_r"].sem, 1)
            dve_xl(dve, A0, 0)
            dve.wait_ge(ld["rows"], 16)
            for i in range(4):
                dve.wait_ge(*cx["c_mm"].at(5 + i))
                if i < 2:
                    v = nc.vector.tensor_copy(VC[:, 0, i, :], PS[0:L, 4 + i, 0:D])
                else:
                    v = nc.vector.tensor_tensor(VC[:, 1, i - 2, :], PS[0:L, 4 + i, 0:D], row("ca_bv")[0:L], ALU.add)
                v.then_inc(cx["c_v"].sem, 1)

            def context_parts():
                for i in range(4):
                    dve.wait_ge(*cx["c_r"].at(i + 1))
                    nc.vector.tensor_copy(KP[:, i, 1, :], KR[:, i, :]).then_inc(cx["c_p2"].sem, 1)
                for i in range(4):
                    dve.wait_ge(*cx["c_p2"].at(i + 1))
                    nc.vector.tensor_tensor(KP[:, i, 2, :], KR[:, i, :], KP[:, i, 1, :], ALU.subtract
                                            ).then_inc(cx["c_p3"].sem, 1)
            dve_front(dve, A0, qk0, None, None, {0: context_parts})
            for blk in range(2, 8):
                low(blk)

            def dve_mlp_weights(split, before):
                for k in range(8):
                    dve.wait_ge(*split["w_high"].at(before + k + 1))
                    nc.vector.tensor_tensor(WL[:, WB_W1 + k, :], RAW2[:, k, :], WH[:, WB_W1 + k, :].bitcast(F32),
                                            ALU.subtract).then_inc(split["w_low"].sem, 1)
            dve_mlp_weights(split0, 8)
            join(dve, A0, "part3 stored0 stored1 stored2 stored3")

            def project(C, Pj, nxt):
                join(dve, C, "ou")
                for c in range(2):
                    dve_norm(dve, Pj, c)
                dve_xl(dve, Pj, 0)
                dve_front(dve, Pj, [], "x", nxt)

            dve_cross(dve, C0)
            project(C0, P0, M0)
            dve_mlp(dve, M0, A1)
            dve_front(dve, A1, qk1, "v")
            dve_self(dve, C1)
            project(C1, P1, A2)
            dve_front(dve, A2, qk2, None)
            dve_mlp_weights(split1, 0)
            join(dve, A2, "part3 stored0 stored1 stored2 stored3")
            dve_cross(dve, C2)
            project(C2, P2, M1)
            dve_mlp(dve, M1)

        @block.gpsimd
        def _(pool):
            nc.gpsimd.memset(identf[:], 0.0).then_inc(s_const, 1)
            nc.gpsimd.memset(half[:], -0.5).then_inc(s_const, 1)
            pool.wait_ge(s_const, 1)
            nc.gpsimd.affine_select(out=identf[:], in_=identf[:], compare_op=ALU.not_equal, fill=1.0, base=0,
                                    pattern=[[-1, P]], channel_multiplier=1).then_inc(s_const, 2)
            nc.gpsimd.memset(VS[:], 0.0).then_inc(s_vs_const, 1)
            pool.wait_ge(s_vs_const, 1)
            nc.gpsimd.memset(VS[:, :, :, :, HD:HD + 1], 1.0).then_inc(s_vs_const, 1)
            pool.wait_ge(*cx["c_bn2"].at(2))
            nc.gpsimd.tensor_scalar(var_eps[0:L, 0:2], mv[0:L, 0:2, 1], EPS, 1.0, ALU.add, ALU.mult
                                    ).then_inc(cx["c_var"].sem, 1)
            join(pool, cx, "c_var")
            pool.wait_ge(s_const, 4)
            nc.gpsimd.tensor_tensor(rstd[0:L, 0:2], var_eps[0:L, 0:2], half[0:L, 0:2], ALU.pow
                                    ).then_inc(cx["c_rs"].sem, 1)
            join(pool, cx, "c_n")
            pool_rstd(pool, A0, 0)
            pool_rstd(pool, A0, 1)
            pool_rstd(pool, A0, 2)
            pool_front(pool, A0)
            pool.wait_ge(s_vs_const, 2)
            pool.wait_ge(ld["rows"], 16)
            join(pool, cx, "c_v")

            def project(Pj, nxt):
                pool_divide(pool, Pj, 0)
                pool_divide(pool, Pj, 1)
                pool_front(pool, Pj, nxt)

            join(pool, A0, "xn")
            pool_cross(pool, C0, 0, P0, "l0_bproj")
            project(P0, M0)
            pool_mlp(pool, M0, "l0_b2", A1)
            pool_front(pool, A1)
            join(pool, A1, "ev")
            pool_self(pool, C1)
            join(pool, A1, "xn")
            pool_bias(P1, "sa_bo", range(NT))
            project(P1, A2)
            pool_front(pool, A2)
            join(pool, A2, "xn")
            pool_cross(pool, C2, 1, P2, "ca_bo")
            project(P2, M1)
            pool_mlp(pool, M1, "l1_b2")


def kernel(**inputs):
    import numpy as np
    import concourse.bacc as bacc
    from concourse.bass_utils import run_bass_kernel_spmd

    a = {k: np.asarray(v) for k, v in inputs.items()}
    l0, l1 = "L0_xattn_", "L1_xattn_"

    def square(w):
        k, n = w.shape
        return w.reshape(k // P, P, n).transpose(1, 0, 2).reshape(P, -1, 512)

    weights = np.concatenate(
        [square(a[l0 + "Wq"]), square(a[l0 + "Wproj"])]
        + [square(a[l1 + n].T) for n in ("sa_wq", "sa_wk", "sa_wv", "sa_wo", "ca_wq", "ca_wo")]
        + [square(a[l0 + "W1"]), square(a[l0 + "W2"])], axis=1)
    weights_mlp1 = np.concatenate([square(a[l1 + "mlp_w1"].T), square(a[l1 + "mlp_w2"].T)], axis=1)

    named = {"l0_ln1_w": l0 + "ln1_w", "l0_ln1_b": l0 + "ln1_b", "l0_ln3_w": l0 + "ln3_w", "l0_ln3_b": l0 + "ln3_b",
             "l1_ln1_w": l1 + "ln1_g", "l1_ln1_b": l1 + "ln1_b", "l1_ln2_w": l1 + "ln2_g", "l1_ln2_b": l1 + "ln2_b",
             "l1_ln3_w": l1 + "ln3_g", "l1_ln3_b": l1 + "ln3_b", "l0_ln2_w": l0 + "ln2_w", "l0_ln2_b": l0 + "ln2_b",
             "sa_bq": l1 + "sa_bq", "sa_bk": l1 + "sa_bk", "ca_bq": l1 + "ca_bq", "ca_bk": l1 + "ca_bk",
             "l0_b1": l0 + "b1", "l1_b1": l1 + "mlp_b1"}
    cols = np.zeros((P, NCOLS), np.float32)
    for name, (at, width) in COLS.items():
        if name in named:
            v = a[named[name]]
            for i in range(width):
                part = v[i * P:(i + 1) * P]
                cols[:len(part), at + i] = part
    rows = np.stack([a[n] for n in (l0 + "bproj", l0 + "b2", l1 + "sa_bv", l1 + "sa_bo", l1 + "ca_bo",
                                    l1 + "mlp_b2", l1 + "ca_bv")])
    arrays = {"x": a["x"], "ctx": a["ctx_768"], "weights": weights, "weights_mlp1": weights_mlp1,
              "wkv": a[l0 + "Wkv"], "wck": a[l1 + "ca_wk"].T, "wcv": a[l1 + "ca_wv"].T, "cols": cols, "rows": rows}
    arrays = {k: np.ascontiguousarray(v) for k, v in arrays.items()}

    nc = bacc.Bacc("TRN2", target_bir_lowering=False, num_devices=1, dynamic_dma_scratch_size=1024)
    args = [nc.dram_tensor(k, v.shape, mybir.dt.from_np(v.dtype), kind="ExternalInput").ap()
            for k, v in arrays.items()]
    out = nc.dram_tensor("out", (B, S, D), F32, kind="ExternalOutput").ap()
    build(nc, *args, out)
    r = run_bass_kernel_spmd(nc, [arrays], core_ids=[0])
    return r.results[0]["out"]
```
